# Optimizing a Trainium2 kernel written in Bass

```python
import numpy as np
import jax
import jax.numpy as jnp

def _softmax(x, axis=-1):
    return jax.nn.softmax(x, axis=axis)

def _gelu(x):
    return jax.nn.gelu(x, approximate=True)

def _silu(x):
    return jax.nn.silu(x)

def _sigmoid(x):
    return jax.nn.sigmoid(x)

def _layernorm(x, axis=-1, eps=1e-05):
    m = jnp.mean(x, axis=axis, keepdims=True)
    v = jnp.var(x, axis=axis, keepdims=True)
    return (x - m) / jnp.sqrt(v + eps)

def _scatter_add(tgt, idx, src, axis=0):
    return tgt.at[idx].add(src)

def _segment_sum(src, seg, n):
    return jax.ops.segment_sum(src, seg, n)
kernel_name = 'mk_lm_tower_d1_tok_ids768_r4_276517'

def setup_inputs(seed: int=0):
    np.random.seed(seed)
    _w = jnp.asarray

    def _rec_inputs():
        import jax
        import jax.numpy as jnp
        _rk = jax.random.key(seed)
        x = jax.random.randint(jax.random.fold_in(_rk, 1), (32, 512), 0, 12565, jnp.int32)
        return x
    x = _rec_inputs()

    def _L0_tok_setup():
        import jax, jax.numpy as jnp
        import numpy as np
        VOCAB, RANK, D_MODEL = (12565, 64, 192)
        B, S = (8, 1024)
        key = jax.random.key(seed)
        k_ids, k_emb, k_proj = jax.random.split(key, 3)
        input_ids = jax.random.randint(k_ids, (B, S), 0, VOCAB)
        embed_table = jax.random.normal(k_emb, (VOCAB, RANK), dtype=jnp.float32) * 0.02
        proj_up = jax.random.normal(k_proj, (D_MODEL, RANK), dtype=jnp.float32) * 0.02
        return {'input_ids': input_ids, 'embed_table': embed_table, 'proj_up': proj_up}
    _L0_tok_all = _L0_tok_setup()
    _L0_tok_in = {k: v for k, v in _L0_tok_all.items() if k in ('embed_table', 'proj_up')}
    del _L0_tok_all

    def _L0_attn_setup():
        import jax, jax.numpy as jnp
        import numpy as np
        D_MODEL = 192
        H = 6
        DQK = 128
        DV = 64
        SCALE_BASE = 512.0

        def _xpos(x, sign):
            B, T, Hn, d = x.shape
            half = d // 2
            pos = jnp.arange(T, dtype=jnp.float32)
            inv_freq = 1.0 / 10000.0 ** (jnp.arange(half, dtype=jnp.float32) / half)
            angles = pos[:, None] * inv_freq[None, :]
            zeta = (jnp.arange(half, dtype=jnp.float32) + half) / d
            decay = zeta[None, :] ** (sign * pos[:, None] / SCALE_BASE)
            cos_a = (jnp.cos(angles) * decay)[None, :, None, :]
            sin_a = (jnp.sin(angles) * decay)[None, :, None, :]
            x1, x2 = (x[..., :half], x[..., half:])
            return jnp.concatenate([x1 * cos_a - x2 * sin_a, x1 * sin_a + x2 * cos_a], axis=-1)

        def _decay_mask(T):
            gammas = jnp.array([1.0 - 2.0 ** (-(5 + h)) for h in range(H)], dtype=jnp.float32)
            i = jnp.arange(T, dtype=jnp.float32)
            diff = i[:, None] - i[None, :]
            causal = (diff >= 0).astype(jnp.float32)
            D = gammas[:, None, None] ** jnp.clip(diff, 0.0)[None] * causal[None]
            row = jnp.clip(jnp.sum(D, axis=-1, keepdims=True), 1e-06)
            return D / jnp.sqrt(row)
        key = jax.random.key(seed)
        ks = jax.random.split(key, 6)
        B, T = (2, 512)

        def xavier(k, shape):
            lim = float(np.sqrt(6.0 / (shape[0] + shape[1])))
            return jax.random.uniform(k, shape, jnp.float32, -lim, lim)
        return {'x': jax.random.normal(ks[0], (B, T, D_MODEL), jnp.float32), 'Wq': xavier(ks[1], (D_MODEL, H * DQK)), 'Wk': xavier(ks[2], (D_MODEL, H * DQK)), 'Wv': xavier(ks[3], (D_MODEL, H * DV)), 'Wg': xavier(ks[4], (D_MODEL, H * DV)), 'Wo': xavier(ks[5], (H * DV, D_MODEL)), 'gn_weight': jnp.ones((H * DV,), jnp.float32), 'gn_bias': jnp.zeros((H * DV,), jnp.float32)}
    _L0_attn_all = _L0_attn_setup()
    _L0_attn_in = {k: v for k, v in _L0_attn_all.items() if k in ('Wq', 'Wk', 'Wv', 'Wg', 'Wo', 'gn_weight', 'gn_bias')}
    del _L0_attn_all

    def _L0_ffn_setup():
        import jax, jax.numpy as jnp
        import numpy as np
        ATOM = {'vm': 0, 'im': 1, 'cm': 2, 'sc': 3, 'cc': 4}
        TASK_PAIRS = [('vm', 'sc'), ('vm', 'cc'), ('im', 'sc'), ('im', 'cc'), ('cm', 'sc'), ('cm', 'cc')]
        SRC_IDX = np.array([[ATOM[l], ATOM[r]] for l, r in TASK_PAIRS], dtype=np.int32)
        DST_IDX = np.array([[ATOM[r], ATOM[l]] for l, r in TASK_PAIRS], dtype=np.int32)
        NCLS = 6
        NATOMS = 5

        def _l2norm(x, eps=1e-12):
            return x / jnp.clip(jnp.linalg.norm(x, axis=-1, keepdims=True), eps)
        key = jax.random.key(seed)
        ks = jax.random.split(key, 12)
        B, NPATCH, D, H = (64, 197, 192, 768)
        std = 0.02
        x = jax.random.normal(ks[0], (B, NCLS + NPATCH, D), dtype=jnp.float32)
        fc1_w = jax.random.normal(ks[1], (H, D), dtype=jnp.float32) * std
        fc1_b = jnp.zeros((H,), jnp.float32)
        fc2_w = jax.random.normal(ks[2], (D, H), dtype=jnp.float32) * std
        fc2_b = jnp.zeros((D,), jnp.float32)
        gate_pair = jax.random.normal(ks[3], (NCLS, 2, D), dtype=jnp.float32) * std
        atom_in_w = jax.random.normal(ks[4], (NATOMS, H, D), dtype=jnp.float32) * std
        atom_in_b = jax.random.normal(ks[5], (NATOMS, H), dtype=jnp.float32) * std
        atom_out_w = jax.random.normal(ks[6], (NATOMS, D, H), dtype=jnp.float32) * std
        atom_out_b = jax.random.normal(ks[7], (NATOMS, D), dtype=jnp.float32) * std
        balance_bias = jnp.zeros((NCLS, 2), jnp.float32)
        return {'x': x, 'fc1_w': fc1_w, 'fc1_b': fc1_b, 'fc2_w': fc2_w, 'fc2_b': fc2_b, 'gate_pair': gate_pair, 'atom_in_w': atom_in_w, 'atom_in_b': atom_in_b, 'atom_out_w': atom_out_w, 'atom_out_b': atom_out_b, 'balance_bias': balance_bias}
    _L0_ffn_all = _L0_ffn_setup()
    _L0_ffn_in = {k: v for k, v in _L0_ffn_all.items() if k in ('fc1_w', 'fc1_b', 'fc2_w', 'fc2_b', 'gate_pair', 'atom_in_w', 'atom_in_b', 'atom_out_w', 'atom_out_b', 'balance_bias')}
    del _L0_ffn_all
    return {'x': x, 'L0_tok_embed_table': _L0_tok_in['embed_table'], 'L0_tok_proj_up': _L0_tok_in['proj_up'], 'L0_attn_Wq': _L0_attn_in['Wq'], 'L0_attn_Wk': _L0_attn_in['Wk'], 'L0_attn_Wv': _L0_attn_in['Wv'], 'L0_attn_Wg': _L0_attn_in['Wg'], 'L0_attn_Wo': _L0_attn_in['Wo'], 'L0_attn_gn_weight': _L0_attn_in['gn_weight'], 'L0_attn_gn_bias': _L0_attn_in['gn_bias'], 'L0_ffn_fc1_w': _L0_ffn_in['fc1_w'], 'L0_ffn_fc1_b': _L0_ffn_in['fc1_b'], 'L0_ffn_fc2_w': _L0_ffn_in['fc2_w'], 'L0_ffn_fc2_b': _L0_ffn_in['fc2_b'], 'L0_ffn_gate_pair': _L0_ffn_in['gate_pair'], 'L0_ffn_atom_in_w': _L0_ffn_in['atom_in_w'], 'L0_ffn_atom_in_b': _L0_ffn_in['atom_in_b'], 'L0_ffn_atom_out_w': _L0_ffn_in['atom_out_w'], 'L0_ffn_atom_out_b': _L0_ffn_in['atom_out_b'], 'L0_ffn_balance_bias': _L0_ffn_in['balance_bias']}

def reference(x, L0_tok_embed_table, L0_tok_proj_up, L0_attn_Wq, L0_attn_Wk, L0_attn_Wv, L0_attn_Wg, L0_attn_Wo, L0_attn_gn_weight, L0_attn_gn_bias, L0_ffn_fc1_w, L0_ffn_fc1_b, L0_ffn_fc2_w, L0_ffn_fc2_b, L0_ffn_gate_pair, L0_ffn_atom_in_w, L0_ffn_atom_in_b, L0_ffn_atom_out_w, L0_ffn_atom_out_b, L0_ffn_balance_bias):
    import jax
    import jax.numpy as jnp

    def _L0_tok_ref(input_ids, embed_table, proj_up):
        import jax, jax.numpy as jnp
        import numpy as np
        VOCAB, RANK, D_MODEL = (12565, 64, 192)
        B, S = (8, 1024)
        low = embed_table[input_ids]
        return jnp.einsum('bsr,dr->bsd', low, proj_up)

    def _L0_attn_ref(x, Wq, Wk, Wv, Wg, Wo, gn_weight, gn_bias):
        import jax, jax.numpy as jnp
        import numpy as np
        D_MODEL = 192
        H = 6
        DQK = 128
        DV = 64
        SCALE_BASE = 512.0

        def _xpos(x, sign):
            B, T, Hn, d = x.shape
            half = d // 2
            pos = jnp.arange(T, dtype=jnp.float32)
            inv_freq = 1.0 / 10000.0 ** (jnp.arange(half, dtype=jnp.float32) / half)
            angles = pos[:, None] * inv_freq[None, :]
            zeta = (jnp.arange(half, dtype=jnp.float32) + half) / d
            decay = zeta[None, :] ** (sign * pos[:, None] / SCALE_BASE)
            cos_a = (jnp.cos(angles) * decay)[None, :, None, :]
            sin_a = (jnp.sin(angles) * decay)[None, :, None, :]
            x1, x2 = (x[..., :half], x[..., half:])
            return jnp.concatenate([x1 * cos_a - x2 * sin_a, x1 * sin_a + x2 * cos_a], axis=-1)

        def _decay_mask(T):
            gammas = jnp.array([1.0 - 2.0 ** (-(5 + h)) for h in range(H)], dtype=jnp.float32)
            i = jnp.arange(T, dtype=jnp.float32)
            diff = i[:, None] - i[None, :]
            causal = (diff >= 0).astype(jnp.float32)
            D = gammas[:, None, None] ** jnp.clip(diff, 0.0)[None] * causal[None]
            row = jnp.clip(jnp.sum(D, axis=-1, keepdims=True), 1e-06)
            return D / jnp.sqrt(row)
        B, T, _ = x.shape
        Q = (x @ Wq).reshape(B, T, H, DQK)
        K = (x @ Wk).reshape(B, T, H, DQK)
        V = (x @ Wv).reshape(B, T, H, DV)
        Q = _xpos(Q, 1.0)
        K = _xpos(K, -1.0)
        scores = jnp.einsum('bihd,bjhd->bhij', Q, K) * DQK ** (-0.5)
        scores = scores * _decay_mask(T)[None]
        out = jnp.einsum('bhij,bjhv->bihv', scores, V)
        concat = out.reshape(B, T, H * DV)
        g = concat.transpose(0, 2, 1).reshape(B, H, DV, T)
        mean = jnp.mean(g, axis=(2, 3), keepdims=True)
        var = jnp.var(g, axis=(2, 3), keepdims=True)
        g = (g - mean) / jnp.sqrt(var + 1e-05)
        g = g.reshape(B, H * DV, T) * gn_weight[None, :, None] + gn_bias[None, :, None]
        normed = g.transpose(0, 2, 1)
        gate = jax.nn.silu(x @ Wg)
        return normed * gate @ Wo

    def _L0_ffn_ref(x, fc1_w, fc1_b, fc2_w, fc2_b, gate_pair, atom_in_w, atom_in_b, atom_out_w, atom_out_b, balance_bias):
        import jax, jax.numpy as jnp
        import numpy as np
        ATOM = {'vm': 0, 'im': 1, 'cm': 2, 'sc': 3, 'cc': 4}
        TASK_PAIRS = [('vm', 'sc'), ('vm', 'cc'), ('im', 'sc'), ('im', 'cc'), ('cm', 'sc'), ('cm', 'cc')]
        SRC_IDX = np.array([[ATOM[l], ATOM[r]] for l, r in TASK_PAIRS], dtype=np.int32)
        DST_IDX = np.array([[ATOM[r], ATOM[l]] for l, r in TASK_PAIRS], dtype=np.int32)
        NCLS = 6
        NATOMS = 5

        def _l2norm(x, eps=1e-12):
            return x / jnp.clip(jnp.linalg.norm(x, axis=-1, keepdims=True), eps)
        src = jnp.asarray(SRC_IDX)
        dst = jnp.asarray(DST_IDX)
        D = x.shape[-1]
        H = atom_in_w.shape[1]
        cls_tokens = x[:, :NCLS]
        patch_tokens = x[:, NCLS:]
        patch_out = jax.nn.gelu(patch_tokens @ fc1_w.T + fc1_b, approximate=False) @ fc2_w.T + fc2_b
        gate_in = _l2norm(cls_tokens.astype(jnp.float32))
        gate_w = _l2norm(gate_pair.astype(jnp.float32))
        gate_logits = jnp.einsum('bnd,nrd->bnr', gate_in, gate_w) + balance_bias[None]
        route_probs = jax.nn.softmax(gate_logits, axis=-1)
        chosen_route = jnp.argmax(route_probs, axis=-1)
        hid_all = jax.nn.gelu(jnp.einsum('bnd,ahd->bnah', cls_tokens, atom_in_w) + atom_in_b[None, None], approximate=False)
        sh_pair = hid_all[:, jnp.arange(NCLS)[:, None], src, :]
        route_out_w = atom_out_w[dst.reshape(-1)].reshape(NCLS, 2, D, H)
        route_candidates = jnp.einsum('bnrh,nrdh->bnrd', sh_pair, route_out_w) + atom_out_b[dst][None]
        chosen_w = jnp.take_along_axis(route_probs, chosen_route[..., None], axis=-1)
        chosen_cand = jnp.take_along_axis(route_candidates, chosen_route[:, :, None, None], axis=2)[:, :, 0]
        cls_out = chosen_cand * chosen_w.astype(chosen_cand.dtype)
        return jnp.concatenate([cls_out, patch_out], axis=1)
    h = _L0_tok_ref(x, L0_tok_embed_table, L0_tok_proj_up)
    h = h + _L0_attn_ref(_layernorm(h, axis=-1), L0_attn_Wq, L0_attn_Wk, L0_attn_Wv, L0_attn_Wg, L0_attn_Wo, L0_attn_gn_weight, L0_attn_gn_bias)
    h = h + _L0_ffn_ref(_layernorm(h, axis=-1), L0_ffn_fc1_w, L0_ffn_fc1_b, L0_ffn_fc2_w, L0_ffn_fc2_b, L0_ffn_gate_pair, L0_ffn_atom_in_w, L0_ffn_atom_in_b, L0_ffn_atom_out_w, L0_ffn_atom_out_b, L0_ffn_balance_bias)
    return h

_drawn_inputs = setup_inputs


def setup_inputs(seed=0):
    import zlib

    import numpy as np

    out = dict(_drawn_inputs(seed))
    spreads = {'L0_attn_gn_weight': (1.0, 0.2),
     'L0_attn_gn_bias': (0.0, 0.1),
     'L0_ffn_fc1_b': (0.0, 0.1),
     'L0_ffn_fc2_b': (0.0, 0.1),
     'L0_ffn_balance_bias': (0.0, 0.8)}
    factors = {'L0_ffn_gate_pair': 8.0,
     'L0_ffn_atom_in_w': 5.05,
     'L0_ffn_atom_in_b': 8.0,
     'L0_ffn_atom_out_w': 4.946,
     'L0_ffn_atom_out_b': 8.0}
    for name, (base, spread) in spreads.items():
        noise = np.random.default_rng([zlib.crc32(name.encode()), seed]).standard_normal(out[name].shape)
        drawn = base * np.exp(spread * noise) if base else spread * noise
        out[name] = jnp.asarray(drawn.astype(out[name].dtype))
    for name, factor in factors.items():
        out[name] = (out[name] * factor).astype(out[name].dtype)
    return out
```

```python
import concourse.bass as bass
from concourse import mybir
from contextlib import ExitStack
import numpy as np

B, T = 32, 512
VOCAB, R, D = 12565, 64, 192
H, DK, DV = 6, 128, 64
F = 768
NCLS, NATOM = 6, 5
SRC = [(0, 3), (0, 4), (1, 3), (1, 4), (2, 3), (2, 4)]
P = 128
NT = T // P
NP = H // 2
HALF = DK // 2
QK = H * DK
VC = H * DV
WC = 2 * QK + 2 * VC
V_AT, G_AT = 2 * QK, 2 * QK + VC
NF = F // P
BC = 3 * DK
LN_EPS = 1e-5

RING = 4


def front_jobs():
    jobs = []
    for t in range(NT):
        jobs += [("rotary_products", 4 * t + k, 4 * NT) for k in range(4)] + [("v_ready", t, NT)]
    jobs += [("gate_ready", m, NP) for m in range(NP)]
    turned = [[("kq_t_ready", 4 * p + j, 4 * NP) for j in range(4)] for p in range(NP)]
    states = [[("state_steps", 3 * p + 2, 3 * NP)] for p in range(NP)]
    scores = [[("probs_ready", 2 * p + j, 2 * NP) for j in range(2)] for p in range(NP)]
    outs = [[("att_ready", p, NP)] for p in range(NP)]
    jobs += turned[0] + states[0] + scores[0]
    jobs += turned[1] + states[1] + outs[0] + scores[1]
    jobs += turned[2] + states[2] + outs[1] + scores[2]
    jobs += [("emb_t_ready", k, 2) for k in range(2)] + outs[2]
    jobs += [("ln1_steps", k, 10) for k in (1, 3)] + [("norm_t_ready", 0, 1)]
    return jobs


JOBS = front_jobs()
assert len(JOBS) % RING == 0
NEXT = ("emb_t_ready", "ln1_steps", "norm_t_ready")


def job(name, index):
    return next(q for q, (n, k, _) in enumerate(JOBS) if (n, k) == (name, index))


def user_before(i, q):
    turn = 0
    while True:
        q -= RING
        if q < 0:
            q += len(JOBS)
            turn -= 1
        name, index, count = JOBS[q]
        if isinstance(i, int):
            if i + turn < -1:
                return None
            if i + turn == -1 and name not in NEXT or i + turn == B - 1 and name in NEXT:
                continue
        return name, (i + turn + (name in NEXT)) * count + index + 1


def build(nc, a):
    fp32, f32r = mybir.dt.float32, mybir.dt.float32r
    u32 = mybir.dt.uint32
    ALU, ACT = mybir.AluOpType, mybir.ActivationFunctionType

    with ExitStack() as ctx:
        def sb(name, shape, dt=fp32):
            return ctx.enter_context(nc.sbuf_tensor(name, shape, dt))

        def sem(name):
            return ctx.enter_context(nc.semaphore(name))

        ident = sb("ident", [P, P])
        head_mean = sb("head_mean", [P, P])
        causal = sb("causal", [P, P])
        cos_t = sb("cos_t", [P, NT, 2, H, HALF])
        sin_t = sb("sin_t", [P, NT, 2, H, DK])
        w_hi = sb("w_hi", [P, WC], f32r)
        w_lo = sb("w_lo", [P, WC], f32r)
        up_hi = sb("up_hi", [P, D], f32r)
        up_lo = sb("up_lo", [P, D], f32r)
        fc1_hi = sb("fc1_hi", [P, 3, F], f32r)
        fc1_lo = sb("fc1_lo", [P, 2, F], f32r)
        fc1_b = sb("fc1_b", [P, NF])
        fc2 = sb("fc2", [P, NF, D])
        fc2_b = sb("fc2_b", [P, D])
        wo = sb("wo", [P, NP, D])
        gn_w = sb("gn_w", [P, NP])
        gn_b = sb("gn_b", [P, NP])
        neg_half = sb("neg_half", [P, NT])

        ids = sb("ids", [P, NT], mybir.dt.int32)
        emb = sb("emb", [P, NT * R])
        emb_split = sb("emb_split", [P, NT, 2 * R], f32r)
        emb_norm = sb("emb_norm", [P, NT, R])
        norm_split = sb("norm_split", [P, NT, 2 * R], f32r)
        emb_t = sb("emb_t", [P, T], f32r)
        norm_t = sb("norm_t", [P, T], f32r)
        ln1_st = sb("ln1_st", [P, NT, 6])
        ln1_mv = sb("ln1_mv", [P, NT, 2])
        ln1_ve = sb("ln1_ve", [P, NT])
        ln1_rstd = sb("ln1_rstd", [P, NT])
        rot_c = sb("rot_c", [P, 2, QK])
        rot_s = sb("rot_s", [P, 2, QK])
        kq = sb("kq", [P, NT, 2, H, DK])
        v = sb("v", [P, NT, VC])
        gate = sb("gate", [P, NP, T])
        kq_t = sb("kq_t", [P, 2, 4, T])
        state = sb("state", [P, 2, NT - 1, P])
        probs = sb("probs", [P, 2, 2, T])
        att = sb("att", [P, NP, T])
        gn_st = sb("gn_st", [P, NP, 6])
        gn_mv = sb("gn_mv", [P, NP, 2])
        gn_mean = sb("gn_mean", [P, NP])
        gn_d = sb("gn_d", [P, NP])
        gn_dd = sb("gn_dd", [P, NP])
        gn_m2 = sb("gn_m2", [P, NP])
        gn_ve = sb("gn_ve", [P, NP])
        gn_rstd = sb("gn_rstd", [P, NP])
        gn_a = sb("gn_a", [P, NP])
        gn_ma = sb("gn_ma", [P, NP])
        gn_c = sb("gn_c", [P, NP])
        ln2_st = sb("ln2_st", [P, NT, 6])
        ln2_mv = sb("ln2_mv", [P, NT, 2])
        ln2_ve = sb("ln2_ve", [P, NT])
        ln2_rstd = sb("ln2_rstd", [P, NT])
        ln2_nmr = sb("ln2_nmr", [P, NT])
        x2 = sb("x2", [P, NT, D])
        x2_split = sb("x2_split", [P, NT, 2 * D], f32r)
        x2_t = sb("x2_t", [P, 3, T], f32r)
        hid = sb("hid", [P, NF, T])
        h2_cls = sb("h2_cls", [NCLS, D])
        res = sb("res", [P, NT, D])

        bank = [ctx.enter_context(nc.psum_tensor(f"ring{k}", [P, 512], fp32)) for k in range(RING)]
        back = [ctx.enter_context(nc.psum_tensor(f"back{k}", [P, 512], fp32)) for k in range(2)]
        hb = [ctx.enter_context(nc.psum_tensor(f"resid{k}", [P, 512], fp32)) for k in range(2)]

        w_stage = kq[:, :, :, :, :].rearrange("p t a h d -> p (t a h d)")
        wa = w_stage[:, 0:WC]
        wb = w_stage[0:D - P, WC:2 * WC]
        fc1_stage = hid[:, :, :].rearrange("p c t -> p (c t)")[:, 0:3 * F]
        center = rot_s[:, 0, 0:2 * D]
        up_dup = rot_s[:, 0, 2 * D:2 * D + 4 * R]
        up_cen = rot_s[:, 1, 0:4 * R]
        up_stage = rot_s[:, 1, 4 * R:4 * R + D]

        s_const = sem("constants_loaded")
        s_stage = sem("weights_staged")
        s_set_pe = sem("setup_products")
        s_set_dve = sem("setup_steps")
        s_set_pool = sem("exponents_ready")
        s_ids = sem("ids_loaded")
        s_emb = sem("embeddings_gathered")
        s_embsplit = sem("embedding_split")
        s_embT = sem("embedding_transposed")
        s_embt = sem("emb_t_ready")
        s_hstat = sem("h_for_ln1")
        s_ln1 = sem("ln1_steps")
        s_ln1p = sem("ln1_rstd_ready")
        s_normsplit = sem("norm_split_ready")
        s_normT = sem("norm_transposed")
        s_normt = sem("norm_t_ready")
        s_proj = sem("kq_projected")
        s_vproj = sem("v_projected")
        s_gproj = sem("gate_projected")
        s_rotm = sem("rotary_products")
        s_rot = sem("kq_rotated")
        s_v = sem("v_ready")
        s_tanh = sem("gate_tanh")
        s_gate = sem("gate_ready")
        s_T = sem("kq_transposed")
        s_t = sem("kq_t_ready")
        s_kv = sem("kv_products")
        s_state = sem("state_steps")
        s_score = sem("scores_done")
        s_prob = sem("probs_ready")
        s_o = sem("attention_out")
        s_att = sem("att_ready")
        s_gns = sem("gn_channel_stats")
        s_gns2 = sem("gn_channel_sums")
        s_gnpe = sem("gn_head_sums")
        s_gn = sem("gn_steps")
        s_gnp = sem("gn_rstd_ready")
        s_aff = sem("gn_applied")
        s_gated = sem("gated_ready")
        s_hres = sem("residual_product")
        s_wo = sem("h2_done")
        s_ln2 = sem("ln2_steps")
        s_ln2p = sem("ln2_rstd_ready")
        s_x2 = sem("x2_ready")
        s_x2s = sem("x2_split_ready")
        s_x2T = sem("x2_transposed")
        s_x2t = sem("x2_t_ready")
        s_fc1 = sem("fc1_product")
        s_hid = sem("hidden_ready")
        s_fc2 = sem("fc2_product")
        s_res = sem("result_ready")
        s_h2c = sem("h2_cls_ready")
        s_stA = sem("result_stored_first_tiles")
        s_stB = sem("result_stored_last_tiles")
        s_xc = sem("x2_cls_stored")
        s_hc = sem("h2_cls_stored")
        by_name = {"rotary_products": s_rotm, "v_ready": s_v, "gate_ready": s_gate, "kq_t_ready": s_t,
                   "state_steps": s_state, "probs_ready": s_prob, "att_ready": s_att,
                   "emb_t_ready": s_embt, "ln1_steps": s_ln1, "norm_t_ready": s_normt}

        s_apart = {nc.vector: sem("dve_went_on"), nc.gpsimd: sem("pool_went_on")}
        N_STAGE, N_CONST = 16 * 20, 16 * 11
        N_SET = 2 + 2 * (WC // BC) + 4
        N_CL, N_CW = 16 * (NCLS * 7 + 1), 16 * NATOM * 3
        CD_T, CD_SQ, CD_DIFF, CLS_STEPS = 5, 15, 23, 36

        def wait_apart(eng, s, value):
            eng.wait_ge(s, value)
            eng.sem_inc(s_apart[eng], 1)

        def later(i):
            return not (isinstance(i, int) and i == 0)

        def bank_of(name, index):
            return bank[job(name, index) % RING]

        def take(pe, i, name, index):
            q = job(name, index)
            before = user_before(i, q)
            if before:
                pe.wait_ge(by_name[before[0]], before[1])
            return bank[q % RING]

        NQ = NCLS // 2
        CT = NQ * B
        flat = w_stage
        rows_c = rot_c[0:CT, :, :].rearrange("p a n -> p (a n)")
        rows_s = rot_s[0:CT, :, :].rearrange("p a n -> p (a n)")
        kq_flat = kq_t[:, :, :, :].rearrange("p s k t -> p (s k t)")
        x2c_sb = rows_c[:, 0:2 * D].rearrange("p (s d) -> p s d", s=2)
        h2c_sb = rows_c[:, 2 * D:4 * D].rearrange("p (s d) -> p s d", s=2)
        gw_sb = rows_c[:, 4 * D:8 * D].rearrange("p (s r d) -> p s r d", s=2, r=2)
        ob_sb = kq_flat[0:CT, 6 * D:10 * D].rearrange("p (s r d) -> p s r d", s=2, r=2)
        c_res = kq_flat[0:CT, 10 * D:12 * D].rearrange("p (s d) -> p s d", s=2)
        bal_sb = kq_flat[0:CT, 12 * D:12 * D + 4].rearrange("p (s r) -> p s r", s=2)
        ib_sb = kq_flat[:, 12 * D + 4:12 * D + 4 + NATOM * NF].rearrange("p (a m) -> p a m", a=NATOM)
        x2c_t = rot_s[:, 0, 0:2 * NCLS * B].rearrange("p (c n) -> p c n", c=2)
        g_junk = rows_s[:, 2 * D:3 * D]
        g_sq, g_dot = rows_s[:, 3 * D:3 * D + 6], rows_s[:, 3 * D + 6:3 * D + 10]
        g_nrm = rows_s[:, 3 * D + 10:3 * D + 16]
        g_log = rows_s[:, 3 * D + 16:3 * D + 20].rearrange("p (s r) -> p s r", s=2)
        g_x = rows_s[:, 3 * D + 20:3 * D + 34]
        g_half = rows_s[:, 3 * D + 34:3 * D + 40]
        c_a, c_b, c_c = (rows_s[:, (4 + k) * D:(5 + k) * D] for k in range(3))
        c_hid = hid[:, 0:5, :].rearrange("p c t -> p (c t)")[:, 0:2 * NF * NCLS * B].rearrange(
            "p (r m s q b) -> p r m s q b", r=2, m=NF, s=2, q=NQ)
        w_in = sin_t[:, :, :, :, :].rearrange("p t a h d -> p (t a h d)")
        w_in2 = flat
        w_outs = v[:, :, :].rearrange("p t n -> p (t n)")
        s_cl = sem("cls_loaded")
        s_cw = sem("cls_weights_loaded")
        s_cd = sem("cls_steps_dve")
        s_cpe = sem("cls_pe_transposes")
        s_ch = sem("cls_hidden_product")
        s_chf = sem("cls_hidden_ready")
        s_co = sem("cls_out_product")
        s_ct = sem("cls_tanh")
        s_cg = sem("cls_pool")
        s_cs = sem("cls_stored")

        def w_in_at(atom, c):
            n = 2 * atom + c
            if n < 8:
                return w_in[:, n * F:(n + 1) * F]
            return w_in2[:, (n - 8) * F:(n - 7) * F]

        def w_out_at(atom):
            size = NF * D
            src = [w_in2[:, 2 * F:2 * F + size], w_in2[:, 2 * F + size:2 * F + 2 * size],
                   w_in2[:, 2 * F + 2 * size:2 * F + 3 * size], w_outs[:, 0:size],
                   kq_flat[:, 0:size]][atom]
            return src.rearrange("p (c d) -> p c d", c=NF)

        block = ctx.enter_context(nc.Block())

        @block.sync
        def _(sp):
            def load(dst, src, s):
                sp.dma_start(dst, src).then_inc(s, 16)

            load(ids[:, :], a["ids"][0, :, :], s_ids)
            load(center[:, 0:D], a["center"][0:P, :], s_stage)
            load(center[0:D - P, D:2 * D], a["center"][P:D, :], s_stage)
            for k in range(2):
                load(up_dup[:, k * R:(k + 1) * R], a["up"][0:P, :], s_stage)
                load(up_dup[0:D - P, 2 * R + k * R:2 * R + (k + 1) * R], a["up"][P:D, :], s_stage)
                load(up_stage[k * R:(k + 1) * R, :], a["up_t"], s_stage)
            at = 0
            for name, n in (("wk", QK), ("wq", QK), ("wv", VC), ("wg", VC)):
                load(wa[:, at:at + n], a[name][0:P, :], s_stage)
                load(wb[:, at:at + n], a[name][P:D, :], s_stage)
                at += n
            load(fc1_stage[:, 0:F], a["fc1_t"][0:P, :], s_stage)
            load(fc1_stage[0:D - P, F:2 * F], a["fc1_t"][P:D, :], s_stage)
            load(fc1_stage[D - P:P, F:2 * F], a["fc1_t"][0:2 * P - D, :], s_stage)
            load(fc1_stage[:, 2 * F:3 * F], a["fc1_t"][D - P:D, :], s_stage)
            load(ident[:, :], a["ident"], s_const)
            load(head_mean[:, :], a["head_mean"], s_const)
            load(causal[:, :], a["causal"], s_const)
            load(cos_t[:, :, :, :, :], a["cos_t"], s_const)
            load(sin_t[:, :, :, :, :], a["sin_t"], s_const)
            load(fc2[:, :, :], a["fc2_t"].rearrange("(c p) d -> p c d", p=P), s_const)
            load(wo[:, :, :], a["wo"].rearrange("(c p) d -> p c d", p=P), s_const)
            load(gn_w[:, :], a["gn_w"], s_const)
            load(gn_b[:, :], a["gn_b"], s_const)
            load(fc1_b[:, :], a["fc1_b"], s_const)
            load(fc2_b[:, :], a["fc2_b"].partition_broadcast(P), s_const)

            def stores(b):
                sp.wait_ge(s_h2c, b + 1)
                sp.dma_start(a["h2c"][:, b, :], h2_cls[:, :]).then_inc(s_hc, 16)
                sp.wait_ge(s_x2, NT * b + 1)
                sp.dma_start(a["x2c"][:, b, :], x2[0:NCLS, 0, :]).then_inc(s_xc, 16)
                sp.wait_ge(s_res, 2 * b + 1)
                sp.dma_start(a["out"][b, NCLS:P, :], res[NCLS:P, 0, :]).then_inc(s_stA, 16)
                sp.dma_start(a["out"][b, P:2 * P, :], res[:, 1, :]).then_inc(s_stA, 16)
                sp.wait_ge(s_res, 2 * b + 2)
                sp.dma_start(a["out"][b, 2 * P:T, :].rearrange("(t p) d -> p t d", p=P),
                             res[:, 2:NT, :]).then_inc(s_stB, 16)

            def body(i, has_back, has_next):
                if has_next:
                    sp.wait_ge(s_emb, 64 * (i + 1))
                    sp.dma_start(ids[:, :], a["ids"][i + 1, :, :]).then_inc(s_ids, 16)
                if has_back:
                    stores(i - 1)

            def cls_weights():
                sp.wait_ge(s_o, NP * B)
                for atom in range(NATOM):
                    sp.dma_start(w_in_at(atom, 0), a["ain_t"][atom, 0:P, :]).then_inc(s_cw, 16)
                    sp.dma_start(w_in_at(atom, 1)[0:D - P, :], a["ain_t"][atom, P:D, :]).then_inc(s_cw, 16)
                for atom in range(NATOM):
                    sp.dma_start(w_out_at(atom), a["aout_t"][atom, :, :].rearrange("(c p) d -> p c d", p=P)).then_inc(s_cw, 16)
                for n in range(NCLS):
                    s, q = n % 2, n // 2
                    rows = slice(q * B, (q + 1) * B)
                    for r in range(2):
                        gate_row = a["gate_pair"][n, r, :]
                        dst = SRC[n][1 - r]
                        sp.dma_start(gw_sb[rows, s, r, :], gate_row.partition_broadcast(B)).then_inc(s_cl, 16)
                        sp.dma_start(ob_sb[rows, s, r, :], a["aout_b"][dst, :].partition_broadcast(B)).then_inc(s_cl, 16)
                    sp.dma_start(bal_sb[rows, s, :], a["balance"][n, :].partition_broadcast(B)).then_inc(s_cl, 16)
                sp.dma_start(ib_sb, a["ain_b"]).then_inc(s_cl, 16)

            def cls_rows():
                sp.wait_ge(s_hc, 16 * B)
                sp.wait_ge(s_xc, 16 * B)
                for n in range(NCLS):
                    s, q = n % 2, n // 2
                    rows = slice(q * B, (q + 1) * B)
                    sp.dma_start(x2c_sb[rows, s, :], a["x2c"][n, :, :]).then_inc(s_cl, 16)
                    sp.dma_start(h2c_sb[rows, s, :], a["h2c"][n, :, :]).then_inc(s_cl, 16)
                sp.wait_ge(s_cd, CLS_STEPS)
                for n in range(NCLS):
                    s, q = n % 2, n // 2
                    sp.dma_start(a["out"][:, n, :], c_res[q * B:(q + 1) * B, s, :]).then_inc(s_cs, 16)
                sp.wait_ge(s_cs, 16 * NCLS)

            body(0, False, True)
            with sp.Fori(1, B - 1) as i:
                body(i, True, True)
            body(B - 1, True, False)
            cls_weights()
            stores(B - 1)
            sp.wait_ge(s_stA, 32 * B)
            sp.wait_ge(s_stB, 16 * B)
            cls_rows()

        @block.gpsimd
        def _(pool):
            nc.gpsimd.memset(neg_half[:, :], -0.5).then_inc(s_set_pool, 1)

            def gather(b):
                wait_apart(pool, s_ids, 16 * (b + 1))
                for t in range(NT):
                    nc.gpsimd.indirect_dma_start(
                        emb[:, t * R:(t + 1) * R], None, a["table"],
                        bass.IndirectOffsetOnAxis(ids[:, t:t + 1].bitcast(u32), 0)).then_inc(s_emb, 16)

            def rsqrt_ln1(b):
                pool.wait_ge(s_ln1, 10 * b + 9)
                nc.gpsimd.tensor_tensor(ln1_rstd[:, :], ln1_ve[:, :], neg_half[:, :], ALU.pow).then_inc(s_ln1p, 1)

            def rsqrt_ln2(b):
                pool.wait_ge(s_ln2, 10 * b + 9)
                nc.gpsimd.tensor_tensor(ln2_rstd[:, :], ln2_ve[:, :], neg_half[:, :], ALU.pow).then_inc(s_ln2p, 1)

            def rsqrt_gn(b):
                pool.wait_ge(s_gn, 8 * b + 5)
                nc.gpsimd.tensor_tensor(gn_rstd[:, :], gn_ve[:, :], neg_half[:, 0:NP], ALU.pow).then_inc(s_gnp, 1)

            def rotate(i, t):
                for k in range(2):
                    pool.wait_ge(s_rotm, 16 * i + 4 * t + 2 * k + 2)
                    if t == 0 and k == 0 and later(i):
                        pool.wait_ge(s_kv, NP * i)
                    nc.gpsimd.tensor_tensor(kq[:, t, k, :, :].rearrange("p h d -> p (h d)"), rot_c[:, k, :],
                                            rot_s[:, k, :], ALU.add).then_inc(s_rot, 1)

            def gating(b):
                pool.wait_ge(s_gate, NP * (b + 1))
                for m in range(NP):
                    pool.wait_ge(s_aff, NP * b + m + 1)
                    nc.gpsimd.tensor_tensor(att[:, m, :], att[:, m, :], gate[:, m, :], ALU.mult).then_inc(s_gated, 1)

            def body(i, has_back, has_next):
                if has_next:
                    pool.wait_ge(s_ln1, 10 * (i + 1))
                    gather(i + 1)
                if has_back:
                    gating(i - 1)
                rotate(i, 0)
                if has_back:
                    rsqrt_ln2(i - 1)
                for t in range(1, NT):
                    rotate(i, t)
                if has_next:
                    rsqrt_ln1(i + 1)
                rsqrt_gn(i)

            gather(0)
            pool.wait_ge(s_set_pool, 1)
            rsqrt_ln1(0)
            body(0, False, True)
            with nc.gpsimd.Fori(1, B - 1) as i:
                body(i, True, True)
            body(B - 1, True, False)
            gating(B - 1)
            rsqrt_ln2(B - 1)
            pool.wait_ge(s_cd, CD_SQ)
            nc.gpsimd.tensor_tensor(g_nrm, g_sq, g_half, ALU.pow).then_inc(s_cg, 1)

        @block.scalar
        def _(act):
            def emb_evac(b):
                if later(b):
                    act.wait_ge(s_hres, b)
                for k in range(2):
                    act.wait_ge(s_embT, 2 * b + k + 1)
                    nc.scalar.activation(emb_t[:, k * 256:(k + 1) * 256], bank_of("emb_t_ready", k)[:, 0:256],
                                         ACT.Copy).then_inc(s_embt, 1)

            def norm_evac(b):
                if later(b):
                    act.wait_ge(s_gproj, NP * b)
                act.wait_ge(s_normT, b + 1)
                nc.scalar.activation(norm_t[:, :], bank_of("norm_t_ready", 0)[:, :], ACT.Copy).then_inc(s_normt, 1)

            def v_evac(i, t):
                act.wait_ge(s_vproj, NT * i + t + 1)
                if t == 0 and later(i):
                    act.wait_ge(s_o, NP * i)
                nc.scalar.activation(v[:, t, :], bank_of("v_ready", t)[:, 0:VC], ACT.Copy).then_inc(s_v, 1)

            def tanhs(i):
                if later(i):
                    act.wait_ge(s_gated, NP * i)
                for m in range(NP):
                    act.wait_ge(s_gproj, NP * i + m + 1)
                    nc.scalar.activation(gate[:, m, :], bank_of("gate_ready", m)[:, :], ACT.Tanh, scale=0.5)\
                        .then_inc(s_tanh, 1)

            def pair_evac(i, p):
                if p == 2:
                    act.wait_ge(s_o, NP * i + 1)
                elif later(i):
                    act.wait_ge(s_o, NP * i - (0 if p == 0 else 1))
                for j in range(4):
                    act.wait_ge(s_T, 12 * i + 4 * p + j + 1)
                    nc.scalar.activation(kq_t[:, p % 2, j, :], bank_of("kq_t_ready", 4 * p + j)[:, :], ACT.Copy)\
                        .then_inc(s_t, 1)

            def att_evac(i, p):
                if p == 0 and later(i):
                    act.wait_ge(s_wo, 2 * i)
                act.wait_ge(s_o, NP * i + p + 1)
                nc.scalar.activation(att[:, p, :], bank_of("att_ready", p)[:, :], ACT.Copy).then_inc(s_att, 1)

            def gn_apply(b):
                act.wait_ge(s_gn, 8 * (b + 1))
                for m in range(NP):
                    nc.scalar.activation(att[:, m, :], att[:, m, :], ACT.Identity, bias=gn_c[:, m:m + 1],
                                         scale=gn_a[:, m:m + 1]).then_inc(s_aff, 1)

            def h2_class_rows(b):
                if later(b):
                    act.wait_ge(s_hc, 16 * b)
                act.wait_ge(s_ln2, 10 * b + 2)
                nc.scalar.activation(h2_cls[:, :], hb[0][0:NCLS, 0:D], ACT.Copy).then_inc(s_h2c, 1)

            def x2_norm(b):
                if later(b):
                    act.wait_ge(s_xc, 16 * b)
                    act.wait_ge(s_x2s, 2 * b)
                act.wait_ge(s_ln2, 10 * b + 10)
                for t in range(NT):
                    nc.scalar.activation(x2[:, t, :], hb[t // 2][:, (t % 2) * D:(t % 2 + 1) * D], ACT.Identity,
                                         bias=ln2_nmr[:, t:t + 1], scale=ln2_rstd[:, t:t + 1]).then_inc(s_x2, 1)

            def x2_evac(b):
                if later(b):
                    act.wait_ge(s_fc1, NF * b)
                for c in range(3):
                    act.wait_ge(s_x2T, 3 * b + c + 1)
                    nc.scalar.activation(x2_t[:, c, :], back[(1 + c) % 2][:, :], ACT.Copy).then_inc(s_x2t, 1)

            def gelu(b, m):
                if m == 0 and later(b):
                    act.wait_ge(s_fc2, 2 * b)
                act.wait_ge(s_fc1, NF * b + m + 1)
                nc.scalar.activation(hid[:, m, :], back[(4 + m) % 2][:, :], ACT.Gelu, bias=fc1_b[:, m:m + 1])\
                    .then_inc(s_hid, 1)

            def body(i, has_back, has_next):
                if has_back:
                    gn_apply(i - 1)
                v_evac(i, 0)
                if has_back:
                    h2_class_rows(i - 1)
                    x2_norm(i - 1)
                v_evac(i, 1)
                if has_back:
                    x2_evac(i - 1)
                    gelu(i - 1, 0)
                    gelu(i - 1, 1)
                v_evac(i, 2)
                if has_back:
                    gelu(i - 1, 2)
                    gelu(i - 1, 3)
                v_evac(i, 3)
                if has_back:
                    gelu(i - 1, 4)
                    gelu(i - 1, 5)
                tanhs(i)
                pair_evac(i, 0)
                pair_evac(i, 1)
                att_evac(i, 0)
                pair_evac(i, 2)
                att_evac(i, 1)
                if has_next:
                    emb_evac(i + 1)
                att_evac(i, 2)
                if has_next:
                    norm_evac(i + 1)

            act.wait_ge(s_const, N_CONST)
            emb_evac(0)
            norm_evac(0)
            body(0, False, True)
            with nc.scalar.Fori(1, B - 1) as i:
                body(i, True, True)
            body(B - 1, True, False)
            gn_apply(B - 1)
            h2_class_rows(B - 1)
            x2_norm(B - 1)
            x2_evac(B - 1)
            for m in range(NF):
                gelu(B - 1, m)

            act.wait_ge(s_cl, N_CL)
            act.wait_ge(s_fc2, 2 * B)
            for atom in range(NATOM):
                for m in range(NF):
                    k = NF * atom + m
                    act.wait_ge(s_ch, k + 1)
                    if atom < NQ:
                        o, n = c_hid[:, 0, m, :, atom, :], 2 * B
                        src = bank[k % RING][:, 0:n].rearrange("p (s b) -> p s b", s=2)
                    else:
                        o, n = c_hid[:, 1, m, atom - NQ, :, :].rearrange("p q b -> p (q b)"), NQ * B
                        src = bank[k % RING][:, 0:n]
                    nc.scalar.activation(o, src, ACT.Gelu, bias=ib_sb[:, atom, m:m + 1]).then_inc(s_chf, 1)
            act.wait_ge(s_cd, CD_DIFF)
            nc.scalar.activation(g_x[:, 4:6], g_x[:, 2:4], ACT.Tanh, scale=0.5).then_inc(s_ct, 1)

        @block.tensor
        def _(pe):
            mm = nc.tensor.matmul

            def turn_embeddings(b):
                pe.wait_ge(s_embsplit, 2 * (b + 1))
                for k in range(2):
                    o = take(pe, b - 1, "emb_t_ready", k)
                    for t in (2 * k, 2 * k + 1):
                        last = nc.tensor.transpose(o[:, (t % 2) * P:(t % 2 + 1) * P], emb_split[:, t, :].bitcast(fp32),
                                                   ident[:, :])
                    last.then_inc(s_embT, 1)

            def embed(o, t, starts):
                tok = emb_t[:, t * P:(t + 1) * P]
                mm(o, tok, up_hi[:, :], start=starts, stop=False, skip_group_check=True)
                return mm(o, tok, up_lo[:, :], start=False, stop=True, skip_group_check=True)

            def h_for_statistics(b):
                for k in range(2):
                    pe.wait_ge(s_embt, 2 * b + k + 1)
                    o = take(pe, b - 1, "ln1_steps", 2 * k + 1)
                    for t in (2 * k, 2 * k + 1):
                        last = embed(o[:, (t % 2) * D:(t % 2 + 1) * D], t, True)
                    last.then_inc(s_hstat, 1)

            def turn_norm(b):
                pe.wait_ge(s_normsplit, 2 * (b + 1))
                o = take(pe, b - 1, "norm_t_ready", 0)
                for t in range(NT):
                    last = nc.tensor.transpose(o[:, t * P:(t + 1) * P], norm_split[:, t, :].bitcast(fp32), ident[:, :])
                last.then_inc(s_normT, 1)

            def project(i, t):
                if t == 0:
                    pe.wait_ge(s_normt, i + 1)
                tok = norm_t[:, t * P:(t + 1) * P]
                for k in range(5):
                    name, index = ("rotary_products", 4 * t + k) if k < 4 else ("v_ready", t)
                    o = take(pe, i, name, index)[:, 0:BC]
                    mm(o, tok, w_hi[:, k * BC:(k + 1) * BC], start=True, stop=False)
                    mm(o, tok, w_lo[:, k * BC:(k + 1) * BC], start=False, stop=True).then_inc(s_proj if k < 4 else s_vproj, 1)

            def project_gate(i):
                for m in range(NP):
                    o = take(pe, i, "gate_ready", m)[:, :]
                    at = slice(G_AT + m * P, G_AT + (m + 1) * P)
                    mm(o, w_hi[:, at], norm_t[:, :], start=True, stop=False)
                    mm(o, w_lo[:, at], norm_t[:, :], start=False, stop=True).then_inc(s_gproj, 1)

            def residual(i):
                for t in range(NT):
                    if t % 2 == 0 and later(i):
                        pe.wait_ge(s_res, 2 * (i - 1) + t // 2 + 1)
                    last = embed(hb[t // 2][:, (t % 2) * D:(t % 2 + 1) * D], t, t % 2 == 0)
                last.then_inc(s_hres, 1)

            def turn_pair(i, p):
                if p == 0:
                    pe.wait_ge(s_rot, 2 * NT * (i + 1))
                for j in range(4):
                    o = take(pe, i, "kq_t_ready", 4 * p + j)
                    for t in range(NT):
                        last = nc.tensor.transpose(o[:, t * P:(t + 1) * P], kq[:, t, j % 2, 2 * p + j // 2, :], ident[:, :])
                    last.then_inc(s_T, 1)

            def key_values(i, p):
                if p == 0:
                    pe.wait_ge(s_v, NT * (i + 1))
                o = take(pe, i, "state_steps", 3 * p + 2)
                for c in range(NT - 1):
                    for j in range(2):
                        h = 2 * p + j
                        last = mm(o[:, c * P + j * DV:c * P + (j + 1) * DV], kq[:, c, 0, h, :],
                                  v[:, c, h * DV:(h + 1) * DV], start=True, stop=True)
                last.then_inc(s_kv, 1)

            def scores(i, p):
                for j in range(2):
                    pe.wait_ge(s_t, 12 * i + 4 * p + 2 * j + 2)
                    o = take(pe, i, "probs_ready", 2 * p + j)
                    for c in range(NT):
                        at = slice(c * P, (c + 1) * P)
                        last = mm(o[:, at], kq_t[:, p % 2, 2 * j, at], kq_t[:, p % 2, 2 * j + 1, at], start=True, stop=True)
                    last.then_inc(s_score, 1)

            def outputs(i, p):
                pe.wait_ge(s_prob, 6 * i + 2 * p + 2)
                pe.wait_ge(s_state, 9 * i + 3 * p + 3)
                o = take(pe, i, "att_ready", p)
                for c in range(NT):
                    at = slice(c * P, (c + 1) * P)
                    for j in range(2):
                        h = 2 * p + j
                        last = mm(o[j * DV:(j + 1) * DV, at], v[:, c, h * DV:(h + 1) * DV], probs[:, p % 2, j, at],
                                  start=True, stop=c == 0)
                    if c:
                        for j in range(2):
                            last = mm(o[j * DV:(j + 1) * DV, at], state[:, p % 2, c - 1, j * DV:(j + 1) * DV],
                                      kq_t[:, p % 2, 2 * j + 1, at], start=False, stop=True)
                last.then_inc(s_o, 1)

            def take_back(b, r):
                if r >= 6:
                    pe.wait_ge(s_hid, NF * b + r - 5)
                elif r >= 3:
                    pe.wait_ge(s_x2t, 3 * b + r - 2)
                elif r == 2:
                    pe.wait_ge(s_gn, 8 * b + 5)
                elif later(b):
                    pe.wait_ge(s_hid, NF * b - (1 - r))
                return back[r % 2]

            def gn_means(i):
                pe.wait_ge(s_gns, 6 * (i + 1))
                o = take_back(i, 0)
                mm(o[:, 0:NP], head_mean[:, :], gn_mean[:, :], start=True, stop=True).then_inc(s_gnpe, 1)

            def gn_variances(i):
                pe.wait_ge(s_gn, 8 * i + 4)
                mm(back[0][:, 4:4 + NP], head_mean[:, :], gn_m2[:, :], start=True, stop=True).then_inc(s_gnpe, 1)

            def out_project(b):
                for t in range(NT):
                    for m in range(NP):
                        if t == 0:
                            pe.wait_ge(s_gated, NP * b + m + 1)
                        last = mm(hb[t // 2][:, (t % 2) * D:(t % 2 + 1) * D], att[:, m, t * P:(t + 1) * P], wo[:, m, :],
                                  start=False, stop=m == NP - 1, skip_group_check=True)
                    if t % 2:
                        last.then_inc(s_wo, 1)

            def turn_x2(b):
                pe.wait_ge(s_x2s, 2 * (b + 1))
                for c in range(3):
                    o = take_back(b, 1 + c)
                    for t in range(NT):
                        last = nc.tensor.transpose(o[:, t * P:(t + 1) * P], x2_split[:, t, c * P:(c + 1) * P].bitcast(fp32),
                                                   ident[:, :])
                    last.then_inc(s_x2T, 1)

            def hidden(b, m):
                if m == 0:
                    pe.wait_ge(s_x2t, 3 * (b + 1))
                o = take_back(b, 4 + m)
                at = slice(m * P, (m + 1) * P)
                for c in range(3):
                    mm(o[:, :], fc1_hi[:, c, at], x2_t[:, c, :], start=c == 0, stop=False)
                for c in range(2):
                    last = mm(o[:, :], fc1_lo[:, c, at], x2_t[:, c, :], start=False, stop=c == 1)
                last.then_inc(s_fc1, 1)

            def second_layer(b):
                pe.wait_ge(s_h2c, b + 1)
                pe.wait_ge(s_x2, NT * (b + 1))
                for t in range(NT):
                    for m in range(NF):
                        if t == 0:
                            pe.wait_ge(s_hid, NF * b + m + 1)
                        last = mm(hb[t // 2][:, (t % 2) * D:(t % 2 + 1) * D], hid[:, m, t * P:(t + 1) * P], fc2[:, m, :],
                                  start=False, stop=m == NF - 1, skip_group_check=True)
                    if t % 2:
                        last.then_inc(s_fc2, 1)

            def body(i, has_back, has_next):
                project(i, 0)
                if has_back:
                    out_project(i - 1)
                project(i, 1)
                if has_back:
                    turn_x2(i - 1)
                    hidden(i - 1, 0)
                    hidden(i - 1, 1)
                project(i, 2)
                if has_back:
                    hidden(i - 1, 2)
                    hidden(i - 1, 3)
                project(i, 3)
                if has_back:
                    hidden(i - 1, 4)
                    hidden(i - 1, 5)
                project_gate(i)
                if has_back:
                    second_layer(i - 1)
                residual(i)
                turn_pair(i, 0)
                key_values(i, 0)
                scores(i, 0)
                turn_pair(i, 1)
                key_values(i, 1)
                outputs(i, 0)
                scores(i, 1)
                turn_pair(i, 2)
                key_values(i, 2)
                outputs(i, 1)
                scores(i, 2)
                if has_next:
                    turn_embeddings(i + 1)
                outputs(i, 2)
                if has_next:
                    h_for_statistics(i + 1)
                gn_means(i)
                if has_next:
                    turn_norm(i + 1)
                gn_variances(i)

            pe.wait_ge(s_stage, N_STAGE)
            for o, cols in ((bank[0][:, 0:2 * R], slice(0, P)), (bank[1][0:D - P, 0:2 * R], slice(P, D))):
                mm(o, center[:, cols], up_dup[:, 0:2 * R], start=True, stop=False)
                last = mm(o, center[0:D - P, D + cols.start:D + cols.stop], up_dup[0:D - P, 2 * R:4 * R], start=False, stop=True)
            last.then_inc(s_set_pe, 1)
            pe.wait_ge(s_set_dve, 2)
            for n in range(WC // BC):
                if n >= RING:
                    pe.wait_ge(s_set_dve, 2 + 2 * (n - RING + 1))
                o, at = bank[n % RING][:, 0:BC], slice(n * BC, (n + 1) * BC)
                mm(o, up_cen[:, 0:2 * R], wa[:, at], start=True, stop=False)
                mm(o, up_cen[0:D - P, 2 * R:4 * R], wb[:, at], start=False, stop=True).then_inc(s_set_pe, 1)
            pe.wait_ge(s_set_dve, N_SET)
            pe.wait_ge(s_const, N_CONST)
            turn_embeddings(0)
            h_for_statistics(0)
            turn_norm(0)

            body(0, False, True)
            with nc.tensor.Fori(1, B - 1) as i:
                body(i, True, True)
            body(B - 1, True, False)
            out_project(B - 1)
            turn_x2(B - 1)
            for m in range(NF):
                hidden(B - 1, m)
            second_layer(B - 1)

            pe.wait_ge(s_cl, N_CL)
            for s in range(2):
                for c, n in ((0, P), (1, D - P)):
                    last = nc.tensor.transpose(bank[2 * s + c][0:n, 0:CT], x2c_sb[:, s, c * P:c * P + n], ident[0:CT, 0:CT])
            last.then_inc(s_cpe, 1)
            pe.wait_ge(s_cw, N_CW)
            pe.wait_ge(s_cd, CD_T)
            for atom in range(NATOM):
                for m in range(NF):
                    k = NF * atom + m
                    if k >= RING:
                        pe.wait_ge(s_chf, k - RING + 1)
                    n = 2 * B if atom < NQ else NQ * B
                    o = bank[k % RING][:, 0:n]
                    for c, rows in ((0, P), (1, D - P)):
                        x = x2c_t[0:rows, c, :].rearrange("p (s q b) -> p s q b", s=2, q=NQ)
                        x = x[:, :, atom, :] if atom < NQ else x[:, atom - NQ, :, :]
                        last = mm(o, w_in_at(atom, c)[0:rows, m * P:(m + 1) * P], x, start=c == 0, stop=c == 1)
                    last.then_inc(s_ch, 1)
            pe.wait_ge(s_chf, NATOM * NF)
            for s in range(2):
                for m in range(NF):
                    last = mm(bank[s][0:CT, 0:D], c_hid[:, 0, m, s, :, :].rearrange("p q b -> p (q b)"),
                              w_out_at(NQ + s)[:, m, :], start=m == 0, stop=m == NF - 1)
            for s in range(2):
                for m in range(NF):
                    for q in range(NQ):
                        last = mm(bank[2 + s][q * B:(q + 1) * B, 0:D], c_hid[:, 1, m, s, q, :],
                                  w_out_at(q)[:, m, :], start=m == 0, stop=m == NF - 1)
            last.then_inc(s_co, 1)

        @block.vector
        def _(dve):
            V = nc.vector

            def split(dst_hi, dst_lo, src, s, at):
                V.tensor_copy(dst_hi, src).then_inc(s, 1)
                dve.wait_ge(s, at + 1)
                V.tensor_tensor(dst_lo, src, dst_hi.bitcast(fp32), ALU.subtract).then_inc(s, 1)

            def split_embeddings(b):
                dve.wait_ge(s_emb, 64 * (b + 1))
                if later(b):
                    dve.wait_ge(s_embT, 2 * b)
                split(emb_split[:, :, 0:R], emb_split[:, :, R:2 * R], emb[:, :].rearrange("p (t r) -> p t r", t=NT),
                      s_embsplit, 2 * b)

            def layer_statistics(b, stats, mv, ve, s, source, ready):
                for t in range(NT):
                    if t % 2 == 0:
                        dve.wait_ge(ready, 2 * b + t // 2 + 1)
                    V.bn_stats(stats[:, t, :], source[t // 2][:, (t % 2) * D:(t % 2 + 1) * D]).then_inc(s, 1)
                wait_apart(dve, s, 10 * b + NT)
                for t in range(NT):
                    V.bn_aggr(mv[:, t, :], stats[:, t, :]).then_inc(s, 1)
                dve.wait_ge(s, 10 * b + 2 * NT)
                V.tensor_scalar(ve[:, :], mv[:, :, 1], LN_EPS, None, ALU.add).then_inc(s, 1)

            def statistics_ln1(b):
                banks = [bank_of("ln1_steps", 1), bank_of("ln1_steps", 3)]
                layer_statistics(b, ln1_st, ln1_mv, ln1_ve, s_ln1, banks, s_hstat)

            def normalise_embeddings(b):
                dve.wait_ge(s_ln1p, b + 1)
                V.tensor_tensor(emb_norm[:, :, :], emb[:, :].rearrange("p (t r) -> p t r", t=NT),
                                ln1_rstd[:, :].unsqueeze(2).broadcast_to([P, NT, R]), ALU.mult).then_inc(s_ln1, 1)
                if later(b):
                    dve.wait_ge(s_normT, b)
                dve.wait_ge(s_ln1, 10 * (b + 1))
                split(norm_split[:, :, 0:R], norm_split[:, :, R:2 * R], emb_norm[:, :, :], s_normsplit, 2 * b)

            def rotary(i, t):
                for k in range(4):
                    if k % 2 == 0 and (t or later(i)):
                        dve.wait_ge(s_rot, 2 * NT * i + 2 * t + k // 2 - 1)
                    dve.wait_ge(s_proj, 16 * i + 4 * t + k + 1)
                    src = bank_of("rotary_products", 4 * t + k)[:, 0:BC].rearrange("p (h s d) -> p h s d", h=3, s=2)
                    at, heads = slice((k % 2) * BC, (k % 2 + 1) * BC), slice(3 * (k % 2), 3 * (k % 2) + 3)
                    V.tensor_tensor(rot_c[:, k // 2, at].rearrange("p (h s d) -> p h s d", h=3, s=2), src,
                                    cos_t[:, t, k // 2, heads, :].unsqueeze(2).broadcast_to([P, 3, 2, HALF]), ALU.mult)
                    V.tensor_tensor(rot_s[:, k // 2, at].rearrange("p (h s d) -> p h s d", h=3, s=2), src[:, :, ::-1, :],
                                    sin_t[:, t, k // 2, heads, :].rearrange("p h (s d) -> p h s d", s=2), ALU.mult)\
                        .then_inc(s_rotm, 1)

            def gates(i):
                for m in range(NP):
                    dve.wait_ge(s_tanh, NP * i + m + 1)
                    V.scalar_tensor_tensor(gate[:, m, :], gate[:, m, :], 1.0, bank_of("gate_ready", m)[:, :], ALU.add, ALU.mult)\
                        .then_inc(s_gate, 1)

            def states(i, p):
                dve.wait_ge(s_kv, NP * i + p + 1)
                if p == 2:
                    dve.wait_ge(s_o, NP * i + 1)
                elif later(i):
                    dve.wait_ge(s_o, NP * i - (0 if p == 0 else 1))
                src = bank_of("state_steps", 3 * p + 2)
                V.tensor_copy(state[:, p % 2, 0, :], src[:, 0:P]).then_inc(s_state, 1)
                for c in range(1, NT - 1):
                    dve.wait_ge(s_state, 9 * i + 3 * p + c)
                    V.tensor_tensor(state[:, p % 2, c, :], src[:, c * P:(c + 1) * P], state[:, p % 2, c - 1, :], ALU.add)\
                        .then_inc(s_state, 1)

            def mask(i, p):
                if p == 2:
                    dve.wait_ge(s_o, NP * i + 1)
                elif later(i):
                    dve.wait_ge(s_o, NP * i - (0 if p == 0 else 1))
                for j in range(2):
                    dve.wait_ge(s_score, 6 * i + 2 * p + j + 1)
                    V.tensor_tensor(probs[:, p % 2, j, :].rearrange("p (c t) -> p c t", c=NT),
                                    bank_of("probs_ready", 2 * p + j)[:, :].rearrange("p (c t) -> p c t", c=NT),
                                    causal[:, :].unsqueeze(1).broadcast_to([P, NT, P]), ALU.mult).then_inc(s_prob, 1)

            def channel_statistics(i, p):
                dve.wait_ge(s_att, NP * i + p + 1)
                V.bn_stats(gn_st[:, p, :], att[:, p, :]).then_inc(s_gns, 1)

            def head_statistics(i):
                wait_apart(dve, s_gns, 6 * i + 3)
                for p in range(NP):
                    V.bn_aggr(gn_mv[:, p, :], gn_st[:, p, :]).then_inc(s_gns2, 1)
                dve.wait_ge(s_gns2, 3 * i + 3)
                for p in range(NP):
                    V.tensor_copy(gn_mean[:, p:p + 1], gn_mv[:, p, 0:1]).then_inc(s_gns, 1)

            def head_means(i):
                dve.wait_ge(s_gnpe, 2 * i + 1)
                V.tensor_copy(gn_dd[:, :], back[0][:, 0:NP]).then_inc(s_gn, 1)
                dve.wait_ge(s_gn, 8 * i + 1)
                V.tensor_tensor(gn_d[:, :], gn_mean[:, :], gn_dd[:, :], ALU.subtract).then_inc(s_gn, 1)
                dve.wait_ge(s_gn, 8 * i + 2)
                V.tensor_tensor(gn_ma[:, :], gn_d[:, :], gn_d[:, :], ALU.mult).then_inc(s_gn, 1)
                dve.wait_ge(s_gn, 8 * i + 3)
                V.tensor_tensor(gn_m2[:, :], gn_ma[:, :], gn_mv[:, :, 1], ALU.add).then_inc(s_gn, 1)

            def head_factors(i):
                dve.wait_ge(s_gnpe, 2 * i + 2)
                V.tensor_scalar(gn_ve[:, :], back[0][:, 4:4 + NP], LN_EPS, None, ALU.add).then_inc(s_gn, 1)
                dve.wait_ge(s_gnp, i + 1)
                V.scalar_tensor_tensor(gn_a[:, :], gn_w[:, :], 0.5, gn_rstd[:, :], ALU.mult, ALU.mult).then_inc(s_gn, 1)
                dve.wait_ge(s_gn, 8 * i + 6)
                V.tensor_tensor(gn_ma[:, :], gn_dd[:, :], gn_a[:, :], ALU.mult).then_inc(s_gn, 1)
                dve.wait_ge(s_gn, 8 * i + 7)
                V.scalar_tensor_tensor(gn_c[:, :], gn_b[:, :], 0.5, gn_ma[:, :], ALU.mult, ALU.subtract).then_inc(s_gn, 1)

            def statistics_ln2(b):
                layer_statistics(b, ln2_st, ln2_mv, ln2_ve, s_ln2, hb, s_wo)

            def shift_ln2(b):
                dve.wait_ge(s_ln2p, b + 1)
                V.scalar_tensor_tensor(ln2_nmr[:, :], ln2_mv[:, :, 0], -1.0, ln2_rstd[:, :], ALU.mult, ALU.mult)\
                    .then_inc(s_ln2, 1)

            def split_x2(b):
                dve.wait_ge(s_x2, NT * (b + 1))
                if later(b):
                    dve.wait_ge(s_x2T, 3 * b)
                split(x2_split[:, :, 0:D], x2_split[:, :, D:2 * D], x2[:, :, :], s_x2s, 2 * b)

            def result(b):
                for k in range(2):
                    dve.wait_ge(s_fc2, 2 * b + k + 1)
                    if later(b):
                        dve.wait_ge((s_stA, s_stB)[k], (32, 16)[k] * b)
                    V.tensor_tensor(res[:, 2 * k:2 * k + 2, :], hb[k][:, 0:2 * D].rearrange("p (t d) -> p t d", t=2),
                                    fc2_b[:, :].unsqueeze(1).broadcast_to([P, 2, D]), ALU.add).then_inc(s_res, 1)

            def body(i, has_back, has_next):
                rotary(i, 0)
                if has_back:
                    statistics_ln2(i - 1)
                    shift_ln2(i - 1)
                rotary(i, 1)
                if has_back:
                    split_x2(i - 1)
                rotary(i, 2)
                rotary(i, 3)
                gates(i)
                if has_back:
                    result(i - 1)
                states(i, 0)
                mask(i, 0)
                states(i, 1)
                channel_statistics(i, 0)
                mask(i, 1)
                states(i, 2)
                channel_statistics(i, 1)
                if has_next:
                    split_embeddings(i + 1)
                mask(i, 2)
                if has_next:
                    statistics_ln1(i + 1)
                channel_statistics(i, 2)
                head_statistics(i)
                if has_next:
                    normalise_embeddings(i + 1)
                head_means(i)
                head_factors(i)

            dve.wait_ge(s_set_pe, 1)
            V.tensor_copy(up_cen[:, 0:2 * R], bank[0][:, 0:2 * R]).then_inc(s_set_dve, 1)
            V.tensor_copy(up_cen[0:D - P, 2 * R:4 * R], bank[1][0:D - P, 0:2 * R]).then_inc(s_set_dve, 1)
            for n in range(WC // BC):
                dve.wait_ge(s_set_pe, 2 + n)
                at = slice(n * BC, (n + 1) * BC)
                split(w_hi[:, at], w_lo[:, at], bank[n % RING][:, 0:BC], s_set_dve, 2 + 2 * n)
            done = 2 + 2 * (WC // BC)
            dve.wait_ge(s_stage, N_STAGE)
            split(up_hi[:, :], up_lo[:, :], up_stage, s_set_dve, done)
            V.tensor_copy(fc1_hi[:, :, :], fc1_stage.rearrange("p (c f) -> p c f", c=3)).then_inc(s_set_dve, 1)
            dve.wait_ge(s_set_dve, done + 3)
            V.tensor_tensor(fc1_lo[:, :, :], fc1_stage[:, 0:2 * F].rearrange("p (c f) -> p c f", c=2),
                            fc1_hi[:, 0:2, :].bitcast(fp32), ALU.subtract).then_inc(s_set_dve, 1)
            dve.wait_ge(s_const, N_CONST)
            split_embeddings(0)
            statistics_ln1(0)
            normalise_embeddings(0)

            body(0, False, True)
            with nc.vector.Fori(1, B - 1) as i:
                body(i, True, True)
            body(B - 1, True, False)
            statistics_ln2(B - 1)
            shift_ln2(B - 1)
            split_x2(B - 1)
            result(B - 1)

            step = [0]

            def chain(ins):
                ins.then_inc(s_cd, 1)
                step[0] += 1
                dve.wait_ge(s_cd, step[0])

            dve.wait_ge(s_rot, 2 * NT * B)
            V.memset(g_half, 0.5).then_inc(s_cd, 1)
            step[0] += 1
            dve.wait_ge(s_cl, N_CL)
            dve.wait_ge(s_cpe, 1)
            for s in range(2):
                for c, n in ((0, P), (1, D - P)):
                    V.tensor_copy(x2c_t[0:n, c, s * CT:(s + 1) * CT], bank[2 * s + c][0:n, 0:CT]).then_inc(s_cd, 1)
                    step[0] += 1
            assert step[0] == CD_T

            def dot(o, x, y):
                chain(V.tensor_tensor_reduce(out=g_junk, in0=x, in1=y, scale=1.0, scalar=0.0, op0=ALU.mult,
                                             op1=ALU.add, accum_out=o))

            for s in range(2):
                dot(g_sq[:, s:s + 1], x2c_sb[:, s, :], x2c_sb[:, s, :])
                for r in range(2):
                    k = 2 * s + r
                    dot(g_sq[:, 2 + k:3 + k], gw_sb[:, s, r, :], gw_sb[:, s, r, :])
                    dot(g_dot[:, k:k + 1], x2c_sb[:, s, :], gw_sb[:, s, r, :])
            assert step[0] == CD_SQ
            dve.wait_ge(s_cg, 1)
            chain(V.tensor_scalar(g_nrm, g_nrm, 1e-12, None, ALU.max))
            chain(V.reciprocal(g_sq, g_nrm))
            logits = g_log.rearrange("p s r -> p (s r)")
            chain(V.tensor_tensor(logits, g_dot, g_sq[:, 2:6], ALU.mult))
            chain(V.tensor_tensor(g_log, g_log, g_sq[:, 0:2].unsqueeze(2).broadcast_to([CT, 2, 2]), ALU.mult))
            chain(V.tensor_tensor(g_log, g_log, bal_sb, ALU.add))
            d = g_x[:, 0:2]
            chain(V.tensor_tensor(d, g_log[:, :, 1], g_log[:, :, 0], ALU.subtract))
            chain(V.tensor_scalar(g_x[:, 8:10], d, -1.0, None, ALU.mult))
            chain(V.tensor_tensor(g_x[:, 2:4], d, g_x[:, 8:10], ALU.max))
            assert step[0] == CD_DIFF
            chain(V.tensor_scalar(g_x[:, 10:12], d, 0.0, None, ALU.is_gt))
            chain(V.tensor_scalar(g_x[:, 12:14], g_x[:, 10:12], -1.0, 1.0, ALU.mult, ALU.add))
            dve.wait_ge(s_ct, 1)
            chain(V.tensor_scalar(g_x[:, 6:8], g_x[:, 4:6], 0.5, 0.5, ALU.mult, ALU.add))
            dve.wait_ge(s_co, 1)
            for s in range(2):
                chain(V.tensor_tensor(c_a, bank[s][0:CT, 0:D], ob_sb[:, s, 0, :], ALU.add))
                chain(V.tensor_scalar(c_b, c_a, g_x[:, 12 + s:13 + s], None, ALU.mult))
                chain(V.tensor_tensor(c_c, bank[2 + s][0:CT, 0:D], ob_sb[:, s, 1, :], ALU.add))
                chain(V.scalar_tensor_tensor(c_a, c_c, g_x[:, 10 + s:11 + s], c_b, ALU.mult, ALU.add))
                chain(V.scalar_tensor_tensor(c_res[:, s, :], c_a, g_x[:, 6 + s:7 + s], h2c_sb[:, s, :], ALU.mult, ALU.add))
            assert step[0] == CLS_STEPS


def tables():
    f = np.float32
    half = np.arange(HALF, dtype=f)
    inv_freq = (f(1.0) / np.power(f(10000.0), half / f(HALF))).astype(f)
    pos = np.arange(T, dtype=f)
    angle = (pos[:, None] * inv_freq[None, :]).astype(f).astype(np.float64)
    zeta = ((half + f(HALF)) / f(DK)).astype(np.float64)
    p64 = np.arange(T, dtype=np.float64)
    cos = np.zeros((T, 2, H, HALF))
    sin = np.zeros((T, 2, H, DK))
    for h in range(H):
        gamma = 1.0 - 2.0 ** (-(5 + h))
        rows = np.cumsum(gamma ** p64)
        for k, sign in ((0, -1.0), (1, 1.0)):
            scale = zeta[None, :] ** (sign * p64[:, None] / 512.0) * (gamma ** (sign * p64))[:, None]
            if k == 1:
                scale = scale * (DK ** -0.5 / np.sqrt(np.maximum(rows, 1e-6)))[:, None]
            cos[:, k, h, :] = np.cos(angle) * scale
            sin[:, k, h, :HALF] = -np.sin(angle) * scale
            sin[:, k, h, HALF:] = np.sin(angle) * scale
    lay = lambda x: np.ascontiguousarray(x.reshape(NT, P, 2, H, -1).transpose(1, 0, 2, 3, 4).astype(f))
    return lay(cos), lay(sin)


def columns(x):
    return x.reshape(-1, P).T


def kernel(**inputs):
    import concourse.bacc as bacc
    from concourse.bass_utils import run_bass_kernel_spmd as run

    given = {k: np.asarray(x) for k, x in inputs.items()}
    cos, sin = tables()
    heads = np.zeros((P, P), np.float32)
    heads[:DV, :DV] = heads[DV:, DV:] = 1.0 / DV
    arrays = {
        "ids": given["x"].reshape(B, NT, P).transpose(0, 2, 1),
        "table": given["L0_tok_embed_table"], "up": given["L0_tok_proj_up"], "up_t": given["L0_tok_proj_up"].T,
        "wk": given["L0_attn_Wk"], "wq": given["L0_attn_Wq"], "wv": given["L0_attn_Wv"], "wg": given["L0_attn_Wg"],
        "wo": given["L0_attn_Wo"], "gn_w": columns(given["L0_attn_gn_weight"]), "gn_b": columns(given["L0_attn_gn_bias"]),
        "fc1_t": given["L0_ffn_fc1_w"].T, "fc1_b": columns(given["L0_ffn_fc1_b"]),
        "fc2_t": given["L0_ffn_fc2_w"].T, "fc2_b": given["L0_ffn_fc2_b"],
        "gate_pair": given["L0_ffn_gate_pair"], "balance": given["L0_ffn_balance_bias"],
        "ain_t": given["L0_ffn_atom_in_w"].transpose(0, 2, 1), "ain_b": given["L0_ffn_atom_in_b"].reshape(NATOM, NF, P).transpose(2, 0, 1),
        "aout_t": given["L0_ffn_atom_out_w"].transpose(0, 2, 1), "aout_b": given["L0_ffn_atom_out_b"],
        "cos_t": cos, "sin_t": sin, "ident": np.eye(P, dtype=np.float32), "head_mean": heads,
        "causal": np.triu(np.ones((P, P), np.float32)),
        "center": (np.eye(D) - 1.0 / D).astype(np.float32),
    }
    nc = bacc.Bacc("TRN2", target_bir_lowering=False, num_devices=1)
    fed, a = {}, {}
    for name, x in arrays.items():
        fed[f"in_{name}"] = np.ascontiguousarray(x)
        a[name] = nc.dram_tensor(f"in_{name}", x.shape, mybir.dt.from_np(x.dtype), kind="ExternalInput").ap()
    for name in ("x2c", "h2c"):
        a[name] = nc.dram_tensor(name, (NCLS, B, D), mybir.dt.float32, kind="Internal").ap()
    a["out"] = nc.dram_tensor("out", (B, T, D), mybir.dt.float32, kind="ExternalOutput").ap()
    build(nc, a)
    return run(nc, [fed], core_ids=[0]).results[0]["out"]
```

```python
import concourse.bass as bass
from concourse import mybir
from contextlib import ExitStack
import numpy as np

B, T = 32, 512
VOCAB, R, D = 12565, 64, 192
H, DK, DV = 6, 128, 64
F = 768
NCLS, NATOM = 6, 5
SRC = [(0, 3), (0, 4), (1, 3), (1, 4), (2, 3), (2, 4)]
P = 128
NT = T // P
NP = H // 2
HALF = DK // 2
QK = H * DK
VC = H * DV
WC = 2 * QK + 2 * VC
V_AT, G_AT = 2 * QK, 2 * QK + VC
NF = F // P
BC = 3 * DK
LN_EPS = 1e-5

RING = 4


def front_jobs():
    jobs = []
    for t in range(NT):
        jobs += [("rotary_products", 4 * t + k, 4 * NT) for k in range(4)] + [("v_ready", t, NT)]
    jobs += [("gate_ready", m, NP) for m in range(NP)]
    turned = [[("kq_t_ready", 4 * p + j, 4 * NP) for j in range(4)] for p in range(NP)]
    states = [[("state_steps", 3 * p + 2, 3 * NP)] for p in range(NP)]
    scores = [[("probs_ready", 2 * p + j, 2 * NP) for j in range(2)] for p in range(NP)]
    outs = [[("att_ready", p, NP)] for p in range(NP)]
    jobs += turned[0] + states[0] + scores[0]
    jobs += turned[1] + states[1] + outs[0] + scores[1]
    jobs += turned[2] + states[2] + outs[1]
    jobs += [("emb_t_ready", k, 2) for k in range(2)] + scores[2]
    jobs += [("ln1_steps", k, 10) for k in (1, 3)] + outs[2] + [("norm_t_ready", 0, 1)]
    return jobs


JOBS = front_jobs()
assert len(JOBS) % RING == 0
NEXT = ("emb_t_ready", "ln1_steps", "norm_t_ready")


def job(name, index):
    return next(q for q, (n, k, _) in enumerate(JOBS) if (n, k) == (name, index))


def user_before(i, q):
    turn = 0
    while True:
        q -= RING
        if q < 0:
            q += len(JOBS)
            turn -= 1
        name, index, count = JOBS[q]
        if isinstance(i, int):
            if i + turn < -1:
                return None
            if i + turn == -1 and name not in NEXT or i + turn == B - 1 and name in NEXT:
                continue
        return name, (i + turn + (name in NEXT)) * count + index + 1


def build(nc, a):
    fp32, f32r = mybir.dt.float32, mybir.dt.float32r
    u32 = mybir.dt.uint32
    ALU, ACT = mybir.AluOpType, mybir.ActivationFunctionType

    with ExitStack() as ctx:
        def sb(name, shape, dt=fp32):
            return ctx.enter_context(nc.sbuf_tensor(name, shape, dt))

        def sem(name):
            return ctx.enter_context(nc.semaphore(name))

        ident = sb("ident", [P, P])
        head_mean = sb("head_mean", [P, P])
        causal = sb("causal", [P, P])
        cos_t = sb("cos_t", [P, NT, 2, H, HALF])
        sin_t = sb("sin_t", [P, NT, 2, H, DK])
        w_hi = sb("w_hi", [P, WC], f32r)
        w_lo = sb("w_lo", [P, WC], f32r)
        up_hi = sb("up_hi", [P, D], f32r)
        up_lo = sb("up_lo", [P, D], f32r)
        fc1_hi = sb("fc1_hi", [P, 3, F], f32r)
        fc1_lo = sb("fc1_lo", [P, 2, F], f32r)
        fc1_b = sb("fc1_b", [P, NF])
        fc2 = sb("fc2", [P, NF, D])
        fc2_b = sb("fc2_b", [P, D])
        wo = sb("wo", [P, NP, D])
        gn_w = sb("gn_w", [P, NP])
        gn_b = sb("gn_b", [P, NP])
        neg_half = sb("neg_half", [P, NT])

        ids = sb("ids", [P, NT], mybir.dt.int32)
        emb = sb("emb", [P, NT * R])
        emb_split = sb("emb_split", [P, NT, 2 * R], f32r)
        emb_norm = sb("emb_norm", [P, NT, R])
        norm_split = sb("norm_split", [P, NT, 2 * R], f32r)
        emb_t = sb("emb_t", [P, T], f32r)
        emb_keep = sb("emb_keep", [P, T], f32r)
        norm_t = sb("norm_t", [P, T], f32r)
        ln1_st = sb("ln1_st", [P, NT, 6])
        ln1_mv = sb("ln1_mv", [P, NT, 2])
        ln1_ve = sb("ln1_ve", [P, NT])
        ln1_rstd = sb("ln1_rstd", [P, NT])
        rot_c = sb("rot_c", [P, 2, QK])
        rot_s = sb("rot_s", [P, 2, QK])
        kq = sb("kq", [P, NT, 2, H, DK])
        v = sb("v", [P, NT, VC])
        gate = sb("gate", [P, NP, T])
        kq_t = sb("kq_t", [P, 2, 4, T])
        state = sb("state", [P, 2, NT - 1, P])
        probs = sb("probs", [P, 2, 2, T])
        att = sb("att", [P, NP, T])
        gn_st = sb("gn_st", [P, NP, 6])
        gn_mv = sb("gn_mv", [P, NP, 2])
        gn_d = sb("gn_d", [P, NP])
        gn_dd = sb("gn_dd", [P, NP])
        gn_m2 = sb("gn_m2", [P, NP])
        gn_ve = sb("gn_ve", [P, NP])
        gn_rstd = sb("gn_rstd", [P, NP])
        gn_a = sb("gn_a", [P, NP])
        gn_ma = sb("gn_ma", [P, NP])
        gn_c = sb("gn_c", [P, NP])
        ln2_st = sb("ln2_st", [P, NT, 6])
        ln2_mv = sb("ln2_mv", [P, NT, 2])
        ln2_ve = sb("ln2_ve", [P, NT])
        ln2_rstd = sb("ln2_rstd", [P, NT])
        ln2_nmr = sb("ln2_nmr", [P, NT])
        x2 = sb("x2", [P, NT, D])
        x2_split = sb("x2_split", [P, NT, 2 * D], f32r)
        x2_t = sb("x2_t", [P, 3, T], f32r)
        hid = sb("hid", [P, NF, T])
        h2_cls = sb("h2_cls", [NCLS, D])
        res = sb("res", [P, NT, D])

        bank = [ctx.enter_context(nc.psum_tensor(f"ring{k}", [P, 512], fp32)) for k in range(RING)]
        back = [ctx.enter_context(nc.psum_tensor(f"back{k}", [P, 512], fp32)) for k in range(2)]
        hb = [ctx.enter_context(nc.psum_tensor(f"resid{k}", [P, 512], fp32)) for k in range(2)]

        w_stage = kq[:, :, :, :, :].rearrange("p t a h d -> p (t a h d)")
        wa = w_stage[:, 0:WC]
        wb = w_stage[0:D - P, WC:2 * WC]
        fc1_stage = hid[:, :, :].rearrange("p c t -> p (c t)")[:, 0:3 * F]
        center = rot_s[:, 0, 0:2 * D]
        up_dup = rot_s[:, 0, 2 * D:2 * D + 4 * R]
        up_cen = rot_s[:, 1, 0:4 * R]
        up_stage = rot_s[:, 1, 4 * R:4 * R + D]

        s_const = sem("constants_loaded")
        s_stage = sem("weights_staged")
        s_set_pe = sem("setup_products")
        s_set_dve = sem("setup_steps")
        s_set_pool = sem("exponents_ready")
        s_ids = sem("ids_loaded")
        s_emb = sem("embeddings_gathered")
        s_embsplit = sem("embedding_split")
        s_embT = sem("embedding_transposed")
        s_embt = sem("emb_t_ready")
        s_hstat = sem("h_for_ln1")
        s_ln1 = sem("ln1_steps")
        s_ln1p = sem("ln1_rstd_ready")
        s_normsplit = sem("norm_split_ready")
        s_normT = sem("norm_transposed")
        s_normt = sem("norm_t_ready")
        s_proj = sem("kq_projected")
        s_vproj = sem("v_projected")
        s_gproj = sem("gate_projected")
        s_rotm = sem("rotary_products")
        s_rot = sem("kq_rotated")
        s_v = sem("v_ready")
        s_tanh = sem("gate_tanh")
        s_gate = sem("gate_ready")
        s_T = sem("kq_transposed")
        s_t = sem("kq_t_ready")
        s_kv = sem("kv_products")
        s_state = sem("state_steps")
        s_score = sem("scores_done")
        s_prob = sem("probs_ready")
        s_o = sem("attention_out")
        s_att = sem("att_ready")
        s_gns = sem("gn_channel_stats")
        s_gns2 = sem("gn_channel_sums")
        s_gnpe = sem("gn_head_sums")
        s_gn = sem("gn_steps")
        s_gnp = sem("gn_rstd_ready")
        s_aff = sem("gn_applied")
        s_gated = sem("gated_ready")
        s_keep = sem("embeddings_kept")
        s_hres = sem("residual_product")
        s_wo = sem("h2_done")
        s_ln2 = sem("ln2_steps")
        s_ln2p = sem("ln2_rstd_ready")
        s_x2 = sem("x2_ready")
        s_x2s = sem("x2_split_ready")
        s_x2T = sem("x2_transposed")
        s_x2t = sem("x2_t_ready")
        s_fc1 = sem("fc1_product")
        s_hid = sem("hidden_ready")
        s_fc2 = sem("fc2_product")
        s_res = sem("result_ready")
        s_h2c = sem("h2_cls_ready")
        s_stA = sem("result_stored_first_tiles")
        s_stB = sem("result_stored_last_tiles")
        s_xc = sem("x2_cls_stored")
        s_hc = sem("h2_cls_stored")
        by_name = {"rotary_products": s_rotm, "v_ready": s_v, "gate_ready": s_gate, "kq_t_ready": s_t,
                   "state_steps": s_state, "probs_ready": s_prob, "att_ready": s_att,
                   "emb_t_ready": s_embt, "ln1_steps": s_ln1, "norm_t_ready": s_normt}

        s_apart = {nc.vector: sem("dve_went_on"), nc.gpsimd: sem("pool_went_on")}
        N_STAGE, N_CONST = 16 * 20, 16 * 11
        N_SET = 2 + 2 * (WC // BC) + 4
        N_CL, N_CW = 16 * (NCLS * 7 + 1), 16 * NATOM * 3
        CD_T, CD_SQ, CD_DIFF, CLS_STEPS = 5, 15, 23, 36

        def wait_apart(eng, s, value):
            eng.wait_ge(s, value)
            eng.sem_inc(s_apart[eng], 1)

        def later(i):
            return not (isinstance(i, int) and i == 0)

        def bank_of(name, index):
            return bank[job(name, index) % RING]

        def take(pe, i, name, index):
            q = job(name, index)
            before = user_before(i, q)
            if before:
                pe.wait_ge(by_name[before[0]], before[1])
            return bank[q % RING]

        NQ = NCLS // 2
        CT = NQ * B
        flat = w_stage
        rows_c = rot_c[0:CT, :, :].rearrange("p a n -> p (a n)")
        rows_s = rot_s[0:CT, :, :].rearrange("p a n -> p (a n)")
        kq_flat = kq_t[:, :, :, :].rearrange("p s k t -> p (s k t)")
        x2c_sb = rows_c[:, 0:2 * D].rearrange("p (s d) -> p s d", s=2)
        h2c_sb = rows_c[:, 2 * D:4 * D].rearrange("p (s d) -> p s d", s=2)
        gw_sb = rows_c[:, 4 * D:8 * D].rearrange("p (s r d) -> p s r d", s=2, r=2)
        ob_sb = kq_flat[0:CT, 6 * D:10 * D].rearrange("p (s r d) -> p s r d", s=2, r=2)
        c_res = kq_flat[0:CT, 10 * D:12 * D].rearrange("p (s d) -> p s d", s=2)
        bal_sb = kq_flat[0:CT, 12 * D:12 * D + 4].rearrange("p (s r) -> p s r", s=2)
        ib_sb = kq_flat[:, 12 * D + 4:12 * D + 4 + NATOM * NF].rearrange("p (a m) -> p a m", a=NATOM)
        x2c_t = rot_s[:, 0, 0:2 * NCLS * B].rearrange("p (c n) -> p c n", c=2)
        g_junk = rows_s[:, 2 * D:3 * D]
        g_sq, g_dot = rows_s[:, 3 * D:3 * D + 6], rows_s[:, 3 * D + 6:3 * D + 10]
        g_nrm = rows_s[:, 3 * D + 10:3 * D + 16]
        g_log = rows_s[:, 3 * D + 16:3 * D + 20].rearrange("p (s r) -> p s r", s=2)
        g_x = rows_s[:, 3 * D + 20:3 * D + 34]
        g_half = rows_s[:, 3 * D + 34:3 * D + 40]
        c_a, c_b, c_c = (rows_s[:, (4 + k) * D:(5 + k) * D] for k in range(3))
        c_hid = hid[:, 0:5, :].rearrange("p c t -> p (c t)")[:, 0:2 * NF * NCLS * B].rearrange(
            "p (r m s q b) -> p r m s q b", r=2, m=NF, s=2, q=NQ)
        w_in = sin_t[:, :, :, :, :].rearrange("p t a h d -> p (t a h d)")
        w_in2 = flat
        w_outs = v[:, :, :].rearrange("p t n -> p (t n)")
        s_cl = sem("cls_loaded")
        s_cw = sem("cls_weights_loaded")
        s_cd = sem("cls_steps_dve")
        s_cpe = sem("cls_pe_transposes")
        s_ch = sem("cls_hidden_product")
        s_chf = sem("cls_hidden_ready")
        s_co = sem("cls_out_product")
        s_ct = sem("cls_tanh")
        s_cg = sem("cls_pool")
        s_cs = sem("cls_stored")

        def w_in_at(atom, c):
            n = 2 * atom + c
            if n < 8:
                return w_in[:, n * F:(n + 1) * F]
            return w_in2[:, (n - 8) * F:(n - 7) * F]

        def w_out_at(atom):
            size = NF * D
            src = [w_in2[:, 2 * F:2 * F + size], w_in2[:, 2 * F + size:2 * F + 2 * size],
                   w_in2[:, 2 * F + 2 * size:2 * F + 3 * size], w_outs[:, 0:size],
                   kq_flat[:, 0:size]][atom]
            return src.rearrange("p (c d) -> p c d", c=NF)

        block = ctx.enter_context(nc.Block())

        @block.sync
        def _(sp):
            def load(dst, src, s):
                sp.dma_start(dst, src).then_inc(s, 16)

            load(ids[:, :], a["ids"][0, :, :], s_ids)
            load(center[:, 0:D], a["center"][0:P, :], s_stage)
            load(center[0:D - P, D:2 * D], a["center"][P:D, :], s_stage)
            for k in range(2):
                load(up_dup[:, k * R:(k + 1) * R], a["up"][0:P, :], s_stage)
                load(up_dup[0:D - P, 2 * R + k * R:2 * R + (k + 1) * R], a["up"][P:D, :], s_stage)
                load(up_stage[k * R:(k + 1) * R, :], a["up_t"], s_stage)
            at = 0
            for name, n in (("wk", QK), ("wq", QK), ("wv", VC), ("wg", VC)):
                load(wa[:, at:at + n], a[name][0:P, :], s_stage)
                load(wb[:, at:at + n], a[name][P:D, :], s_stage)
                at += n
            load(fc1_stage[:, 0:F], a["fc1_t"][0:P, :], s_stage)
            load(fc1_stage[0:D - P, F:2 * F], a["fc1_t"][P:D, :], s_stage)
            load(fc1_stage[D - P:P, F:2 * F], a["fc1_t"][0:2 * P - D, :], s_stage)
            load(fc1_stage[:, 2 * F:3 * F], a["fc1_t"][D - P:D, :], s_stage)
            load(ident[:, :], a["ident"], s_const)
            load(head_mean[:, :], a["head_mean"], s_const)
            load(causal[:, :], a["causal"], s_const)
            load(cos_t[:, :, :, :, :], a["cos_t"], s_const)
            load(sin_t[:, :, :, :, :], a["sin_t"], s_const)
            load(fc2[:, :, :], a["fc2_t"].rearrange("(c p) d -> p c d", p=P), s_const)
            load(wo[:, :, :], a["wo"].rearrange("(c p) d -> p c d", p=P), s_const)
            load(gn_w[:, :], a["gn_w"], s_const)
            load(gn_b[:, :], a["gn_b"], s_const)
            load(fc1_b[:, :], a["fc1_b"], s_const)
            load(fc2_b[:, :], a["fc2_b"].partition_broadcast(P), s_const)

            def stores(b):
                sp.wait_ge(s_h2c, b + 1)
                sp.dma_start(a["h2c"][:, b, :], h2_cls[:, :]).then_inc(s_hc, 16)
                sp.wait_ge(s_x2, NT * b + 1)
                sp.dma_start(a["x2c"][:, b, :], x2[0:NCLS, 0, :]).then_inc(s_xc, 16)
                sp.wait_ge(s_res, 2 * b + 1)
                sp.dma_start(a["out"][b, NCLS:P, :], res[NCLS:P, 0, :]).then_inc(s_stA, 16)
                sp.dma_start(a["out"][b, P:2 * P, :], res[:, 1, :]).then_inc(s_stA, 16)
                sp.wait_ge(s_res, 2 * b + 2)
                sp.dma_start(a["out"][b, 2 * P:T, :].rearrange("(t p) d -> p t d", p=P),
                             res[:, 2:NT, :]).then_inc(s_stB, 16)

            def body(i, has_back, has_next):
                if has_next:
                    sp.wait_ge(s_emb, 64 * (i + 1))
                    sp.dma_start(ids[:, :], a["ids"][i + 1, :, :]).then_inc(s_ids, 16)
                if has_back:
                    stores(i - 1)

            def cls_weights():
                sp.wait_ge(s_o, NP * B)
                for atom in range(NATOM):
                    sp.dma_start(w_in_at(atom, 0), a["ain_t"][atom, 0:P, :]).then_inc(s_cw, 16)
                    sp.dma_start(w_in_at(atom, 1)[0:D - P, :], a["ain_t"][atom, P:D, :]).then_inc(s_cw, 16)
                for atom in range(NATOM):
                    sp.dma_start(w_out_at(atom), a["aout_t"][atom, :, :].rearrange("(c p) d -> p c d", p=P)).then_inc(s_cw, 16)
                for n in range(NCLS):
                    s, q = n % 2, n // 2
                    rows = slice(q * B, (q + 1) * B)
                    for r in range(2):
                        gate_row = a["gate_pair"][n, r, :]
                        dst = SRC[n][1 - r]
                        sp.dma_start(gw_sb[rows, s, r, :], gate_row.partition_broadcast(B)).then_inc(s_cl, 16)
                        sp.dma_start(ob_sb[rows, s, r, :], a["aout_b"][dst, :].partition_broadcast(B)).then_inc(s_cl, 16)
                    sp.dma_start(bal_sb[rows, s, :], a["balance"][n, :].partition_broadcast(B)).then_inc(s_cl, 16)
                sp.dma_start(ib_sb, a["ain_b"]).then_inc(s_cl, 16)

            def cls_rows():
                sp.wait_ge(s_hc, 16 * B)
                sp.wait_ge(s_xc, 16 * B)
                for n in range(NCLS):
                    s, q = n % 2, n // 2
                    rows = slice(q * B, (q + 1) * B)
                    sp.dma_start(x2c_sb[rows, s, :], a["x2c"][n, :, :]).then_inc(s_cl, 16)
                    sp.dma_start(h2c_sb[rows, s, :], a["h2c"][n, :, :]).then_inc(s_cl, 16)
                sp.wait_ge(s_cd, CLS_STEPS)
                for n in range(NCLS):
                    s, q = n % 2, n // 2
                    sp.dma_start(a["out"][:, n, :], c_res[q * B:(q + 1) * B, s, :]).then_inc(s_cs, 16)
                sp.wait_ge(s_cs, 16 * NCLS)

            body(0, False, True)
            with sp.Fori(1, B - 1) as i:
                body(i, True, True)
            body(B - 1, True, False)
            cls_weights()
            stores(B - 1)
            sp.wait_ge(s_stA, 32 * B)
            sp.wait_ge(s_stB, 16 * B)
            cls_rows()

        @block.gpsimd
        def _(pool):
            nc.gpsimd.memset(neg_half[:, :], -0.5).then_inc(s_set_pool, 1)

            def gather(b):
                wait_apart(pool, s_ids, 16 * (b + 1))
                for t in range(NT):
                    nc.gpsimd.indirect_dma_start(
                        emb[:, t * R:(t + 1) * R], None, a["table"],
                        bass.IndirectOffsetOnAxis(ids[:, t:t + 1].bitcast(u32), 0)).then_inc(s_emb, 16)

            def rsqrt_ln1(b):
                pool.wait_ge(s_ln1, 10 * b + 9)
                nc.gpsimd.tensor_tensor(ln1_rstd[:, :], ln1_ve[:, :], neg_half[:, :], ALU.pow).then_inc(s_ln1p, 1)

            def rsqrt_ln2(b):
                pool.wait_ge(s_ln2, 10 * b + 9)
                nc.gpsimd.tensor_tensor(ln2_rstd[:, :], ln2_ve[:, :], neg_half[:, :], ALU.pow).then_inc(s_ln2p, 1)

            def rsqrt_gn(i, p):
                pool.wait_ge(s_gn, 24 * i + 8 * p + 5)
                nc.gpsimd.tensor_tensor(gn_rstd[:, p:p + 1], gn_ve[:, p:p + 1], neg_half[:, 0:1], ALU.pow)\
                    .then_inc(s_gnp, 1)

            def rotate(i, t):
                for k in range(2):
                    pool.wait_ge(s_rotm, 16 * i + 4 * t + 2 * k + 2)
                    if t == 0 and k == 0 and later(i):
                        pool.wait_ge(s_kv, NP * i)
                    nc.gpsimd.tensor_tensor(kq[:, t, k, :, :].rearrange("p h d -> p (h d)"), rot_c[:, k, :],
                                            rot_s[:, k, :], ALU.add).then_inc(s_rot, 1)

            def body(i, has_back, has_next):
                if has_back:
                    rsqrt_ln2(i - 1)
                for t in range(NT):
                    rotate(i, t)
                if has_next:
                    pool.wait_ge(s_ln1, 10 * (i + 1))
                    gather(i + 1)
                rsqrt_gn(i, 0)
                if has_next:
                    rsqrt_ln1(i + 1)
                rsqrt_gn(i, 1)
                rsqrt_gn(i, 2)

            gather(0)
            pool.wait_ge(s_set_pool, 1)
            rsqrt_ln1(0)
            body(0, False, True)
            with nc.gpsimd.Fori(1, B - 1) as i:
                body(i, True, True)
            body(B - 1, True, False)
            rsqrt_ln2(B - 1)
            pool.wait_ge(s_cd, CD_SQ)
            nc.gpsimd.tensor_tensor(g_nrm, g_sq, g_half, ALU.pow).then_inc(s_cg, 1)

        @block.scalar
        def _(act):
            def emb_evac(b):
                if later(b):
                    act.wait_ge(s_keep, b)
                for k in range(2):
                    act.wait_ge(s_embT, 2 * b + k + 1)
                    nc.scalar.activation(emb_t[:, k * 256:(k + 1) * 256], bank_of("emb_t_ready", k)[:, 0:256],
                                         ACT.Copy).then_inc(s_embt, 1)

            def keep_embeddings(i):
                if later(i):
                    act.wait_ge(s_hres, 2 * i)
                act.wait_ge(s_embt, 2 * i + 2)
                nc.scalar.activation(emb_keep[:, :], emb_t[:, :].bitcast(fp32), ACT.Copy).then_inc(s_keep, 1)

            def norm_evac(b):
                if later(b):
                    act.wait_ge(s_gproj, NP * b)
                act.wait_ge(s_normT, b + 1)
                nc.scalar.activation(norm_t[:, :], bank_of("norm_t_ready", 0)[:, :], ACT.Copy).then_inc(s_normt, 1)

            def v_evac(i, t):
                act.wait_ge(s_vproj, NT * i + t + 1)
                if t == 0 and later(i):
                    act.wait_ge(s_o, NP * i)
                nc.scalar.activation(v[:, t, :], bank_of("v_ready", t)[:, 0:VC], ACT.Copy).then_inc(s_v, 1)

            def tanhs(i):
                if later(i):
                    act.wait_ge(s_gated, NP * i)
                for m in range(NP):
                    act.wait_ge(s_gproj, NP * i + m + 1)
                    nc.scalar.activation(gate[:, m, :], bank_of("gate_ready", m)[:, :], ACT.Tanh, scale=0.5)\
                        .then_inc(s_tanh, 1)

            def pair_evac(i, p):
                if p == 2:
                    act.wait_ge(s_o, NP * i + 1)
                elif later(i):
                    act.wait_ge(s_o, NP * i - (0 if p == 0 else 1))
                for j in range(4):
                    act.wait_ge(s_T, 12 * i + 4 * p + j + 1)
                    nc.scalar.activation(kq_t[:, p % 2, j, :], bank_of("kq_t_ready", 4 * p + j)[:, :], ACT.Copy)\
                        .then_inc(s_t, 1)

            def att_evac(i, p):
                if p == 0 and later(i):
                    act.wait_ge(s_wo, 2 * i)
                act.wait_ge(s_o, NP * i + p + 1)
                nc.scalar.activation(att[:, p, :], bank_of("att_ready", p)[:, :], ACT.Copy).then_inc(s_att, 1)

            def gn_apply(i, m):
                act.wait_ge(s_gn, 24 * i + 8 * m + 8)
                nc.scalar.activation(att[:, m, :], att[:, m, :], ACT.Identity, bias=gn_c[:, m:m + 1],
                                     scale=gn_a[:, m:m + 1]).then_inc(s_aff, 1)

            def h2_class_rows(b):
                if later(b):
                    act.wait_ge(s_hc, 16 * b)
                act.wait_ge(s_ln2, 10 * b + 2)
                nc.scalar.activation(h2_cls[:, :], hb[0][0:NCLS, 0:D], ACT.Copy).then_inc(s_h2c, 1)

            def x2_norm(b):
                if later(b):
                    act.wait_ge(s_xc, 16 * b)
                    act.wait_ge(s_x2s, 2 * b)
                act.wait_ge(s_ln2, 10 * b + 10)
                for t in range(NT):
                    nc.scalar.activation(x2[:, t, :], hb[t // 2][:, (t % 2) * D:(t % 2 + 1) * D], ACT.Identity,
                                         bias=ln2_nmr[:, t:t + 1], scale=ln2_rstd[:, t:t + 1]).then_inc(s_x2, 1)

            def x2_evac(b):
                if later(b):
                    act.wait_ge(s_fc1, NF * b)
                for c in range(3):
                    act.wait_ge(s_x2T, 3 * b + c + 1)
                    nc.scalar.activation(x2_t[:, c, :], back[(1 + c) % 2][:, :], ACT.Copy).then_inc(s_x2t, 1)

            def gelu(b, m):
                if m == 0 and later(b):
                    act.wait_ge(s_fc2, 2 * b)
                act.wait_ge(s_fc1, NF * b + m + 1)
                nc.scalar.activation(hid[:, m, :], back[(4 + m) % 2][:, :], ACT.Gelu, bias=fc1_b[:, m:m + 1])\
                    .then_inc(s_hid, 1)

            def body(i, has_back, has_next):
                keep_embeddings(i)
                v_evac(i, 0)
                if has_back:
                    h2_class_rows(i - 1)
                    x2_norm(i - 1)
                v_evac(i, 1)
                if has_back:
                    x2_evac(i - 1)
                v_evac(i, 2)
                if has_back:
                    gelu(i - 1, 0)
                    gelu(i - 1, 1)
                v_evac(i, 3)
                if has_back:
                    for m in range(2, NF):
                        gelu(i - 1, m)
                tanhs(i)
                pair_evac(i, 0)
                pair_evac(i, 1)
                att_evac(i, 0)
                pair_evac(i, 2)
                att_evac(i, 1)
                if has_next:
                    emb_evac(i + 1)
                gn_apply(i, 0)
                att_evac(i, 2)
                gn_apply(i, 1)
                if has_next:
                    norm_evac(i + 1)
                gn_apply(i, 2)

            nc.scalar.preload_act_table(ACT.Gelu)
            act.wait_ge(s_const, N_CONST)
            emb_evac(0)
            norm_evac(0)
            body(0, False, True)
            with nc.scalar.Fori(1, B - 1) as i:
                body(i, True, True)
            body(B - 1, True, False)
            h2_class_rows(B - 1)
            x2_norm(B - 1)
            x2_evac(B - 1)
            for m in range(NF):
                gelu(B - 1, m)

            act.wait_ge(s_cl, N_CL)
            act.wait_ge(s_fc2, 2 * B)
            for atom in range(NATOM):
                for m in range(NF):
                    k = NF * atom + m
                    act.wait_ge(s_ch, k + 1)
                    if atom < NQ:
                        o, n = c_hid[:, 0, m, :, atom, :], 2 * B
                        src = bank[k % RING][:, 0:n].rearrange("p (s b) -> p s b", s=2)
                    else:
                        o, n = c_hid[:, 1, m, atom - NQ, :, :].rearrange("p q b -> p (q b)"), NQ * B
                        src = bank[k % RING][:, 0:n]
                    nc.scalar.activation(o, src, ACT.Gelu, bias=ib_sb[:, atom, m:m + 1]).then_inc(s_chf, 1)
            act.wait_ge(s_cd, CD_DIFF)
            nc.scalar.activation(g_x[:, 4:6], g_x[:, 2:4], ACT.Tanh, scale=0.5).then_inc(s_ct, 1)

        @block.tensor
        def _(pe):
            mm = nc.tensor.matmul

            def turn_embeddings(b):
                pe.wait_ge(s_embsplit, 2 * (b + 1))
                for k in range(2):
                    o = take(pe, b - 1, "emb_t_ready", k)
                    for t in (2 * k, 2 * k + 1):
                        last = nc.tensor.transpose(o[:, (t % 2) * P:(t % 2 + 1) * P], emb_split[:, t, :].bitcast(fp32),
                                                   ident[:, :])
                    last.then_inc(s_embT, 1)

            def embed(o, source, t, starts):
                tok = source[:, t * P:(t + 1) * P]
                mm(o, tok, up_hi[:, :], start=starts, stop=False, skip_group_check=True)
                return mm(o, tok, up_lo[:, :], start=False, stop=True, skip_group_check=True)

            def h_for_statistics(b):
                for k in range(2):
                    pe.wait_ge(s_embt, 2 * b + k + 1)
                    o = take(pe, b - 1, "ln1_steps", 2 * k + 1)
                    for t in (2 * k, 2 * k + 1):
                        last = embed(o[:, (t % 2) * D:(t % 2 + 1) * D], emb_t, t, True)
                    last.then_inc(s_hstat, 1)

            def turn_norm(b):
                pe.wait_ge(s_normsplit, 2 * (b + 1))
                o = take(pe, b - 1, "norm_t_ready", 0)
                for t in range(NT):
                    last = nc.tensor.transpose(o[:, t * P:(t + 1) * P], norm_split[:, t, :].bitcast(fp32), ident[:, :])
                last.then_inc(s_normT, 1)

            def project(i, t):
                if t == 0:
                    pe.wait_ge(s_normt, i + 1)
                tok = norm_t[:, t * P:(t + 1) * P]
                for k in range(5):
                    name, index = ("rotary_products", 4 * t + k) if k < 4 else ("v_ready", t)
                    o = take(pe, i, name, index)[:, 0:BC]
                    mm(o, tok, w_hi[:, k * BC:(k + 1) * BC], start=True, stop=False)
                    mm(o, tok, w_lo[:, k * BC:(k + 1) * BC], start=False, stop=True).then_inc(s_proj if k < 4 else s_vproj, 1)

            def project_gate(i):
                for m in range(NP):
                    o = take(pe, i, "gate_ready", m)[:, :]
                    at = slice(G_AT + m * P, G_AT + (m + 1) * P)
                    mm(o, w_hi[:, at], norm_t[:, :], start=True, stop=False)
                    mm(o, w_lo[:, at], norm_t[:, :], start=False, stop=True).then_inc(s_gproj, 1)

            def residual(i, k):
                if k == 0:
                    pe.wait_ge(s_keep, i + 1)
                if later(i):
                    pe.wait_ge(s_res, 2 * (i - 1) + k + 1)
                for t in (2 * k, 2 * k + 1):
                    last = embed(hb[k][:, (t % 2) * D:(t % 2 + 1) * D], emb_keep, t, t % 2 == 0)
                last.then_inc(s_hres, 1)

            def turn_pair(i, p):
                if p == 0:
                    pe.wait_ge(s_rot, 2 * NT * (i + 1))
                for j in range(4):
                    o = take(pe, i, "kq_t_ready", 4 * p + j)
                    for t in range(NT):
                        last = nc.tensor.transpose(o[:, t * P:(t + 1) * P], kq[:, t, j % 2, 2 * p + j // 2, :], ident[:, :])
                    last.then_inc(s_T, 1)

            def key_values(i, p):
                if p == 0:
                    pe.wait_ge(s_v, NT * (i + 1))
                o = take(pe, i, "state_steps", 3 * p + 2)
                for c in range(NT - 1):
                    for j in range(2):
                        h = 2 * p + j
                        last = mm(o[:, c * P + j * DV:c * P + (j + 1) * DV], kq[:, c, 0, h, :],
                                  v[:, c, h * DV:(h + 1) * DV], start=True, stop=True)
                last.then_inc(s_kv, 1)

            def scores(i, p):
                for j in range(2):
                    pe.wait_ge(s_t, 12 * i + 4 * p + 2 * j + 2)
                    o = take(pe, i, "probs_ready", 2 * p + j)
                    for c in range(NT):
                        at = slice(c * P, (c + 1) * P)
                        last = mm(o[:, at], kq_t[:, p % 2, 2 * j, at], kq_t[:, p % 2, 2 * j + 1, at], start=True, stop=True)
                    last.then_inc(s_score, 1)

            def outputs(i, p):
                pe.wait_ge(s_prob, 6 * i + 2 * p + 2)
                pe.wait_ge(s_state, 9 * i + 3 * p + 3)
                o = take(pe, i, "att_ready", p)
                for c in range(NT):
                    at = slice(c * P, (c + 1) * P)
                    for j in range(2):
                        h = 2 * p + j
                        last = mm(o[j * DV:(j + 1) * DV, at], v[:, c, h * DV:(h + 1) * DV], probs[:, p % 2, j, at],
                                  start=True, stop=c == 0)
                    if c:
                        for j in range(2):
                            last = mm(o[j * DV:(j + 1) * DV, at], state[:, p % 2, c - 1, j * DV:(j + 1) * DV],
                                      kq_t[:, p % 2, 2 * j + 1, at], start=False, stop=True)
                last.then_inc(s_o, 1)

            def take_back(b, r):
                if r >= 6:
                    pe.wait_ge(s_hid, NF * b + r - 5)
                elif r >= 3:
                    pe.wait_ge(s_x2t, 3 * b + r - 2)
                elif r == 2:
                    pe.wait_ge(s_gn, 24 * b + 21)
                elif later(b):
                    pe.wait_ge(s_hid, NF * b - (1 - r))
                return back[r % 2]

            def gn_means(i, p):
                pe.wait_ge(s_gns2, NP * i + p + 1)
                if p == 0:
                    take_back(i, 0)
                else:
                    pe.wait_ge(s_gn, 24 * i + 8 * p - 3)
                mm(back[0][:, 8 * p:8 * p + 1], head_mean[:, :], gn_mv[:, p, 0:1], start=True, stop=True).then_inc(s_gnpe, 1)

            def gn_variances(i, p):
                pe.wait_ge(s_gn, 24 * i + 8 * p + 4)
                mm(back[0][:, 8 * p + 4:8 * p + 5], head_mean[:, :], gn_m2[:, p:p + 1], start=True, stop=True)\
                    .then_inc(s_gnpe, 1)

            def out_project(b, k, pairs):
                for t in (2 * k, 2 * k + 1):
                    for m in pairs:
                        if t == 0:
                            pe.wait_ge(s_gated, NP * b + m + 1)
                        last = mm(hb[k][:, (t % 2) * D:(t % 2 + 1) * D], att[:, m, t * P:(t + 1) * P], wo[:, m, :],
                                  start=False, stop=m == NP - 1, skip_group_check=True)
                if NP - 1 in pairs:
                    last.then_inc(s_wo, 1)

            def turn_x2(b):
                pe.wait_ge(s_x2s, 2 * (b + 1))
                for c in range(3):
                    o = take_back(b, 1 + c)
                    for t in range(NT):
                        last = nc.tensor.transpose(o[:, t * P:(t + 1) * P], x2_split[:, t, c * P:(c + 1) * P].bitcast(fp32),
                                                   ident[:, :])
                    last.then_inc(s_x2T, 1)

            def hidden(b, m):
                if m == 0:
                    pe.wait_ge(s_x2t, 3 * (b + 1))
                o = take_back(b, 4 + m)
                at = slice(m * P, (m + 1) * P)
                for c in range(3):
                    mm(o[:, :], fc1_hi[:, c, at], x2_t[:, c, :], start=c == 0, stop=False)
                for c in range(2):
                    last = mm(o[:, :], fc1_lo[:, c, at], x2_t[:, c, :], start=False, stop=c == 1)
                last.then_inc(s_fc1, 1)

            def second_layer(b, t):
                if t == 0:
                    pe.wait_ge(s_h2c, b + 1)
                    pe.wait_ge(s_x2, NT * (b + 1))
                for m in range(NF):
                    if t == 0:
                        pe.wait_ge(s_hid, NF * b + m + 1)
                    last = mm(hb[t // 2][:, (t % 2) * D:(t % 2 + 1) * D], hid[:, m, t * P:(t + 1) * P], fc2[:, m, :],
                              start=False, stop=m == NF - 1, skip_group_check=True)
                if t % 2:
                    last.then_inc(s_fc2, 1)

            def body(i, has_back, has_next):
                b = i - 1
                project(i, 0)
                project(i, 1)
                if has_back:
                    turn_x2(b)
                project(i, 2)
                if has_back:
                    hidden(b, 0)
                    hidden(b, 1)
                project(i, 3)
                if has_back:
                    for m in range(2, NF):
                        hidden(b, m)
                project_gate(i)
                turn_pair(i, 0)
                key_values(i, 0)
                if has_back:
                    second_layer(b, 0)
                scores(i, 0)
                turn_pair(i, 1)
                key_values(i, 1)
                outputs(i, 0)
                if has_back:
                    second_layer(b, 1)
                scores(i, 1)
                turn_pair(i, 2)
                key_values(i, 2)
                gn_means(i, 0)
                outputs(i, 1)
                if has_next:
                    turn_embeddings(i + 1)
                gn_variances(i, 0)
                scores(i, 2)
                residual(i, 0)
                if has_next:
                    h_for_statistics(i + 1)
                gn_means(i, 1)
                outputs(i, 2)
                gn_variances(i, 1)
                if has_back:
                    second_layer(b, 2)
                if has_next:
                    turn_norm(i + 1)
                gn_means(i, 2)
                if has_back:
                    second_layer(b, 3)
                gn_variances(i, 2)
                out_project(i, 0, (0, 1))
                residual(i, 1)
                out_project(i, 1, (0, 1))
                out_project(i, 0, (2,))
                out_project(i, 1, (2,))

            pe.wait_ge(s_stage, N_STAGE)
            for o, cols in ((bank[0][:, 0:2 * R], slice(0, P)), (bank[1][0:D - P, 0:2 * R], slice(P, D))):
                mm(o, center[:, cols], up_dup[:, 0:2 * R], start=True, stop=False)
                last = mm(o, center[0:D - P, D + cols.start:D + cols.stop], up_dup[0:D - P, 2 * R:4 * R], start=False, stop=True)
            last.then_inc(s_set_pe, 1)
            pe.wait_ge(s_set_dve, 2)
            for n in range(WC // BC):
                if n >= RING:
                    pe.wait_ge(s_set_dve, 2 + 2 * (n - RING + 1))
                o, at = bank[n % RING][:, 0:BC], slice(n * BC, (n + 1) * BC)
                mm(o, up_cen[:, 0:2 * R], wa[:, at], start=True, stop=False)
                mm(o, up_cen[0:D - P, 2 * R:4 * R], wb[:, at], start=False, stop=True).then_inc(s_set_pe, 1)
            pe.wait_ge(s_set_dve, N_SET)
            pe.wait_ge(s_const, N_CONST)
            turn_embeddings(0)
            h_for_statistics(0)
            turn_norm(0)

            body(0, False, True)
            with nc.tensor.Fori(1, B - 1) as i:
                body(i, True, True)
            body(B - 1, True, False)
            turn_x2(B - 1)
            for m in range(NF):
                hidden(B - 1, m)
            for t in range(NT):
                second_layer(B - 1, t)

            pe.wait_ge(s_cl, N_CL)
            for s in range(2):
                for c, n in ((0, P), (1, D - P)):
                    last = nc.tensor.transpose(bank[2 * s + c][0:n, 0:CT], x2c_sb[:, s, c * P:c * P + n], ident[0:CT, 0:CT])
            last.then_inc(s_cpe, 1)
            pe.wait_ge(s_cw, N_CW)
            pe.wait_ge(s_cd, CD_T)
            for atom in range(NATOM):
                for m in range(NF):
                    k = NF * atom + m
                    if k >= RING:
                        pe.wait_ge(s_chf, k - RING + 1)
                    n = 2 * B if atom < NQ else NQ * B
                    o = bank[k % RING][:, 0:n]
                    for c, rows in ((0, P), (1, D - P)):
                        x = x2c_t[0:rows, c, :].rearrange("p (s q b) -> p s q b", s=2, q=NQ)
                        x = x[:, :, atom, :] if atom < NQ else x[:, atom - NQ, :, :]
                        last = mm(o, w_in_at(atom, c)[0:rows, m * P:(m + 1) * P], x, start=c == 0, stop=c == 1)
                    last.then_inc(s_ch, 1)
            pe.wait_ge(s_chf, NATOM * NF)
            for s in range(2):
                for m in range(NF):
                    last = mm(bank[s][0:CT, 0:D], c_hid[:, 0, m, s, :, :].rearrange("p q b -> p (q b)"),
                              w_out_at(NQ + s)[:, m, :], start=m == 0, stop=m == NF - 1)
            for s in range(2):
                for m in range(NF):
                    for q in range(NQ):
                        last = mm(bank[2 + s][q * B:(q + 1) * B, 0:D], c_hid[:, 1, m, s, q, :],
                                  w_out_at(q)[:, m, :], start=m == 0, stop=m == NF - 1)
            last.then_inc(s_co, 1)

        @block.vector
        def _(dve):
            V = nc.vector

            def split(dst_hi, dst_lo, src, s, at):
                V.tensor_copy(dst_hi, src).then_inc(s, 1)
                dve.wait_ge(s, at + 1)
                V.tensor_tensor(dst_lo, src, dst_hi.bitcast(fp32), ALU.subtract).then_inc(s, 1)

            def split_embeddings(b):
                dve.wait_ge(s_emb, 64 * (b + 1))
                if later(b):
                    dve.wait_ge(s_embT, 2 * b)
                split(emb_split[:, :, 0:R], emb_split[:, :, R:2 * R], emb[:, :].rearrange("p (t r) -> p t r", t=NT),
                      s_embsplit, 2 * b)

            def layer_statistics(b, stats, mv, ve, s, source, ready):
                for t in range(NT):
                    if t % 2 == 0:
                        dve.wait_ge(ready, 2 * b + t // 2 + 1)
                    V.bn_stats(stats[:, t, :], source[t // 2][:, (t % 2) * D:(t % 2 + 1) * D]).then_inc(s, 1)
                wait_apart(dve, s, 10 * b + NT)
                for t in range(NT):
                    V.bn_aggr(mv[:, t, :], stats[:, t, :]).then_inc(s, 1)
                dve.wait_ge(s, 10 * b + 2 * NT)
                V.tensor_scalar(ve[:, :], mv[:, :, 1], LN_EPS, None, ALU.add).then_inc(s, 1)

            def statistics_ln1(b):
                banks = [bank_of("ln1_steps", 1), bank_of("ln1_steps", 3)]
                layer_statistics(b, ln1_st, ln1_mv, ln1_ve, s_ln1, banks, s_hstat)

            def normalise_embeddings(b):
                dve.wait_ge(s_ln1p, b + 1)
                V.tensor_tensor(emb_norm[:, :, :], emb[:, :].rearrange("p (t r) -> p t r", t=NT),
                                ln1_rstd[:, :].unsqueeze(2).broadcast_to([P, NT, R]), ALU.mult).then_inc(s_ln1, 1)
                if later(b):
                    dve.wait_ge(s_normT, b)
                dve.wait_ge(s_ln1, 10 * (b + 1))
                split(norm_split[:, :, 0:R], norm_split[:, :, R:2 * R], emb_norm[:, :, :], s_normsplit, 2 * b)

            def rotary(i, t, a):
                if t or later(i):
                    dve.wait_ge(s_rot, 2 * NT * i + 2 * t + a - 1)
                for j in range(2):
                    k = 2 * a + j
                    dve.wait_ge(s_proj, 16 * i + 4 * t + k + 1)
                    src = bank_of("rotary_products", 4 * t + k)[:, 0:BC].rearrange("p (h s d) -> p h s d", h=3, s=2)
                    at, heads = slice(j * BC, (j + 1) * BC), slice(3 * j, 3 * j + 3)
                    V.tensor_tensor(rot_c[:, a, at].rearrange("p (h s d) -> p h s d", h=3, s=2), src,
                                    cos_t[:, t, a, heads, :].unsqueeze(2).broadcast_to([P, 3, 2, HALF]), ALU.mult)
                    V.tensor_tensor(rot_s[:, a, at].rearrange("p (h s d) -> p h s d", h=3, s=2), src[:, :, ::-1, :],
                                    sin_t[:, t, a, heads, :].rearrange("p h (s d) -> p h s d", s=2), ALU.mult)\
                        .then_inc(s_rotm, 1)

            def gates(i):
                for m in range(NP):
                    dve.wait_ge(s_tanh, NP * i + m + 1)
                    V.scalar_tensor_tensor(gate[:, m, :], gate[:, m, :], 1.0, bank_of("gate_ready", m)[:, :], ALU.add, ALU.mult)\
                        .then_inc(s_gate, 1)

            def states(i, p):
                dve.wait_ge(s_kv, NP * i + p + 1)
                if p == 2:
                    dve.wait_ge(s_o, NP * i + 1)
                elif later(i):
                    dve.wait_ge(s_o, NP * i - (0 if p == 0 else 1))
                src = bank_of("state_steps", 3 * p + 2)
                V.tensor_copy(state[:, p % 2, 0, :], src[:, 0:P]).then_inc(s_state, 1)
                for c in range(1, NT - 1):
                    dve.wait_ge(s_state, 9 * i + 3 * p + c)
                    V.tensor_tensor(state[:, p % 2, c, :], src[:, c * P:(c + 1) * P], state[:, p % 2, c - 1, :], ALU.add)\
                        .then_inc(s_state, 1)

            def mask(i, p):
                if p == 2:
                    dve.wait_ge(s_o, NP * i + 1)
                elif later(i):
                    dve.wait_ge(s_o, NP * i - (0 if p == 0 else 1))
                for j in range(2):
                    dve.wait_ge(s_score, 6 * i + 2 * p + j + 1)
                    V.tensor_tensor(probs[:, p % 2, j, :].rearrange("p (c t) -> p c t", c=NT),
                                    bank_of("probs_ready", 2 * p + j)[:, :].rearrange("p (c t) -> p c t", c=NT),
                                    causal[:, :].unsqueeze(1).broadcast_to([P, NT, P]), ALU.mult).then_inc(s_prob, 1)

            def channel_statistics(i, p):
                dve.wait_ge(s_att, NP * i + p + 1)
                V.bn_stats(gn_st[:, p, :], att[:, p, :]).then_inc(s_gns, 1)
                wait_apart(dve, s_gns, NP * i + p + 1)
                V.bn_aggr(gn_mv[:, p, :], gn_st[:, p, :]).then_inc(s_gns2, 1)

            def head_means(i, p):
                one, at = slice(p, p + 1), 24 * i + 8 * p
                dve.wait_ge(s_gnpe, 6 * i + 2 * p + 1)
                V.tensor_copy(gn_dd[:, one], back[0][:, 8 * p:8 * p + 1]).then_inc(s_gn, 1)
                dve.wait_ge(s_gn, at + 1)
                V.tensor_tensor(gn_d[:, one], gn_mv[:, p, 0:1], gn_dd[:, one], ALU.subtract).then_inc(s_gn, 1)
                dve.wait_ge(s_gn, at + 2)
                V.tensor_tensor(gn_ma[:, one], gn_d[:, one], gn_d[:, one], ALU.mult).then_inc(s_gn, 1)
                dve.wait_ge(s_gn, at + 3)
                V.tensor_tensor(gn_m2[:, one], gn_ma[:, one], gn_mv[:, p, 1:2], ALU.add).then_inc(s_gn, 1)

            def head_factors(i, p):
                one, at = slice(p, p + 1), 24 * i + 8 * p
                dve.wait_ge(s_gnpe, 6 * i + 2 * p + 2)
                V.tensor_scalar(gn_ve[:, one], back[0][:, 8 * p + 4:8 * p + 5], LN_EPS, None, ALU.add).then_inc(s_gn, 1)
                dve.wait_ge(s_gnp, NP * i + p + 1)
                V.scalar_tensor_tensor(gn_a[:, one], gn_w[:, one], 0.5, gn_rstd[:, one], ALU.mult, ALU.mult).then_inc(s_gn, 1)
                dve.wait_ge(s_gn, at + 6)
                V.tensor_tensor(gn_ma[:, one], gn_dd[:, one], gn_a[:, one], ALU.mult).then_inc(s_gn, 1)
                dve.wait_ge(s_gn, at + 7)
                V.scalar_tensor_tensor(gn_c[:, one], gn_b[:, one], 0.5, gn_ma[:, one], ALU.mult, ALU.subtract)\
                    .then_inc(s_gn, 1)

            def gating(i, m):
                dve.wait_ge(s_aff, NP * i + m + 1)
                V.tensor_tensor(att[:, m, :], att[:, m, :], gate[:, m, :], ALU.mult).then_inc(s_gated, 1)

            def statistics_ln2(b):
                layer_statistics(b, ln2_st, ln2_mv, ln2_ve, s_ln2, hb, s_wo)

            def shift_ln2(b):
                dve.wait_ge(s_ln2p, b + 1)
                V.scalar_tensor_tensor(ln2_nmr[:, :], ln2_mv[:, :, 0], -1.0, ln2_rstd[:, :], ALU.mult, ALU.mult)\
                    .then_inc(s_ln2, 1)

            def split_x2(b):
                dve.wait_ge(s_x2, NT * (b + 1))
                if later(b):
                    dve.wait_ge(s_x2T, 3 * b)
                split(x2_split[:, :, 0:D], x2_split[:, :, D:2 * D], x2[:, :, :], s_x2s, 2 * b)

            def result(b, k):
                dve.wait_ge(s_fc2, 2 * b + k + 1)
                if later(b):
                    dve.wait_ge((s_stA, s_stB)[k], (32, 16)[k] * b)
                V.tensor_tensor(res[:, 2 * k:2 * k + 2, :], hb[k][:, 0:2 * D].rearrange("p (t d) -> p t d", t=2),
                                fc2_b[:, :].unsqueeze(1).broadcast_to([P, 2, D]), ALU.add).then_inc(s_res, 1)

            def body(i, has_back, has_next):
                b = i - 1
                if has_back:
                    statistics_ln2(b)
                rotary(i, 0, 0)
                if has_back:
                    shift_ln2(b)
                rotary(i, 0, 1)
                if has_back:
                    split_x2(b)
                for t in range(1, NT):
                    rotary(i, t, 0)
                    rotary(i, t, 1)
                gates(i)
                states(i, 0)
                mask(i, 0)
                states(i, 1)
                channel_statistics(i, 0)
                if has_back:
                    result(b, 0)
                mask(i, 1)
                states(i, 2)
                head_means(i, 0)
                if has_next:
                    split_embeddings(i + 1)
                head_factors(i, 0)
                channel_statistics(i, 1)
                mask(i, 2)
                gating(i, 0)
                if has_next:
                    statistics_ln1(i + 1)
                head_means(i, 1)
                head_factors(i, 1)
                if has_next:
                    normalise_embeddings(i + 1)
                channel_statistics(i, 2)
                gating(i, 1)
                head_means(i, 2)
                if has_back:
                    result(b, 1)
                head_factors(i, 2)
                gating(i, 2)

            dve.wait_ge(s_set_pe, 1)
            V.tensor_copy(up_cen[:, 0:2 * R], bank[0][:, 0:2 * R]).then_inc(s_set_dve, 1)
            V.tensor_copy(up_cen[0:D - P, 2 * R:4 * R], bank[1][0:D - P, 0:2 * R]).then_inc(s_set_dve, 1)
            for n in range(WC // BC):
                dve.wait_ge(s_set_pe, 2 + n)
                at = slice(n * BC, (n + 1) * BC)
                split(w_hi[:, at], w_lo[:, at], bank[n % RING][:, 0:BC], s_set_dve, 2 + 2 * n)
            done = 2 + 2 * (WC // BC)
            dve.wait_ge(s_stage, N_STAGE)
            split(up_hi[:, :], up_lo[:, :], up_stage, s_set_dve, done)
            V.tensor_copy(fc1_hi[:, :, :], fc1_stage.rearrange("p (c f) -> p c f", c=3)).then_inc(s_set_dve, 1)
            dve.wait_ge(s_set_dve, done + 3)
            V.tensor_tensor(fc1_lo[:, :, :], fc1_stage[:, 0:2 * F].rearrange("p (c f) -> p c f", c=2),
                            fc1_hi[:, 0:2, :].bitcast(fp32), ALU.subtract).then_inc(s_set_dve, 1)
            dve.wait_ge(s_const, N_CONST)
            split_embeddings(0)
            statistics_ln1(0)
            normalise_embeddings(0)

            body(0, False, True)
            with nc.vector.Fori(1, B - 1) as i:
                body(i, True, True)
            body(B - 1, True, False)
            statistics_ln2(B - 1)
            shift_ln2(B - 1)
            split_x2(B - 1)
            result(B - 1, 0)
            result(B - 1, 1)

            step = [0]

            def chain(ins):
                ins.then_inc(s_cd, 1)
                step[0] += 1
                dve.wait_ge(s_cd, step[0])

            dve.wait_ge(s_rot, 2 * NT * B)
            V.memset(g_half, 0.5).then_inc(s_cd, 1)
            step[0] += 1
            dve.wait_ge(s_cl, N_CL)
            dve.wait_ge(s_cpe, 1)
            for s in range(2):
                for c, n in ((0, P), (1, D - P)):
                    V.tensor_copy(x2c_t[0:n, c, s * CT:(s + 1) * CT], bank[2 * s + c][0:n, 0:CT]).then_inc(s_cd, 1)
                    step[0] += 1
            assert step[0] == CD_T

            def dot(o, x, y):
                chain(V.tensor_tensor_reduce(out=g_junk, in0=x, in1=y, scale=1.0, scalar=0.0, op0=ALU.mult,
                                             op1=ALU.add, accum_out=o))

            for s in range(2):
                dot(g_sq[:, s:s + 1], x2c_sb[:, s, :], x2c_sb[:, s, :])
                for r in range(2):
                    k = 2 * s + r
                    dot(g_sq[:, 2 + k:3 + k], gw_sb[:, s, r, :], gw_sb[:, s, r, :])
                    dot(g_dot[:, k:k + 1], x2c_sb[:, s, :], gw_sb[:, s, r, :])
            assert step[0] == CD_SQ
            dve.wait_ge(s_cg, 1)
            chain(V.tensor_scalar(g_nrm, g_nrm, 1e-12, None, ALU.max))
            chain(V.reciprocal(g_sq, g_nrm))
            logits = g_log.rearrange("p s r -> p (s r)")
            chain(V.tensor_tensor(logits, g_dot, g_sq[:, 2:6], ALU.mult))
            chain(V.tensor_tensor(g_log, g_log, g_sq[:, 0:2].unsqueeze(2).broadcast_to([CT, 2, 2]), ALU.mult))
            chain(V.tensor_tensor(g_log, g_log, bal_sb, ALU.add))
            d = g_x[:, 0:2]
            chain(V.tensor_tensor(d, g_log[:, :, 1], g_log[:, :, 0], ALU.subtract))
            chain(V.tensor_scalar(g_x[:, 8:10], d, -1.0, None, ALU.mult))
            chain(V.tensor_tensor(g_x[:, 2:4], d, g_x[:, 8:10], ALU.max))
            assert step[0] == CD_DIFF
            chain(V.tensor_scalar(g_x[:, 10:12], d, 0.0, None, ALU.is_gt))
            chain(V.tensor_scalar(g_x[:, 12:14], g_x[:, 10:12], -1.0, 1.0, ALU.mult, ALU.add))
            dve.wait_ge(s_ct, 1)
            chain(V.tensor_scalar(g_x[:, 6:8], g_x[:, 4:6], 0.5, 0.5, ALU.mult, ALU.add))
            dve.wait_ge(s_co, 1)
            for s in range(2):
                chain(V.tensor_tensor(c_a, bank[s][0:CT, 0:D], ob_sb[:, s, 0, :], ALU.add))
                chain(V.tensor_scalar(c_b, c_a, g_x[:, 12 + s:13 + s], None, ALU.mult))
                chain(V.tensor_tensor(c_c, bank[2 + s][0:CT, 0:D], ob_sb[:, s, 1, :], ALU.add))
                chain(V.scalar_tensor_tensor(c_a, c_c, g_x[:, 10 + s:11 + s], c_b, ALU.mult, ALU.add))
                chain(V.scalar_tensor_tensor(c_res[:, s, :], c_a, g_x[:, 6 + s:7 + s], h2c_sb[:, s, :], ALU.mult, ALU.add))
            assert step[0] == CLS_STEPS


def tables():
    f = np.float32
    half = np.arange(HALF, dtype=f)
    inv_freq = (f(1.0) / np.power(f(10000.0), half / f(HALF))).astype(f)
    pos = np.arange(T, dtype=f)
    angle = (pos[:, None] * inv_freq[None, :]).astype(f).astype(np.float64)
    zeta = ((half + f(HALF)) / f(DK)).astype(np.float64)
    p64 = np.arange(T, dtype=np.float64)
    cos = np.zeros((T, 2, H, HALF))
    sin = np.zeros((T, 2, H, DK))
    for h in range(H):
        gamma = 1.0 - 2.0 ** (-(5 + h))
        rows = np.cumsum(gamma ** p64)
        for k, sign in ((0, -1.0), (1, 1.0)):
            scale = zeta[None, :] ** (sign * p64[:, None] / 512.0) * (gamma ** (sign * p64))[:, None]
            if k == 1:
                scale = scale * (DK ** -0.5 / np.sqrt(np.maximum(rows, 1e-6)))[:, None]
            cos[:, k, h, :] = np.cos(angle) * scale
            sin[:, k, h, :HALF] = -np.sin(angle) * scale
            sin[:, k, h, HALF:] = np.sin(angle) * scale
    lay = lambda x: np.ascontiguousarray(x.reshape(NT, P, 2, H, -1).transpose(1, 0, 2, 3, 4).astype(f))
    return lay(cos), lay(sin)


def columns(x):
    return x.reshape(-1, P).T


def kernel(**inputs):
    import concourse.bacc as bacc
    from concourse.bass_utils import run_bass_kernel_spmd as run

    given = {k: np.asarray(x) for k, x in inputs.items()}
    cos, sin = tables()
    heads = np.zeros((P, P), np.float32)
    heads[:DV, :DV] = heads[DV:, DV:] = 1.0 / DV
    arrays = {
        "ids": given["x"].reshape(B, NT, P).transpose(0, 2, 1),
        "table": given["L0_tok_embed_table"], "up": given["L0_tok_proj_up"], "up_t": given["L0_tok_proj_up"].T,
        "wk": given["L0_attn_Wk"], "wq": given["L0_attn_Wq"], "wv": given["L0_attn_Wv"], "wg": given["L0_attn_Wg"],
        "wo": given["L0_attn_Wo"], "gn_w": columns(given["L0_attn_gn_weight"]), "gn_b": columns(given["L0_attn_gn_bias"]),
        "fc1_t": given["L0_ffn_fc1_w"].T, "fc1_b": columns(given["L0_ffn_fc1_b"]),
        "fc2_t": given["L0_ffn_fc2_w"].T, "fc2_b": given["L0_ffn_fc2_b"],
        "gate_pair": given["L0_ffn_gate_pair"], "balance": given["L0_ffn_balance_bias"],
        "ain_t": given["L0_ffn_atom_in_w"].transpose(0, 2, 1), "ain_b": given["L0_ffn_atom_in_b"].reshape(NATOM, NF, P).transpose(2, 0, 1),
        "aout_t": given["L0_ffn_atom_out_w"].transpose(0, 2, 1), "aout_b": given["L0_ffn_atom_out_b"],
        "cos_t": cos, "sin_t": sin, "ident": np.eye(P, dtype=np.float32), "head_mean": heads,
        "causal": np.triu(np.ones((P, P), np.float32)),
        "center": (np.eye(D) - 1.0 / D).astype(np.float32),
    }
    nc = bacc.Bacc("TRN2", target_bir_lowering=False, num_devices=1)
    fed, a = {}, {}
    for name, x in arrays.items():
        fed[f"in_{name}"] = np.ascontiguousarray(x)
        a[name] = nc.dram_tensor(f"in_{name}", x.shape, mybir.dt.from_np(x.dtype), kind="ExternalInput").ap()
    for name in ("x2c", "h2c"):
        a[name] = nc.dram_tensor(name, (NCLS, B, D), mybir.dt.float32, kind="Internal").ap()
    a["out"] = nc.dram_tensor("out", (B, T, D), mybir.dt.float32, kind="ExternalOutput").ap()
    build(nc, a)
    return run(nc, [fed], core_ids=[0]).results[0]["out"]
```

```python
import concourse.bass as bass
from concourse import mybir
from contextlib import ExitStack
import numpy as np

B, T = 32, 512
VOCAB, R, D = 12565, 64, 192
H, DK, DV = 6, 128, 64
F = 768
NCLS, NATOM = 6, 5
SRC = [(0, 3), (0, 4), (1, 3), (1, 4), (2, 3), (2, 4)]
P = 128
NT = T // P
NP = H // 2
HALF = DK // 2
QK = H * DK
VC = H * DV
WC = 2 * QK + 2 * VC
V_AT, G_AT = 2 * QK, 2 * QK + VC
NF = F // P
PC = 4 * DK
LN_EPS = 1e-5

RING = 6
SC = WC // RING
BACK, NEXT = -1, 1


def ring_jobs():
    def rotary(p, t, turn=0):
        return ("rotary_products", NT * p + t, NT * NP, turn)

    def value(t, turn=0):
        return ("v_ready", t, NT, turn)

    def gate(m):
        return ("gate_ready", m, NP, 0)

    def hidden(m):
        return ("hidden_ready", m, NF, BACK)

    def gn(p):
        return ("gn_steps", 8 * p + 4, 8 * NP, 0)

    turned = [[("kq_t_ready", 4 * p + j, 4 * NP, 0) for j in range(4)] for p in range(NP)]
    states = [("state_steps", 3 * p + 2, 3 * NP, 0) for p in range(NP)]
    scores = [[("probs_ready", 2 * p + j, 2 * NP, 0) for j in range(2)] for p in range(NP)]
    outs = [("att_ready", p, NP, 0) for p in range(NP)]
    jobs = [value(2), value(3), rotary(1, 0)] + turned[0] + [rotary(1, 1), states[0]]
    jobs += scores[0] + [gate(0)] + [("x2_t_ready", c, 3, BACK) for c in range(3)] + [rotary(1, 2), outs[0]]
    jobs += [rotary(1, 3), hidden(0), rotary(2, 0), hidden(1), gate(1), gn(0)] + turned[1] + [states[1]]
    jobs += [hidden(2), rotary(2, 1)] + [("emb_t_ready", k, 2, NEXT) for k in range(2)] + [hidden(3)] + scores[1]
    jobs += [gate(2)] + [("ln1_steps", k, 10, NEXT) for k in (1, 3)] + [hidden(4), rotary(2, 2), outs[1]]
    jobs += [hidden(5), rotary(2, 3), ("norm_t_ready", 0, 1, NEXT), gn(1), rotary(0, 0, NEXT)] + turned[2]
    jobs += [states[2], rotary(0, 1, NEXT)] + scores[2] + [rotary(0, 2, NEXT), rotary(0, 3, NEXT), outs[2], gn(2)]
    jobs += [value(0, NEXT), value(1, NEXT)]
    return jobs


JOBS = ring_jobs()
assert len(JOBS) % RING == 0 and all(turn != BACK for _, _, _, turn in JOBS[-RING:])


def job(name, index):
    return next(q for q, (n, k, _, _) in enumerate(JOBS) if (n, k) == (name, index))


def user_before(i, q):
    turn = 0
    while True:
        q -= RING
        if q < 0:
            q += len(JOBS)
            turn -= 1
        name, index, count, of = JOBS[q]
        sequence = i + turn + of
        if isinstance(i, int):
            if i + turn < -1:
                return None
            if not 0 <= sequence < B:
                continue
        return name, sequence * count + index + 1


def build(nc, a):
    fp32, f32r = mybir.dt.float32, mybir.dt.float32r
    u32 = mybir.dt.uint32
    ALU, ACT = mybir.AluOpType, mybir.ActivationFunctionType

    with ExitStack() as ctx:
        def sb(name, shape, dt=fp32):
            return ctx.enter_context(nc.sbuf_tensor(name, shape, dt))

        def sem(name):
            return ctx.enter_context(nc.semaphore(name))

        ident = sb("ident", [P, P])
        head_mean = sb("head_mean", [P, P])
        causal = sb("causal", [P, P])
        cos_t = sb("cos_t", [P, NT, NP, 4, HALF])
        sin_t = sb("sin_t", [P, NT, NP, 4, DK])
        w_hi = sb("w_hi", [P, WC], f32r)
        w_lo = sb("w_lo", [P, WC], f32r)
        up_hi = sb("up_hi", [P, D], f32r)
        up_lo = sb("up_lo", [P, D], f32r)
        fc1_hi = sb("fc1_hi", [P, 3, F], f32r)
        fc1_lo = sb("fc1_lo", [P, 2, F], f32r)
        fc1_b = sb("fc1_b", [P, NF])
        fc2 = sb("fc2", [P, NF, D])
        fc2_b = sb("fc2_b", [P, D])
        wo = sb("wo", [P, NP, D])
        gn_w = sb("gn_w", [P, NP])
        gn_b = sb("gn_b", [P, NP])
        neg_half = sb("neg_half", [P, NT])

        ids = sb("ids", [P, NT], mybir.dt.int32)
        emb = sb("emb", [P, NT * R])
        emb_split = sb("emb_split", [P, NT, 2 * R], f32r)
        emb_norm = sb("emb_norm", [P, NT, R])
        norm_split = sb("norm_split", [P, NT, 2 * R], f32r)
        emb_t = sb("emb_t", [P, T], f32r)
        emb_keep = sb("emb_keep", [P, T], f32r)
        norm_t = sb("norm_t", [P, T], f32r)
        ln1_st = sb("ln1_st", [P, NT, 6])
        ln1_mv = sb("ln1_mv", [P, NT, 2])
        ln1_ve = sb("ln1_ve", [P, NT])
        ln1_rstd = sb("ln1_rstd", [P, NT])
        rot_c = sb("rot_c", [P, 3, PC])
        rot_s = sb("rot_s", [P, 3, PC])
        kq = sb("kq", [P, NP, NT, 4, DK])
        v = sb("v", [P, NT, VC])
        gate = sb("gate", [P, NP, T])
        kq_t = sb("kq_t", [P, 2, 4, T])
        state = sb("state", [P, 2, NT - 1, P])
        probs = sb("probs", [P, 2, 2, T])
        att = sb("att", [P, NP, T])
        gn_st = sb("gn_st", [P, NP, 6])
        gn_mv = sb("gn_mv", [P, NP, 2])
        gn_d = sb("gn_d", [P, NP])
        gn_dd = sb("gn_dd", [P, NP])
        gn_m2 = sb("gn_m2", [P, NP])
        gn_ve = sb("gn_ve", [P, NP])
        gn_rstd = sb("gn_rstd", [P, NP])
        gn_a = sb("gn_a", [P, NP])
        gn_ma = sb("gn_ma", [P, NP])
        gn_c = sb("gn_c", [P, NP])
        ln2_st = sb("ln2_st", [P, NT, 6])
        ln2_mv = sb("ln2_mv", [P, NT, 2])
        ln2_ve = sb("ln2_ve", [P, NT])
        ln2_rstd = sb("ln2_rstd", [P, NT])
        ln2_nmr = sb("ln2_nmr", [P, NT])
        x2 = sb("x2", [P, NT, D])
        x2_split = sb("x2_split", [P, NT, 2 * D], f32r)
        x2_t = sb("x2_t", [P, 3, T], f32r)
        hid = sb("hid", [P, NF, T])
        h2_cls = sb("h2_cls", [NCLS, D])
        res = sb("res", [P, NT, D])

        bank = [ctx.enter_context(nc.psum_tensor(f"ring{k}", [P, 512], fp32)) for k in range(RING)]
        hb = [ctx.enter_context(nc.psum_tensor(f"resid{k}", [P, 512], fp32)) for k in range(2)]

        w_stage = kq[:, :, :, :, :].rearrange("p a t g d -> p (a t g d)")
        wa = w_stage[:, 0:WC]
        wb = w_stage[0:D - P, WC:2 * WC]
        fc1_stage = hid[:, :, :].rearrange("p c t -> p (c t)")[:, 0:3 * F]
        center = rot_s[:, 0, 0:2 * D]
        up_dup = rot_s[:, 1, 0:4 * R]
        up_cen = rot_s[:, 1, 4 * R:8 * R]
        up_stage = rot_s[:, 2, 0:D]

        s_first = sem("up_and_identity_loaded")
        s_center = sem("centring_loaded")
        s_stage = sem("projections_staged")
        s_tables = sem("rotary_tables_loaded")
        s_const = sem("constants_loaded")
        s_set_pe = sem("setup_products")
        s_set_dve = sem("setup_steps")
        s_set_pool = sem("exponents_ready")
        s_ids = sem("ids_loaded")
        s_emb = sem("embeddings_gathered")
        s_embsplit = sem("embedding_split")
        s_embT = sem("embedding_transposed")
        s_embt = sem("emb_t_ready")
        s_hstat = sem("h_for_ln1")
        s_ln1 = sem("ln1_steps")
        s_ln1p = sem("ln1_rstd_ready")
        s_normsplit = sem("norm_split_ready")
        s_normT = sem("norm_transposed")
        s_normt = sem("norm_t_ready")
        s_proj = sem("kq_projected")
        s_vproj = sem("v_projected")
        s_gproj = sem("gate_projected")
        s_rotm = sem("rotary_products")
        s_rot = sem("kq_rotated")
        s_v = sem("v_ready")
        s_tanh = sem("gate_tanh")
        s_gate = sem("gate_ready")
        s_T = sem("kq_transposed")
        s_t = sem("kq_t_ready")
        s_kv = sem("kv_products")
        s_state = sem("state_steps")
        s_score = sem("scores_done")
        s_prob = sem("probs_ready")
        s_o = sem("attention_out")
        s_att = sem("att_ready")
        s_gns = sem("gn_channel_stats")
        s_gns2 = sem("gn_channel_sums")
        s_gnpe = sem("gn_head_sums")
        s_gn = sem("gn_steps")
        s_gnp = sem("gn_rstd_ready")
        s_aff = sem("gn_applied")
        s_aff2 = sem("gn_applied_last_pair")
        s_gated = sem("gated_ready")
        s_keep = sem("embeddings_kept")
        s_hres = sem("residual_product")
        s_wo = sem("h2_done")
        s_ln2 = sem("ln2_steps")
        s_ln2p = sem("ln2_rstd_ready")
        s_x2 = sem("x2_ready")
        s_x2s = sem("x2_split_ready")
        s_x2T = sem("x2_transposed")
        s_x2t = sem("x2_t_ready")
        s_fc1 = sem("fc1_product")
        s_hid = sem("hidden_ready")
        s_fc2 = sem("fc2_product")
        s_res = sem("result_ready")
        s_h2c = sem("h2_cls_ready")
        s_stA = sem("result_stored_first_tiles")
        s_stB = sem("result_stored_last_tiles")
        s_xc = sem("x2_cls_stored")
        s_hc = sem("h2_cls_stored")
        by_name = {"rotary_products": s_rotm, "v_ready": s_v, "gate_ready": s_gate, "kq_t_ready": s_t,
                   "state_steps": s_state, "probs_ready": s_prob, "att_ready": s_att,
                   "emb_t_ready": s_embt, "ln1_steps": s_ln1, "norm_t_ready": s_normt,
                   "x2_t_ready": s_x2t, "hidden_ready": s_hid, "gn_steps": s_gn}

        s_apart = {nc.vector: sem("dve_went_on"), nc.gpsimd: sem("pool_went_on")}
        N_FIRST, N_CENTER, N_STAGE, N_TABLES, N_CONST = 16 * 3, 16 * 6, 16 * 2, 16 * 2, 16 * 12
        SET_UP, SET_CEN, SET_W, SET_FC1 = 2, 4, 4 + 2 * RING, 6 + 2 * RING
        NQ = NCLS // 2
        N_CL, N_CW = 16 * (NQ * 5 + 1), 16 * NATOM * 2
        CD_T, CD_SQ, CD_DIFF, CLS_STEPS = 6, 16, 24, 35

        def wait_apart(eng, s, value):
            eng.wait_ge(s, value)
            eng.sem_inc(s_apart[eng], 1)

        def later(i):
            return not (isinstance(i, int) and i == 0)

        def bank_of(name, index):
            return bank[job(name, index) % RING]

        def back_bank(b, name, index):
            if isinstance(b, int) and b == B - 1:
                return bank[(index if name == "x2_t_ready" else 3 + index) % RING]
            return bank_of(name, index)

        def take(pe, i, name, index):
            if isinstance(i, int) and i == B:
                return back_bank(B - 1, name, index)
            q = job(name, index)
            before = user_before(i, q)
            if before:
                pe.wait_ge(by_name[before[0]], before[1])
            return bank[q % RING]

        CT = NQ * B
        rows_c = rot_c[0:CT, :, :].rearrange("p a n -> p (a n)")
        rows_s = rot_s[0:CT, :, :].rearrange("p a n -> p (a n)")
        kq_flat = kq_t[:, :, :, :].rearrange("p s k t -> p (s k t)")
        x2c_sb = rows_c[:, 0:2 * D].rearrange("p (s d) -> p s d", s=2)
        h2c_sb = rows_c[:, 2 * D:4 * D].rearrange("p (s d) -> p s d", s=2)
        gw_sb = rows_c[:, 4 * D:8 * D].rearrange("p (s r d) -> p s r d", s=2, r=2)
        ob_sb = kq_flat[0:CT, 6 * D:10 * D].rearrange("p (s r d) -> p s r d", s=2, r=2)
        c_res = kq_flat[0:CT, 10 * D:12 * D].rearrange("p (s d) -> p s d", s=2)
        bal_sb = kq_flat[0:CT, 12 * D:12 * D + 4].rearrange("p (s r) -> p s r", s=2)
        ib_sb = kq_flat[:, 12 * D + 4:12 * D + 4 + NATOM * NF].rearrange("p (a m) -> p a m", a=NATOM)
        x2c_t = rot_s[:, 0, 0:2 * NCLS * B].rearrange("p (c n) -> p c n", c=2)
        g_junk = rows_s[:, 2 * D:3 * D]
        g_sq, g_dot = rows_s[:, 3 * D:3 * D + 6], rows_s[:, 3 * D + 6:3 * D + 10]
        g_nrm = rows_s[:, 3 * D + 10:3 * D + 16]
        g_log = rows_s[:, 3 * D + 16:3 * D + 20].rearrange("p (s r) -> p s r", s=2)
        g_x = rows_s[:, 3 * D + 20:3 * D + 34]
        g_half = rows_s[:, 3 * D + 34:3 * D + 40]
        c_a, c_b = (rows_s[:, k * D:(k + 2) * D].rearrange("p (s d) -> p s d", s=2) for k in (4, 6))
        c_hid = cos_t[:, :, :, :, :].rearrange("p t a g d -> p (t a g d)")[:, 0:2 * NF * NCLS * B].rearrange(
            "p (r m s q b) -> p r m s q b", r=2, m=NF, s=2, q=NQ)
        w_in = sin_t[:, :, :, :, :].rearrange("p t a g d -> p (t a g d)")
        w_outs = v[:, :, :].rearrange("p t n -> p (t n)")
        s_cl = sem("cls_loaded")
        s_cw = sem("cls_first_layers_loaded")
        s_cwo = sem("cls_second_layers_loaded")
        s_cd = sem("cls_steps_dve")
        s_cpe = sem("cls_pe_transposes")
        s_ch = sem("cls_hidden_product")
        s_chf = sem("cls_hidden_ready")
        s_co = sem("cls_out_product")
        s_ct = sem("cls_tanh")
        s_cg = sem("cls_pool")
        s_cs = sem("cls_stored")

        def w_in_at(atom, c):
            n = 2 * atom + c
            if n < 8:
                return w_in[:, n * F:(n + 1) * F]
            return w_stage[:, (n - 8) * F:(n - 7) * F]

        def w_out_at(atom):
            size = NF * D
            src = [w_stage[:, 2 * F:2 * F + size], w_stage[:, 2 * F + size:2 * F + 2 * size],
                   w_stage[:, 2 * F + 2 * size:2 * F + 3 * size], w_outs[:, 0:size],
                   kq_flat[:, 0:size]][atom]
            return src.rearrange("p (c d) -> p c d", c=NF)

        block = ctx.enter_context(nc.Block())

        @block.sync
        def _(sp):
            def load(dst, src, s):
                sp.dma_start(dst, src).then_inc(s, 16)

            load(ids[:, :], a["ids"][0, :, :], s_ids)
            for k in range(2):
                load(up_stage[k * R:(k + 1) * R, :], a["up_t"], s_first)
            load(ident[:, :], a["ident"], s_first)
            load(center[:, 0:D], a["center"][0:P, :], s_center)
            load(center[0:D - P, D:2 * D], a["center"][P:D, :], s_center)
            for k in range(2):
                load(up_dup[:, k * R:(k + 1) * R], a["up"][0:P, :], s_center)
                load(up_dup[0:D - P, 2 * R + k * R:2 * R + (k + 1) * R], a["up"][P:D, :], s_center)
            load(wa, a["w"][0:P, :], s_stage)
            load(wb, a["w"][P:D, :], s_stage)
            load(cos_t[:, :, :, :, :], a["cos_t"], s_tables)
            load(sin_t[:, :, :, :, :], a["sin_t"], s_tables)
            load(causal[:, :], a["causal"], s_const)
            load(head_mean[:, :], a["head_mean"], s_const)
            load(gn_w[:, :], a["gn_w"], s_const)
            load(gn_b[:, :], a["gn_b"], s_const)
            load(wo[:, :, :], a["wo"].rearrange("(c p) d -> p c d", p=P), s_const)
            load(fc1_stage[:, 0:F], a["fc1_t"][0:P, :], s_const)
            load(fc1_stage[0:D - P, F:2 * F], a["fc1_t"][P:D, :], s_const)
            load(fc1_stage[D - P:P, F:2 * F], a["fc1_t"][0:2 * P - D, :], s_const)
            load(fc1_stage[:, 2 * F:3 * F], a["fc1_t"][D - P:D, :], s_const)
            load(fc1_b[:, :], a["fc1_b"], s_const)
            load(fc2[:, :, :], a["fc2_t"].rearrange("(c p) d -> p c d", p=P), s_const)
            load(fc2_b[:, :], a["fc2_b"].partition_broadcast(P), s_const)

            def store_class_rows(b):
                sp.wait_ge(s_h2c, b + 1)
                sp.dma_start(a["h2c"][:, b, :], h2_cls[:, :]).then_inc(s_hc, 16)
                sp.wait_ge(s_x2, NT * b + 1)
                sp.dma_start(a["x2c"][:, b, :], x2[0:NCLS, 0, :]).then_inc(s_xc, 16)

            def store_first_tiles(b):
                sp.wait_ge(s_res, 2 * b + 1)
                sp.dma_start(a["out"][b, NCLS:P, :], res[NCLS:P, 0, :]).then_inc(s_stA, 16)
                sp.dma_start(a["out"][b, P:2 * P, :], res[:, 1, :]).then_inc(s_stA, 16)

            def store_last_tiles(b):
                sp.wait_ge(s_res, 2 * b + 2)
                sp.dma_start(a["out"][b, 2 * P:T, :].rearrange("(t p) d -> p t d", p=P),
                             res[:, 2:NT, :]).then_inc(s_stB, 16)

            def cls_weights():
                sp.wait_ge(s_rotm, NT * NP * B)
                for atom in range(NATOM):
                    if atom == NATOM - 1:
                        sp.wait_ge(s_o, NP * B)
                    sp.dma_start(w_in_at(atom, 0), a["ain_t"][atom, 0:P, :]).then_inc(s_cw, 16)
                    sp.dma_start(w_in_at(atom, 1), a["ain_t"][atom, D - P:D, :]).then_inc(s_cw, 16)
                for q in range(NQ):
                    rows, two = slice(q * B, (q + 1) * B), slice(2 * q, 2 * q + 2)
                    for dst, name in ((gw_sb, "gate_pair"), (ob_sb, "route_b")):
                        src = a[name][two, :, :].rearrange("s r d -> (s r d)")
                        sp.dma_start(dst[rows, :, :, :].rearrange("b s r d -> b (s r d)"), src.partition_broadcast(B))\
                            .then_inc(s_cl, 16)
                    sp.dma_start(bal_sb[rows, :, :].rearrange("b s r -> b (s r)"),
                                 a["balance"][two, :].rearrange("s r -> (s r)").partition_broadcast(B)).then_inc(s_cl, 16)
                sp.dma_start(ib_sb, a["ain_b"]).then_inc(s_cl, 16)

            def body(i, has_back, has_next):
                if has_next:
                    sp.wait_ge(s_emb, 64 * (i + 1))
                    sp.dma_start(ids[:, :], a["ids"][i + 1, :, :]).then_inc(s_ids, 16)
                if has_back:
                    store_class_rows(i - 1)
                    store_first_tiles(i - 1)
                    if not has_next:
                        cls_weights()
                    store_last_tiles(i - 1)

            def cls_rows():
                sp.wait_ge(s_hc, 16 * B)
                sp.wait_ge(s_xc, 16 * B)
                for q in range(NQ):
                    rows = slice(q * B, (q + 1) * B)
                    for dst, name in ((x2c_sb, "x2c"), (h2c_sb, "h2c")):
                        sp.dma_start(dst[rows, :, :], a[name][2 * q:2 * q + 2, :, :].rearrange("s b d -> b s d"))\
                            .then_inc(s_cl, 16)
                for atom in range(NATOM):
                    sp.dma_start(w_out_at(atom), a["aout_t"][atom, :, :].rearrange("(c p) d -> p c d", p=P)).then_inc(s_cwo, 16)
                store_first_tiles(B - 1)
                store_last_tiles(B - 1)
                sp.wait_ge(s_cd, CLS_STEPS)
                for n in range(NCLS):
                    s, q = n % 2, n // 2
                    sp.dma_start(a["out"][:, n, :], c_res[q * B:(q + 1) * B, s, :]).then_inc(s_cs, 16)

            body(0, False, True)
            with sp.Fori(1, B - 1) as i:
                body(i, True, True)
            body(B - 1, True, False)
            store_class_rows(B - 1)
            cls_rows()
            sp.wait_ge(s_stA, 32 * B)
            sp.wait_ge(s_stB, 16 * B)
            sp.wait_ge(s_cs, 16 * NCLS)

        @block.gpsimd
        def _(pool):
            nc.gpsimd.memset(neg_half[:, :], -0.5).then_inc(s_set_pool, 1)

            def gather(b):
                wait_apart(pool, s_ids, 16 * (b + 1))
                for t in range(NT):
                    nc.gpsimd.indirect_dma_start(
                        emb[:, t * R:(t + 1) * R], None, a["table"],
                        bass.IndirectOffsetOnAxis(ids[:, t:t + 1].bitcast(u32), 0)).then_inc(s_emb, 16)

            def rsqrt_ln1(b):
                pool.wait_ge(s_ln1, 10 * b + 9)
                nc.gpsimd.tensor_tensor(ln1_rstd[:, :], ln1_ve[:, :], neg_half[:, :], ALU.pow).then_inc(s_ln1p, 1)

            def rsqrt_ln2(b):
                pool.wait_ge(s_ln2, 10 * b + 9)
                nc.gpsimd.tensor_tensor(ln2_rstd[:, :], ln2_ve[:, :], neg_half[:, :], ALU.pow).then_inc(s_ln2p, 1)

            def rsqrt_gn(i, p):
                pool.wait_ge(s_gn, 24 * i + 8 * p + 5)
                nc.gpsimd.tensor_tensor(gn_rstd[:, p:p + 1], gn_ve[:, p:p + 1], neg_half[:, 0:1], ALU.pow)\
                    .then_inc(s_gnp, 1)

            def rotate(i, p, t):
                n = NT * p + t
                pool.wait_ge(s_rotm, NT * NP * i + n + 1)
                if t == 0 and later(i):
                    pool.wait_ge(s_kv, NP * (i - 1) + p + 1)
                nc.gpsimd.tensor_tensor(kq[:, p, t, :, :].rearrange("p g d -> p (g d)"), rot_c[:, n % 3, :],
                                        rot_s[:, n % 3, :], ALU.add).then_inc(s_rot, 1)

            def body(i, has_back, has_next):
                b = i - 1
                if has_back:
                    rsqrt_ln2(b)
                rotate(i, 1, 0)
                rotate(i, 1, 1)
                if has_next:
                    pool.wait_ge(s_ln1, 10 * (i + 1))
                    gather(i + 1)
                rotate(i, 1, 2)
                rotate(i, 1, 3)
                rotate(i, 2, 0)
                rsqrt_gn(i, 0)
                rotate(i, 2, 1)
                if has_next:
                    rsqrt_ln1(i + 1)
                rotate(i, 2, 2)
                rotate(i, 2, 3)
                rsqrt_gn(i, 1)
                if has_next:
                    rotate(i + 1, 0, 0)
                    rotate(i + 1, 0, 1)
                    rotate(i + 1, 0, 2)
                    rotate(i + 1, 0, 3)
                rsqrt_gn(i, 2)

            gather(0)
            pool.wait_ge(s_set_pool, 1)
            rsqrt_ln1(0)
            for t in range(NT):
                rotate(0, 0, t)
            body(0, False, True)
            with nc.gpsimd.Fori(1, B - 1) as i:
                body(i, True, True)
            body(B - 1, True, False)
            rsqrt_ln2(B - 1)
            pool.wait_ge(s_cd, CD_SQ)
            nc.gpsimd.tensor_tensor(g_nrm, g_sq, g_half, ALU.pow).then_inc(s_cg, 1)

        @block.scalar
        def _(act):
            def emb_evac(b):
                if later(b):
                    act.wait_ge(s_keep, b)
                for k in range(2):
                    act.wait_ge(s_embT, 2 * b + k + 1)
                    nc.scalar.activation(emb_t[:, k * 256:(k + 1) * 256], bank_of("emb_t_ready", k)[:, 0:256],
                                         ACT.Copy).then_inc(s_embt, 1)

            def keep_embeddings(i):
                if later(i):
                    act.wait_ge(s_hres, 2 * i)
                act.wait_ge(s_embt, 2 * i + 2)
                nc.scalar.activation(emb_keep[:, :], emb_t[:, :].bitcast(fp32), ACT.Copy).then_inc(s_keep, 1)

            def norm_evac(b):
                if later(b):
                    act.wait_ge(s_gproj, NP * b)
                    act.wait_ge(s_proj, NT * NP * b)
                act.wait_ge(s_normT, b + 1)
                nc.scalar.activation(norm_t[:, :], bank_of("norm_t_ready", 0)[:, :], ACT.Copy).then_inc(s_normt, 1)

            def v_evac(i, t):
                act.wait_ge(s_vproj, NT * i + t + 1)
                if t == 0 and later(i):
                    act.wait_ge(s_o, NP * i)
                nc.scalar.activation(v[:, t, :], bank_of("v_ready", t)[:, 0:VC], ACT.Copy).then_inc(s_v, 1)

            def gate_tanh(i, m):
                if m == 0 and later(i):
                    act.wait_ge(s_gated, NP * i)
                act.wait_ge(s_gproj, NP * i + m + 1)
                nc.scalar.activation(gate[:, m, :], bank_of("gate_ready", m)[:, :], ACT.Tanh, scale=0.5)\
                    .then_inc(s_tanh, 1)

            def pair_evac(i, p, parts=range(4)):
                if p == 2:
                    act.wait_ge(s_o, NP * i + 1)
                elif later(i):
                    act.wait_ge(s_o, NP * i - (0 if p == 0 else 1))
                for j in parts:
                    act.wait_ge(s_T, 12 * i + 4 * p + j + 1)
                    nc.scalar.activation(kq_t[:, p % 2, j, :], bank_of("kq_t_ready", 4 * p + j)[:, :], ACT.Copy)\
                        .then_inc(s_t, 1)

            def att_evac(i, p):
                if p == 0 and later(i):
                    act.wait_ge(s_wo, 2 * i)
                act.wait_ge(s_o, NP * i + p + 1)
                nc.scalar.activation(att[:, p, :], bank_of("att_ready", p)[:, :], ACT.Copy).then_inc(s_att, 1)

            def gn_apply(i, m):
                act.wait_ge(s_gn, 24 * i + 8 * m + 8)
                nc.scalar.activation(att[:, m, :], att[:, m, :], ACT.Identity, bias=gn_c[:, m:m + 1],
                                     scale=gn_a[:, m:m + 1]).then_inc(s_aff, 1)

            def h2_class_rows(b):
                if later(b):
                    act.wait_ge(s_hc, 16 * b)
                act.wait_ge(s_ln2, 10 * b + 2)
                nc.scalar.activation(h2_cls[:, :], hb[0][0:NCLS, 0:D], ACT.Copy).then_inc(s_h2c, 1)

            def x2_norm(b):
                if later(b):
                    act.wait_ge(s_xc, 16 * b)
                    act.wait_ge(s_x2s, 2 * b)
                act.wait_ge(s_ln2, 10 * b + 10)
                for t in range(NT):
                    nc.scalar.activation(x2[:, t, :], hb[t // 2][:, (t % 2) * D:(t % 2 + 1) * D], ACT.Identity,
                                         bias=ln2_nmr[:, t:t + 1], scale=ln2_rstd[:, t:t + 1]).then_inc(s_x2, 1)

            def x2_evac(b):
                if later(b):
                    act.wait_ge(s_fc1, NF * b)
                for c in range(3):
                    act.wait_ge(s_x2T, 3 * b + c + 1)
                    nc.scalar.activation(x2_t[:, c, :], back_bank(b, "x2_t_ready", c)[:, :], ACT.Copy).then_inc(s_x2t, 1)

            def gelu(b, m):
                if m == 0 and later(b):
                    act.wait_ge(s_fc2, 2 * b)
                act.wait_ge(s_fc1, NF * b + m + 1)
                nc.scalar.activation(hid[:, m, :], back_bank(b, "hidden_ready", m)[:, :], ACT.Gelu, bias=fc1_b[:, m:m + 1])\
                    .then_inc(s_hid, 1)

            def body(i, has_back, has_next):
                b = i - 1
                keep_embeddings(i)
                v_evac(i, 2)
                v_evac(i, 3)
                if has_back:
                    h2_class_rows(b)
                pair_evac(i, 0, range(3))
                if has_back:
                    x2_norm(b)
                pair_evac(i, 0, (3,))
                gate_tanh(i, 0)
                if has_back:
                    x2_evac(b)
                att_evac(i, 0)
                if has_back:
                    gelu(b, 0)
                    gelu(b, 1)
                gate_tanh(i, 1)
                pair_evac(i, 1)
                if has_back:
                    gelu(b, 2)
                if has_next:
                    emb_evac(i + 1)
                if has_back:
                    gelu(b, 3)
                gn_apply(i, 0)
                gate_tanh(i, 2)
                if has_back:
                    gelu(b, 4)
                att_evac(i, 1)
                if has_back:
                    gelu(b, 5)
                if has_next:
                    norm_evac(i + 1)
                pair_evac(i, 2)
                gn_apply(i, 1)
                att_evac(i, 2)
                if has_next:
                    v_evac(i + 1, 0)
                    v_evac(i + 1, 1)

            nc.scalar.preload_act_table(ACT.Gelu)
            emb_evac(0)
            norm_evac(0)
            v_evac(0, 0)
            v_evac(0, 1)
            act.wait_ge(s_const, N_CONST)
            body(0, False, True)
            with nc.scalar.Fori(1, B - 1) as i:
                body(i, True, True)
            body(B - 1, True, False)
            h2_class_rows(B - 1)
            x2_norm(B - 1)
            x2_evac(B - 1)
            for m in range(NF):
                gelu(B - 1, m)

            act.wait_ge(s_cl, N_CL)
            act.wait_ge(s_rotm, NT * NP * B)
            for atom in range(NATOM):
                for m in range(NF):
                    k = NF * atom + m
                    act.wait_ge(s_ch, k + 1)
                    if atom < NQ:
                        o, n = c_hid[:, 0, m, :, atom, :], 2 * B
                        src = bank[k % RING][:, 0:n].rearrange("p (s b) -> p s b", s=2)
                    else:
                        o, n = c_hid[:, 1, m, atom - NQ, :, :].rearrange("p q b -> p (q b)"), NQ * B
                        src = bank[k % RING][:, 0:n]
                    nc.scalar.activation(o, src, ACT.Gelu, bias=ib_sb[:, atom, m:m + 1]).then_inc(s_chf, 1)
            act.wait_ge(s_cd, CD_DIFF)
            nc.scalar.activation(g_x[:, 4:6], g_x[:, 2:4], ACT.Tanh, scale=0.5).then_inc(s_ct, 1)

        @block.tensor
        def _(pe):
            mm = nc.tensor.matmul

            def turn_embeddings(b):
                pe.wait_ge(s_embsplit, 2 * (b + 1))
                for k in range(2):
                    o = take(pe, b - 1, "emb_t_ready", k)
                    for t in (2 * k, 2 * k + 1):
                        last = nc.tensor.transpose(o[:, (t % 2) * P:(t % 2 + 1) * P], emb_split[:, t, :].bitcast(fp32),
                                                   ident[:, :])
                    last.then_inc(s_embT, 1)

            def embed(o, source, t, starts):
                tok = source[:, t * P:(t + 1) * P]
                mm(o, tok, up_hi[:, :], start=starts, stop=False, skip_group_check=True)
                return mm(o, tok, up_lo[:, :], start=False, stop=True, skip_group_check=True)

            def h_for_statistics(b):
                for k in range(2):
                    pe.wait_ge(s_embt, 2 * b + k + 1)
                    o = take(pe, b - 1, "ln1_steps", 2 * k + 1)
                    for t in (2 * k, 2 * k + 1):
                        last = embed(o[:, (t % 2) * D:(t % 2 + 1) * D], emb_t, t, True)
                    last.then_inc(s_hstat, 1)

            def turn_norm(b):
                pe.wait_ge(s_normsplit, 2 * (b + 1))
                o = take(pe, b - 1, "norm_t_ready", 0)
                for t in range(NT):
                    last = nc.tensor.transpose(o[:, t * P:(t + 1) * P], norm_split[:, t, :].bitcast(fp32), ident[:, :])
                last.then_inc(s_normT, 1)

            def project(i, p, t, turn=0):
                if p == 0 and t == 0:
                    pe.wait_ge(s_normt, i + 1)
                tok = norm_t[:, t * P:(t + 1) * P]
                o = take(pe, i - turn, "rotary_products", NT * p + t)
                mm(o[:, :], tok, w_hi[:, p * PC:(p + 1) * PC], start=True, stop=False)
                mm(o[:, :], tok, w_lo[:, p * PC:(p + 1) * PC], start=False, stop=True).then_inc(s_proj, 1)

            def project_v(i, t, turn=0):
                tok = norm_t[:, t * P:(t + 1) * P]
                o = take(pe, i - turn, "v_ready", t)[:, 0:VC]
                mm(o, tok, w_hi[:, V_AT:V_AT + VC], start=True, stop=False)
                mm(o, tok, w_lo[:, V_AT:V_AT + VC], start=False, stop=True).then_inc(s_vproj, 1)

            def project_gate(i, m):
                o = take(pe, i, "gate_ready", m)[:, :]
                at = slice(G_AT + m * P, G_AT + (m + 1) * P)
                mm(o, w_hi[:, at], norm_t[:, :], start=True, stop=False)
                mm(o, w_lo[:, at], norm_t[:, :], start=False, stop=True).then_inc(s_gproj, 1)

            def residual(i, k):
                if k == 0:
                    pe.wait_ge(s_keep, i + 1)
                if later(i):
                    pe.wait_ge(s_res, 2 * (i - 1) + k + 1)
                for t in (2 * k, 2 * k + 1):
                    last = embed(hb[k][:, (t % 2) * D:(t % 2 + 1) * D], emb_keep, t, t % 2 == 0)
                last.then_inc(s_hres, 1)

            def turn_pair(i, p):
                pe.wait_ge(s_rot, NT * NP * i + NT * (p + 1))
                for j in range(4):
                    o = take(pe, i, "kq_t_ready", 4 * p + j)
                    for t in range(NT):
                        last = nc.tensor.transpose(o[:, t * P:(t + 1) * P], kq[:, p, t, 2 * (j % 2) + j // 2, :], ident[:, :])
                    last.then_inc(s_T, 1)

            def key_values(i, p):
                if p == 0:
                    pe.wait_ge(s_v, NT * (i + 1))
                o = take(pe, i, "state_steps", 3 * p + 2)
                for c in range(NT - 1):
                    for j in range(2):
                        h = 2 * p + j
                        last = mm(o[:, c * P + j * DV:c * P + (j + 1) * DV], kq[:, p, c, j, :],
                                  v[:, c, h * DV:(h + 1) * DV], start=True, stop=True)
                last.then_inc(s_kv, 1)

            def scores(i, p, j):
                pe.wait_ge(s_t, 12 * i + 4 * p + 2 * j + 2)
                o = take(pe, i, "probs_ready", 2 * p + j)
                for c in range(NT):
                    at = slice(c * P, (c + 1) * P)
                    last = mm(o[:, at], kq_t[:, p % 2, 2 * j, at], kq_t[:, p % 2, 2 * j + 1, at], start=True, stop=True)
                last.then_inc(s_score, 1)

            def outputs(i, p):
                pe.wait_ge(s_prob, 6 * i + 2 * p + 2)
                pe.wait_ge(s_state, 9 * i + 3 * p + 3)
                o = take(pe, i, "att_ready", p)
                for c in range(NT):
                    at = slice(c * P, (c + 1) * P)
                    for j in range(2):
                        h = 2 * p + j
                        last = mm(o[j * DV:(j + 1) * DV, at], v[:, c, h * DV:(h + 1) * DV], probs[:, p % 2, j, at],
                                  start=True, stop=c == 0)
                    if c:
                        for j in range(2):
                            last = mm(o[j * DV:(j + 1) * DV, at], state[:, p % 2, c - 1, j * DV:(j + 1) * DV],
                                      kq_t[:, p % 2, 2 * j + 1, at], start=False, stop=True)
                last.then_inc(s_o, 1)

            def gn_means(i, p):
                pe.wait_ge(s_gns2, NP * i + p + 1)
                o = take(pe, i, "gn_steps", 8 * p + 4)
                mm(o[:, 0:1], head_mean[:, :], gn_mv[:, p, 0:1], start=True, stop=True).then_inc(s_gnpe, 1)

            def gn_variances(i, p):
                pe.wait_ge(s_gn, 24 * i + 8 * p + 4)
                mm(bank_of("gn_steps", 8 * p + 4)[:, 4:5], head_mean[:, :], gn_m2[:, p:p + 1], start=True, stop=True)\
                    .then_inc(s_gnpe, 1)

            def out_project(b, t, pairs):
                for m in pairs:
                    if t == 0:
                        pe.wait_ge(s_gated, NP * b + m + 1)
                    last = mm(hb[t // 2][:, (t % 2) * D:(t % 2 + 1) * D], att[:, m, t * P:(t + 1) * P], wo[:, m, :],
                              start=False, stop=m == NP - 1, skip_group_check=True)
                if NP - 1 in pairs and t % 2:
                    last.then_inc(s_wo, 1)

            def turn_x2(b):
                pe.wait_ge(s_x2s, 2 * (b + 1))
                for c in range(3):
                    o = take(pe, b + 1, "x2_t_ready", c)
                    for t in range(NT):
                        last = nc.tensor.transpose(o[:, t * P:(t + 1) * P], x2_split[:, t, c * P:(c + 1) * P].bitcast(fp32),
                                                   ident[:, :])
                    last.then_inc(s_x2T, 1)

            def hidden(b, m):
                if m == 0:
                    pe.wait_ge(s_x2t, 3 * (b + 1))
                o = take(pe, b + 1, "hidden_ready", m)
                at = slice(m * P, (m + 1) * P)
                for c in range(3):
                    mm(o[:, :], fc1_hi[:, c, at], x2_t[:, c, :], start=c == 0, stop=False)
                for c in range(2):
                    last = mm(o[:, :], fc1_lo[:, c, at], x2_t[:, c, :], start=False, stop=c == 1)
                last.then_inc(s_fc1, 1)

            def second_layer(b, t, chunks=range(NF)):
                for m in chunks:
                    if t == 0 and m == 0:
                        pe.wait_ge(s_h2c, b + 1)
                        pe.wait_ge(s_x2, NT * (b + 1))
                    if t == 0:
                        pe.wait_ge(s_hid, NF * b + m + 1)
                    last = mm(hb[t // 2][:, (t % 2) * D:(t % 2 + 1) * D], hid[:, m, t * P:(t + 1) * P], fc2[:, m, :],
                              start=False, stop=m == NF - 1, skip_group_check=True)
                    if t % 2 and m == NF - 1:
                        last.then_inc(s_fc2, 1)

            def body(i, has_back, has_next):
                b = i - 1
                project_v(i, 2)
                project_v(i, 3)
                project(i, 1, 0)
                turn_pair(i, 0)
                project(i, 1, 1)
                key_values(i, 0)
                scores(i, 0, 0)
                scores(i, 0, 1)
                project_gate(i, 0)
                if has_back:
                    turn_x2(b)
                project(i, 1, 2)
                outputs(i, 0)
                project(i, 1, 3)
                if has_back:
                    hidden(b, 0)
                project(i, 2, 0)
                if has_back:
                    hidden(b, 1)
                project_gate(i, 1)
                gn_means(i, 0)
                turn_pair(i, 1)
                gn_variances(i, 0)
                key_values(i, 1)
                if has_back:
                    hidden(b, 2)
                project(i, 2, 1)
                if has_next:
                    turn_embeddings(i + 1)
                if has_back:
                    hidden(b, 3)
                scores(i, 1, 0)
                scores(i, 1, 1)
                project_gate(i, 2)
                if has_next:
                    h_for_statistics(i + 1)
                if has_back:
                    hidden(b, 4)
                project(i, 2, 2)
                outputs(i, 1)
                if has_back:
                    hidden(b, 5)
                project(i, 2, 3)
                if has_next:
                    turn_norm(i + 1)
                if has_back:
                    second_layer(b, 0)
                gn_means(i, 1)
                if has_back:
                    second_layer(b, 1)
                if has_next:
                    project(i + 1, 0, 0, NEXT)
                gn_variances(i, 1)
                turn_pair(i, 2)
                key_values(i, 2)
                if has_next:
                    project(i + 1, 0, 1, NEXT)
                scores(i, 2, 0)
                scores(i, 2, 1)
                residual(i, 0)
                if has_next:
                    project(i + 1, 0, 2, NEXT)
                if has_back:
                    second_layer(b, 2)
                if has_next:
                    project(i + 1, 0, 3, NEXT)
                outputs(i, 2)
                if has_back:
                    second_layer(b, 3)
                gn_means(i, 2)
                out_project(i, 0, (0, 1))
                if has_next:
                    project_v(i + 1, 0, NEXT)
                gn_variances(i, 2)
                out_project(i, 1, (0, 1))
                residual(i, 1)
                out_project(i, 2, (0, 1))
                out_project(i, 3, (0, 1))
                if has_next:
                    project_v(i + 1, 1, NEXT)
                for t in range(NT):
                    out_project(i, t, (2,))

            pe.wait_ge(s_center, N_CENTER)
            for o, cols in ((hb[0][:, 0:2 * R], slice(0, P)), (hb[1][0:D - P, 0:2 * R], slice(P, D))):
                mm(o, center[:, cols], up_dup[:, 0:2 * R], start=True, stop=False)
                last = mm(o, center[0:D - P, D + cols.start:D + cols.stop], up_dup[0:D - P, 2 * R:4 * R], start=False, stop=True)
            last.then_inc(s_set_pe, 1)
            pe.wait_ge(s_first, N_FIRST)
            turn_embeddings(0)
            pe.wait_ge(s_set_dve, SET_CEN)
            pe.wait_ge(s_stage, N_STAGE)
            for n in range(RING):
                if n >= 2:
                    pe.wait_ge(s_set_dve, SET_CEN + 2 * (n - 1))
                if n == 1:
                    h_for_statistics(0)
                if n == 3:
                    turn_norm(0)
                o, at = hb[n % 2][:, 0:SC], slice(n * SC, (n + 1) * SC)
                mm(o, up_cen[:, 0:2 * R], wa[:, at], start=True, stop=False)
                mm(o, up_cen[0:D - P, 2 * R:4 * R], wb[:, at], start=False, stop=True).then_inc(s_set_pe, 1)
            pe.wait_ge(s_set_dve, SET_W)
            for t in range(NT):
                project(0, 0, t, NEXT)
            project_v(0, 0, NEXT)
            project_v(0, 1, NEXT)
            pe.wait_ge(s_const, N_CONST)

            body(0, False, True)
            pe.wait_ge(s_set_dve, SET_FC1)
            with nc.tensor.Fori(1, B - 1) as i:
                body(i, True, True)
            body(B - 1, True, False)
            turn_x2(B - 1)
            for m in range(NF):
                hidden(B - 1, m)

            second_layer(B - 1, 0)
            pe.wait_ge(s_cl, N_CL)
            pe.wait_ge(s_hid, NF * B)
            for s in range(2):
                for c, at in enumerate((0, D - P)):
                    last = nc.tensor.transpose(bank[2 * s + c][:, 0:CT], x2c_sb[:, s, at:at + P], ident[0:CT, 0:CT])
            last.then_inc(s_cpe, 1)
            second_layer(B - 1, 1)
            pe.wait_ge(s_cw, N_CW)
            pe.wait_ge(s_cd, CD_T)
            for atom in range(NATOM):
                for m in range(NF):
                    k = NF * atom + m
                    if k >= RING:
                        pe.wait_ge(s_chf, k - RING + 1)
                    n = 2 * B if atom < NQ else NQ * B
                    o = bank[k % RING][:, 0:n]
                    for c in range(2):
                        x = x2c_t[:, c, :].rearrange("p (s q b) -> p s q b", s=2, q=NQ)
                        x = x[:, :, atom, :] if atom < NQ else x[:, atom - NQ, :, :]
                        last = mm(o, w_in_at(atom, c)[:, m * P:(m + 1) * P], x, start=c == 0, stop=c == 1)
                    last.then_inc(s_ch, 1)
                    if atom < 2:
                        second_layer(B - 1, 2 + atom, (m,))
            pe.wait_ge(s_chf, NATOM * NF)
            pe.wait_ge(s_cwo, 16 * NATOM)
            for s in range(2):
                for m in range(NF):
                    for q in range(NQ):
                        last = mm(bank[1][q * B:(q + 1) * B, s * D:(s + 1) * D], c_hid[:, 1, m, s, q, :],
                                  w_out_at(q)[:, m, :], start=s == 0 and m == 0, stop=m == NF - 1, skip_group_check=True)
            last.then_inc(s_co, 1)
            for s in range(2):
                for m in range(NF):
                    last = mm(bank[0][0:CT, s * D:(s + 1) * D], c_hid[:, 0, m, s, :, :].rearrange("p q b -> p (q b)"),
                              w_out_at(NQ + s)[:, m, :], start=s == 0 and m == 0, stop=m == NF - 1, skip_group_check=True)
            last.then_inc(s_co, 1)

        @block.vector
        def _(dve):
            V = nc.vector

            def split(dst_hi, dst_lo, src, s, at):
                V.tensor_copy(dst_hi, src).then_inc(s, 1)
                dve.wait_ge(s, at + 1)
                V.tensor_tensor(dst_lo, src, dst_hi.bitcast(fp32), ALU.subtract).then_inc(s, 1)

            def split_embeddings(b):
                dve.wait_ge(s_emb, 64 * (b + 1))
                if later(b):
                    dve.wait_ge(s_embT, 2 * b)
                split(emb_split[:, :, 0:R], emb_split[:, :, R:2 * R], emb[:, :].rearrange("p (t r) -> p t r", t=NT),
                      s_embsplit, 2 * b)

            def layer_statistics(b, stats, mv, ve, s, source, ready):
                for t in range(NT):
                    if t % 2 == 0:
                        dve.wait_ge(ready, 2 * b + t // 2 + 1)
                    V.bn_stats(stats[:, t, :], source[t // 2][:, (t % 2) * D:(t % 2 + 1) * D]).then_inc(s, 1)
                wait_apart(dve, s, 10 * b + NT)
                for t in range(NT):
                    V.bn_aggr(mv[:, t, :], stats[:, t, :]).then_inc(s, 1)
                dve.wait_ge(s, 10 * b + 2 * NT)
                V.tensor_scalar(ve[:, :], mv[:, :, 1], LN_EPS, None, ALU.add).then_inc(s, 1)

            def statistics_ln1(b):
                banks = [bank_of("ln1_steps", 1), bank_of("ln1_steps", 3)]
                layer_statistics(b, ln1_st, ln1_mv, ln1_ve, s_ln1, banks, s_hstat)

            def normalise_embeddings(b):
                dve.wait_ge(s_ln1p, b + 1)
                V.tensor_tensor(emb_norm[:, :, :], emb[:, :].rearrange("p (t r) -> p t r", t=NT),
                                ln1_rstd[:, :].unsqueeze(2).broadcast_to([P, NT, R]), ALU.mult).then_inc(s_ln1, 1)
                if later(b):
                    dve.wait_ge(s_normT, b)
                dve.wait_ge(s_ln1, 10 * (b + 1))
                split(norm_split[:, :, 0:R], norm_split[:, :, R:2 * R], emb_norm[:, :, :], s_normsplit, 2 * b)

            def rotary(i, p, t):
                n = NT * p + t
                if n >= 3 or later(i):
                    dve.wait_ge(s_rot, NT * NP * i + n - 2)
                dve.wait_ge(s_proj, NT * NP * i + n + 1)
                src = bank_of("rotary_products", n)[:, :].rearrange("p (g s d) -> p g s d", g=4, s=2)
                V.tensor_tensor(rot_c[:, n % 3, :].rearrange("p (g s d) -> p g s d", g=4, s=2), src,
                                cos_t[:, t, p, :, :].unsqueeze(2).broadcast_to([P, 4, 2, HALF]), ALU.mult)
                V.tensor_tensor(rot_s[:, n % 3, :].rearrange("p (g s d) -> p g s d", g=4, s=2), src[:, :, ::-1, :],
                                sin_t[:, t, p, :, :].rearrange("p g (s d) -> p g s d", s=2), ALU.mult)\
                    .then_inc(s_rotm, 1)

            def gate_product(i, m):
                dve.wait_ge(s_tanh, NP * i + m + 1)
                V.scalar_tensor_tensor(gate[:, m, :], gate[:, m, :], 1.0, bank_of("gate_ready", m)[:, :], ALU.add, ALU.mult)\
                    .then_inc(s_gate, 1)

            def states(i, p):
                dve.wait_ge(s_kv, NP * i + p + 1)
                if p == 2:
                    dve.wait_ge(s_o, NP * i + 1)
                elif later(i):
                    dve.wait_ge(s_o, NP * i - (0 if p == 0 else 1))
                src = bank_of("state_steps", 3 * p + 2)
                V.tensor_copy(state[:, p % 2, 0, :], src[:, 0:P]).then_inc(s_state, 1)
                for c in range(1, NT - 1):
                    dve.wait_ge(s_state, 9 * i + 3 * p + c)
                    V.tensor_tensor(state[:, p % 2, c, :], src[:, c * P:(c + 1) * P], state[:, p % 2, c - 1, :], ALU.add)\
                        .then_inc(s_state, 1)

            def mask(i, p):
                if p == 2:
                    dve.wait_ge(s_o, NP * i + 1)
                elif later(i):
                    dve.wait_ge(s_o, NP * i - (0 if p == 0 else 1))
                for j in range(2):
                    dve.wait_ge(s_score, 6 * i + 2 * p + j + 1)
                    V.tensor_tensor(probs[:, p % 2, j, :].rearrange("p (c t) -> p c t", c=NT),
                                    bank_of("probs_ready", 2 * p + j)[:, :].rearrange("p (c t) -> p c t", c=NT),
                                    causal[:, :].unsqueeze(1).broadcast_to([P, NT, P]), ALU.mult).then_inc(s_prob, 1)

            def channel_statistics(i, p):
                dve.wait_ge(s_att, NP * i + p + 1)
                V.bn_stats(gn_st[:, p, :], att[:, p, :]).then_inc(s_gns, 1)
                wait_apart(dve, s_gns, NP * i + p + 1)
                V.bn_aggr(gn_mv[:, p, :], gn_st[:, p, :]).then_inc(s_gns2, 1)

            def head_means(i, p):
                one, at = slice(p, p + 1), 24 * i + 8 * p
                dve.wait_ge(s_gnpe, 6 * i + 2 * p + 1)
                V.tensor_copy(gn_dd[:, one], bank_of("gn_steps", 8 * p + 4)[:, 0:1]).then_inc(s_gn, 1)
                dve.wait_ge(s_gn, at + 1)
                V.tensor_tensor(gn_d[:, one], gn_mv[:, p, 0:1], gn_dd[:, one], ALU.subtract).then_inc(s_gn, 1)
                dve.wait_ge(s_gn, at + 2)
                V.tensor_tensor(gn_ma[:, one], gn_d[:, one], gn_d[:, one], ALU.mult).then_inc(s_gn, 1)
                dve.wait_ge(s_gn, at + 3)
                V.tensor_tensor(gn_m2[:, one], gn_ma[:, one], gn_mv[:, p, 1:2], ALU.add).then_inc(s_gn, 1)

            def head_variances(i, p):
                dve.wait_ge(s_gnpe, 6 * i + 2 * p + 2)
                V.tensor_scalar(gn_ve[:, p:p + 1], bank_of("gn_steps", 8 * p + 4)[:, 4:5], LN_EPS, None, ALU.add)\
                    .then_inc(s_gn, 1)

            def head_factors(i, p):
                one, at = slice(p, p + 1), 24 * i + 8 * p
                dve.wait_ge(s_gnp, NP * i + p + 1)
                V.scalar_tensor_tensor(gn_a[:, one], gn_w[:, one], 0.5, gn_rstd[:, one], ALU.mult, ALU.mult).then_inc(s_gn, 1)
                dve.wait_ge(s_gn, at + 6)
                V.tensor_tensor(gn_ma[:, one], gn_dd[:, one], gn_a[:, one], ALU.mult).then_inc(s_gn, 1)
                dve.wait_ge(s_gn, at + 7)
                V.scalar_tensor_tensor(gn_c[:, one], gn_b[:, one], 0.5, gn_ma[:, one], ALU.mult, ALU.subtract)\
                    .then_inc(s_gn, 1)

            def gating(i, m):
                if m < NP - 1:
                    dve.wait_ge(s_aff, (NP - 1) * i + m + 1)
                else:
                    dve.wait_ge(s_gn, 24 * (i + 1))
                    V.tensor_scalar(att[:, m, :], att[:, m, :], gn_a[:, m:m + 1], gn_c[:, m:m + 1], ALU.mult, ALU.add)\
                        .then_inc(s_aff2, 1)
                    dve.wait_ge(s_aff2, i + 1)
                V.tensor_tensor(att[:, m, :], att[:, m, :], gate[:, m, :], ALU.mult).then_inc(s_gated, 1)

            def statistics_ln2(b):
                layer_statistics(b, ln2_st, ln2_mv, ln2_ve, s_ln2, hb, s_wo)

            def shift_ln2(b):
                dve.wait_ge(s_ln2p, b + 1)
                V.scalar_tensor_tensor(ln2_nmr[:, :], ln2_mv[:, :, 0], -1.0, ln2_rstd[:, :], ALU.mult, ALU.mult)\
                    .then_inc(s_ln2, 1)

            def split_x2(b):
                dve.wait_ge(s_x2, NT * (b + 1))
                if later(b):
                    dve.wait_ge(s_x2T, 3 * b)
                split(x2_split[:, :, 0:D], x2_split[:, :, D:2 * D], x2[:, :, :], s_x2s, 2 * b)

            def result(b, k):
                dve.wait_ge(s_fc2, 2 * b + k + 1)
                if later(b):
                    dve.wait_ge((s_stA, s_stB)[k], (32, 16)[k] * b)
                V.tensor_tensor(res[:, 2 * k:2 * k + 2, :], hb[k][:, 0:2 * D].rearrange("p (t d) -> p t d", t=2),
                                fc2_b[:, :].unsqueeze(1).broadcast_to([P, 2, D]), ALU.add).then_inc(s_res, 1)

            def body(i, has_back, has_next):
                b = i - 1
                if has_back:
                    statistics_ln2(b)
                rotary(i, 1, 0)
                if has_back:
                    shift_ln2(b)
                rotary(i, 1, 1)
                if has_back:
                    split_x2(b)
                states(i, 0)
                mask(i, 0)
                gate_product(i, 0)
                rotary(i, 1, 2)
                rotary(i, 1, 3)
                channel_statistics(i, 0)
                rotary(i, 2, 0)
                head_means(i, 0)
                gate_product(i, 1)
                head_variances(i, 0)
                if has_next:
                    split_embeddings(i + 1)
                states(i, 1)
                head_factors(i, 0)
                rotary(i, 2, 1)
                mask(i, 1)
                if has_next:
                    statistics_ln1(i + 1)
                gate_product(i, 2)
                gating(i, 0)
                if has_next:
                    normalise_embeddings(i + 1)
                rotary(i, 2, 2)
                channel_statistics(i, 1)
                rotary(i, 2, 3)
                head_means(i, 1)
                if has_back:
                    result(b, 0)
                if has_next:
                    rotary(i + 1, 0, 0)
                head_variances(i, 1)
                states(i, 2)
                head_factors(i, 1)
                if has_next:
                    rotary(i + 1, 0, 1)
                mask(i, 2)
                gating(i, 1)
                if has_next:
                    rotary(i + 1, 0, 2)
                    rotary(i + 1, 0, 3)
                channel_statistics(i, 2)
                head_means(i, 2)
                if has_back:
                    result(b, 1)
                head_variances(i, 2)
                head_factors(i, 2)
                gating(i, 2)

            dve.wait_ge(s_first, N_FIRST)
            split(up_hi[:, :], up_lo[:, :], up_stage, s_set_dve, 0)
            dve.wait_ge(s_set_pe, 1)
            V.tensor_copy(up_cen[:, 0:2 * R], hb[0][:, 0:2 * R]).then_inc(s_set_dve, 1)
            V.tensor_copy(up_cen[0:D - P, 2 * R:4 * R], hb[1][0:D - P, 0:2 * R]).then_inc(s_set_dve, 1)
            split_embeddings(0)
            for n in range(RING):
                dve.wait_ge(s_set_pe, 2 + n)
                at = slice(n * SC, (n + 1) * SC)
                split(w_hi[:, at], w_lo[:, at], hb[n % 2][:, 0:SC], s_set_dve, SET_CEN + 2 * n)
                if n == 0:
                    statistics_ln1(0)
                if n == 1:
                    normalise_embeddings(0)
            dve.wait_ge(s_tables, N_TABLES)
            for t in range(NT):
                rotary(0, 0, t)
            dve.wait_ge(s_const, N_CONST)

            body(0, False, True)
            V.tensor_copy(fc1_hi[:, :, :], fc1_stage.rearrange("p (c f) -> p c f", c=3)).then_inc(s_set_dve, 1)
            dve.wait_ge(s_set_dve, SET_W + 1)
            V.tensor_tensor(fc1_lo[:, :, :], fc1_stage[:, 0:2 * F].rearrange("p (c f) -> p c f", c=2),
                            fc1_hi[:, 0:2, :].bitcast(fp32), ALU.subtract).then_inc(s_set_dve, 1)
            with nc.vector.Fori(1, B - 1) as i:
                body(i, True, True)
            body(B - 1, True, False)
            statistics_ln2(B - 1)
            shift_ln2(B - 1)
            split_x2(B - 1)

            step = [0]

            def chain(ins):
                ins.then_inc(s_cd, 1)
                step[0] += 1
                dve.wait_ge(s_cd, step[0])

            dve.wait_ge(s_rot, NT * NP * B)
            V.memset(g_half, 0.5).then_inc(s_cd, 1)
            V.memset(x2c_t[0:2 * P - D, 1, :], 0.0).then_inc(s_cd, 1)
            step[0] += 2
            dve.wait_ge(s_cl, N_CL)
            dve.wait_ge(s_cpe, 1)
            for s in range(2):
                for c, at in ((0, 0), (1, 2 * P - D)):
                    V.tensor_copy(x2c_t[at:P, c, s * CT:(s + 1) * CT], bank[2 * s + c][at:P, 0:CT]).then_inc(s_cd, 1)
                    step[0] += 1
            assert step[0] == CD_T

            def dot(o, x, y):
                chain(V.tensor_tensor_reduce(out=g_junk, in0=x, in1=y, scale=1.0, scalar=0.0, op0=ALU.mult,
                                             op1=ALU.add, accum_out=o))

            for s in range(2):
                dot(g_sq[:, s:s + 1], x2c_sb[:, s, :], x2c_sb[:, s, :])
                for r in range(2):
                    k = 2 * s + r
                    dot(g_sq[:, 2 + k:3 + k], gw_sb[:, s, r, :], gw_sb[:, s, r, :])
                    dot(g_dot[:, k:k + 1], x2c_sb[:, s, :], gw_sb[:, s, r, :])
            assert step[0] == CD_SQ
            dve.wait_ge(s_cg, 1)
            chain(V.tensor_scalar(g_nrm, g_nrm, 1e-12, None, ALU.max))
            chain(V.reciprocal(g_sq, g_nrm))
            logits = g_log.rearrange("p s r -> p (s r)")
            chain(V.tensor_tensor(logits, g_dot, g_sq[:, 2:6], ALU.mult))
            chain(V.tensor_tensor(g_log, g_log, g_sq[:, 0:2].unsqueeze(2).broadcast_to([CT, 2, 2]), ALU.mult))
            chain(V.tensor_tensor(g_log, g_log, bal_sb, ALU.add))
            d = g_x[:, 0:2]
            chain(V.tensor_tensor(d, g_log[:, :, 1], g_log[:, :, 0], ALU.subtract))
            chain(V.tensor_scalar(g_x[:, 8:10], d, -1.0, None, ALU.mult))
            chain(V.tensor_tensor(g_x[:, 2:4], d, g_x[:, 8:10], ALU.max))
            assert step[0] == CD_DIFF
            chain(V.tensor_scalar(g_x[:, 10:12], d, 0.0, None, ALU.is_gt))
            chain(V.tensor_scalar(g_x[:, 12:14], g_x[:, 10:12], -1.0, 1.0, ALU.mult, ALU.add))
            dve.wait_ge(s_ct, 1)
            weight, route1, route0 = g_x[:, 6:8], g_x[:, 10:12], g_x[:, 12:14]
            chain(V.tensor_scalar(weight, g_x[:, 4:6], 0.5, 0.5, ALU.mult, ALU.add))
            chain(V.tensor_tensor(route1, route1, weight, ALU.mult))
            chain(V.tensor_tensor(route0, route0, weight, ALU.mult))
            result(B - 1, 0)
            result(B - 1, 1)

            def candidate(o, k, r, share):
                dve.wait_ge(s_co, k)
                chain(V.tensor_tensor(o, bank[r][0:CT, 0:2 * D].rearrange("p (s d) -> p s d", s=2), ob_sb[:, :, r, :],
                                      ALU.add))
                chain(V.tensor_tensor(o, o, share.unsqueeze(2).broadcast_to([CT, 2, D]), ALU.mult))

            candidate(c_b, 1, 1, route1)
            chain(V.tensor_tensor(c_b, c_b, h2c_sb, ALU.add))
            candidate(c_a, 2, 0, route0)
            chain(V.tensor_tensor(c_res, c_a, c_b, ALU.add))
            assert step[0] == CLS_STEPS


def tables():
    f = np.float32
    half = np.arange(HALF, dtype=f)
    inv_freq = (f(1.0) / np.power(f(10000.0), half / f(HALF))).astype(f)
    pos = np.arange(T, dtype=f)
    angle = (pos[:, None] * inv_freq[None, :]).astype(f).astype(np.float64)
    zeta = ((half + f(HALF)) / f(DK)).astype(np.float64)
    p64 = np.arange(T, dtype=np.float64)
    cos = np.zeros((T, 2, H, HALF))
    sin = np.zeros((T, 2, H, DK))
    for h in range(H):
        gamma = 1.0 - 2.0 ** (-(5 + h))
        rows = np.cumsum(gamma ** p64)
        for k, sign in ((0, -1.0), (1, 1.0)):
            scale = zeta[None, :] ** (sign * p64[:, None] / 512.0) * (gamma ** (sign * p64))[:, None]
            if k == 1:
                scale = scale * (DK ** -0.5 / np.sqrt(np.maximum(rows, 1e-6)))[:, None]
            cos[:, k, h, :] = np.cos(angle) * scale
            sin[:, k, h, :HALF] = -np.sin(angle) * scale
            sin[:, k, h, HALF:] = np.sin(angle) * scale
    lay = lambda x: np.ascontiguousarray(
        x.reshape(NT, P, 2, NP, 2, -1).transpose(1, 0, 3, 2, 4, 5).reshape(P, NT, NP, 4, -1).astype(f))
    return lay(cos), lay(sin)


def columns(x):
    return x.reshape(-1, P).T


def kernel(**inputs):
    import concourse.bacc as bacc
    from concourse.bass_utils import run_bass_kernel_spmd as run

    given = {k: np.asarray(x) for k, x in inputs.items()}
    cos, sin = tables()
    wk, wq = (given[name].reshape(D, NP, 2 * DK) for name in ("L0_attn_Wk", "L0_attn_Wq"))
    heads = np.zeros((P, P), np.float32)
    heads[:DV, :DV] = heads[DV:, DV:] = 1.0 / DV
    arrays = {
        "ids": given["x"].reshape(B, NT, P).transpose(0, 2, 1),
        "table": given["L0_tok_embed_table"], "up": given["L0_tok_proj_up"], "up_t": given["L0_tok_proj_up"].T,
        "w": np.concatenate([np.concatenate([wk, wq], axis=2).reshape(D, 2 * QK), given["L0_attn_Wv"],
                             given["L0_attn_Wg"]], axis=1),
        "wo": given["L0_attn_Wo"],
        "gn_w": columns(given["L0_attn_gn_weight"]), "gn_b": columns(given["L0_attn_gn_bias"]),
        "fc1_t": given["L0_ffn_fc1_w"].T, "fc1_b": columns(given["L0_ffn_fc1_b"]),
        "fc2_t": given["L0_ffn_fc2_w"].T, "fc2_b": given["L0_ffn_fc2_b"],
        "gate_pair": given["L0_ffn_gate_pair"], "balance": given["L0_ffn_balance_bias"],
        "route_b": given["L0_ffn_atom_out_b"][np.array([atoms[::-1] for atoms in SRC])],
        "ain_t": given["L0_ffn_atom_in_w"].transpose(0, 2, 1),
        "ain_b": given["L0_ffn_atom_in_b"].reshape(NATOM, NF, P).transpose(2, 0, 1),
        "aout_t": given["L0_ffn_atom_out_w"].transpose(0, 2, 1),
        "cos_t": cos, "sin_t": sin, "ident": np.eye(P, dtype=np.float32), "head_mean": heads,
        "causal": np.triu(np.ones((P, P), np.float32)),
        "center": (np.eye(D) - 1.0 / D).astype(np.float32),
    }
    nc = bacc.Bacc("TRN2", target_bir_lowering=False, num_devices=1)
    fed, a = {}, {}
    for name, x in arrays.items():
        fed[f"in_{name}"] = np.ascontiguousarray(x)
        a[name] = nc.dram_tensor(f"in_{name}", x.shape, mybir.dt.from_np(x.dtype), kind="ExternalInput").ap()
    for name in ("x2c", "h2c"):
        a[name] = nc.dram_tensor(name, (NCLS, B, D), mybir.dt.float32, kind="Internal").ap()
    a["out"] = nc.dram_tensor("out", (B, T, D), mybir.dt.float32, kind="ExternalOutput").ap()
    build(nc, a)
    return run(nc, [fed], core_ids=[0]).results[0]["out"]
```
